# Optimizing a Trainium2 kernel written in Bass

```python
import numpy as np
import jax
import jax.numpy as jnp

def _softmax(x, axis=-1):
    return jax.nn.softmax(x, axis=axis)

def _gelu(x):
    return jax.nn.gelu(x, approximate=True)

def _silu(x):
    return jax.nn.silu(x)

def _sigmoid(x):
    return jax.nn.sigmoid(x)

def _layernorm(x, axis=-1, eps=1e-05):
    m = jnp.mean(x, axis=axis, keepdims=True)
    v = jnp.var(x, axis=axis, keepdims=True)
    return (x - m) / jnp.sqrt(v + eps)

def _scatter_add(tgt, idx, src, axis=0):
    return tgt.at[idx].add(src)

def _segment_sum(src, seg, n):
    return jax.ops.segment_sum(src, seg, n)
kernel_name = 'mk_adaln_d4_jaxref_r8_47aadd'

def setup_inputs(seed: int=0):
    np.random.seed(seed)
    _w = jnp.asarray

    def _L0_attn_setup():
        import jax, jax.numpy as jnp
        import numpy as np
        EMBED_DIM = 128
        NUM_HEADS = 16
        DEPTH = 12
        HEAD_DIM = EMBED_DIM // NUM_HEADS // 2
        LAMBDA_INIT = float(0.8 - 0.6 * np.exp(-0.3 * DEPTH))
        B, T = (2, 256)
        key = jax.random.key(seed)
        ks = jax.random.split(key, 10)
        s = 0.02
        return {'query': jax.random.normal(ks[0], (B, T, EMBED_DIM), jnp.float32), 'Wq': jax.random.normal(ks[1], (EMBED_DIM, EMBED_DIM), jnp.float32) * s, 'Wk': jax.random.normal(ks[2], (EMBED_DIM, EMBED_DIM), jnp.float32) * s, 'Wv': jax.random.normal(ks[3], (EMBED_DIM, EMBED_DIM), jnp.float32) * s, 'Wo': jax.random.normal(ks[4], (EMBED_DIM, EMBED_DIM), jnp.float32) * s, 'lambda_q1': jax.random.normal(ks[5], (HEAD_DIM,), jnp.float32) * 0.1, 'lambda_k1': jax.random.normal(ks[6], (HEAD_DIM,), jnp.float32) * 0.1, 'lambda_q2': jax.random.normal(ks[7], (HEAD_DIM,), jnp.float32) * 0.1, 'lambda_k2': jax.random.normal(ks[8], (HEAD_DIM,), jnp.float32) * 0.1, 'subln_w': jnp.ones((2 * HEAD_DIM,), jnp.float32)}
    _L0_attn_in = _L0_attn_setup()

    def _L0_ffn_setup():
        import jax, jax.numpy as jnp
        import numpy as np
        LORA_DIM = 16
        LORA_TOKEN_INDEX = 1
        B, S, D, H = (4, 256, 128, 512)
        key = jax.random.key(seed)
        ks = jax.random.split(key, 6)
        x = jax.random.normal(ks[0], (B, S, D), dtype=jnp.float32)
        W1 = jax.random.normal(ks[1], (H, D), dtype=jnp.float32) * 0.02
        b1 = jnp.zeros((H,), dtype=jnp.float32)
        W2 = jax.random.normal(ks[2], (D, H), dtype=jnp.float32) * 0.02
        b2 = jnp.zeros((D,), dtype=jnp.float32)
        scale = jnp.asarray(0.001, dtype=jnp.float32)
        return {'x': x, 'W1': W1, 'b1': b1, 'W2': W2, 'b2': b2, 'scale': scale}
    _L0_ffn_in = _L0_ffn_setup()
    _L0_c = _w((lambda *s: np.random.randn(*s).astype(np.float32) * 0.05)(2, 128))
    _L0_wmod = _w((lambda *s: np.random.randn(*s).astype(np.float32) * 0.05)(128, 6 * 128) * 128 ** (-0.5))

    def _L1_attn_setup():
        import jax, jax.numpy as jnp
        import numpy as np
        NUM_HEADS = 16
        PAD_ID = 0.0
        key = jax.random.key(seed)
        ks = jax.random.split(key, 9)
        B, T, C = (2, 256, 128)
        x = jax.random.normal(ks[0], (B, T, C), dtype=jnp.float32)
        lim = (6.0 / (C + C)) ** 0.5

        def w(k):
            return jax.random.uniform(k, (C, C), dtype=jnp.float32, minval=-lim, maxval=lim)

        def b(k):
            return jax.random.uniform(k, (C,), dtype=jnp.float32)
        return {'x': x, 'wq_w': w(ks[1]), 'wq_b': b(ks[2]), 'wk_w': w(ks[3]), 'wk_b': b(ks[4]), 'wv_w': w(ks[5]), 'wv_b': b(ks[6]), 'wo_w': w(ks[7]), 'wo_b': b(ks[8])}
    _L1_attn_in = _L1_attn_setup()

    def _L1_ffn_setup():
        import jax, jax.numpy as jnp
        import numpy as np
        DIM = 128

        def _reference_tuple_inner(x, W_r, W_k, W_v, mu_r, mu_k):
            B, T, C = x.shape
            x_prev = jnp.concatenate([jnp.zeros((B, 1, C), x.dtype), x[:, :-1, :]], axis=1)
            xr = mu_r * x + (1.0 - mu_r) * x_prev
            xk = mu_k * x + (1.0 - mu_k) * x_prev
            r = jax.nn.sigmoid(jnp.einsum('btc,dc->btd', xr, W_r))
            k = jnp.einsum('btc,dc->btd', xk, W_k)
            k_act = jnp.square(jax.nn.relu(k))
            out = r * jnp.einsum('btc,dc->btd', k_act, W_v)
            new_state = x[:, -1, :]
            return (out, new_state)
        key = jax.random.key(seed)
        ks = jax.random.split(key, 6)
        B, T, C = (8, 256, DIM)
        x = jax.random.normal(ks[0], (B, T, C), dtype=jnp.float32)
        s = 1.0 / np.sqrt(C)
        W_r = jax.random.uniform(ks[1], (C, C), jnp.float32, -s, s)
        W_k = jax.random.uniform(ks[2], (C, C), jnp.float32, -s, s)
        W_v = jax.random.uniform(ks[3], (C, C), jnp.float32, -s, s)
        mu_r = jax.random.uniform(ks[4], (C,), jnp.float32)
        mu_k = jax.random.uniform(ks[5], (C,), jnp.float32)
        return {'x': x, 'W_r': W_r, 'W_k': W_k, 'W_v': W_v, 'mu_r': mu_r, 'mu_k': mu_k}
    _L1_ffn_in = _L1_ffn_setup()
    _L1_c = _w((lambda *s: np.random.randn(*s).astype(np.float32) * 0.05)(2, 128))
    _L1_wmod = _w((lambda *s: np.random.randn(*s).astype(np.float32) * 0.05)(128, 6 * 128) * 128 ** (-0.5))

    def _L2_attn_setup():
        import jax, jax.numpy as jnp
        import numpy as np
        B, T, C = (64, 32, 128)
        N_HEAD, HEAD_SIZE, KV_RANK = (16, 64, 128)
        BLOCK_SIZE = 32
        key = jax.random.key(seed)
        ks = jax.random.split(key, 5)
        HD = N_HEAD * HEAD_SIZE

        def init(k, shape):
            fan_in = shape[0]
            bound = 1.0 / np.sqrt(fan_in)
            return jax.random.uniform(k, shape, jnp.float32, -bound, bound)
        return {'x': jax.random.normal(ks[0], (B, T, C), jnp.float32), 'w_kv_down': init(ks[1], (C, KV_RANK)), 'w_kv_up': init(ks[2], (KV_RANK, 2 * HD)), 'w_q': init(ks[3], (C, HD)), 'w_out': init(ks[4], (HD, C))}
    _L2_attn_in = _L2_attn_setup()

    def _L2_ffn_setup():
        import jax, jax.numpy as jnp
        import numpy as np
        B, T, C = (1, 512, 128)
        E, K = (64, 8)
        G, TG = (8, 4)
        H, HS = (64, 256)
        STD = 0.02

        def _route(xf, router_w, e_bias):
            S = xf.shape[0]
            scores = jax.nn.sigmoid(xf @ router_w.T)
            sb = scores + e_bias
            epg = E // G
            grp = jax.lax.top_k(sb.reshape(S, G, epg), K // TG)[0].sum(-1)
            gidx = jax.lax.top_k(grp, TG)[1]
            gmask = jnp.zeros((S, G), bool).at[jnp.arange(S)[:, None], gidx].set(True)
            emask = jnp.repeat(gmask, epg, axis=1)
            masked = jnp.where(emask, sb, -jnp.inf)
            topk_idx = jax.lax.top_k(masked, K)[1]
            w = jnp.take_along_axis(scores, topk_idx, axis=1)
            w = w / (w.sum(-1, keepdims=True) + 1e-20)
            return (topk_idx, w)
        key = jax.random.key(seed)
        ks = jax.random.split(key, 9)
        return {'x': jax.random.normal(ks[0], (B, T, C), jnp.float32), 'router_w': jax.random.normal(ks[1], (E, C), jnp.float32) * C ** (-0.5), 'e_bias': jnp.zeros((E,), jnp.float32), 'gate_w': jax.random.normal(ks[2], (E, C, H), jnp.float32) * STD, 'up_w': jax.random.normal(ks[3], (E, C, H), jnp.float32) * STD, 'down_w': jax.random.normal(ks[4], (E, H, C), jnp.float32) * STD, 'sh_gate_w': jax.random.normal(ks[5], (C, HS), jnp.float32) * STD, 'sh_up_w': jax.random.normal(ks[6], (C, HS), jnp.float32) * STD, 'sh_down_w': jax.random.normal(ks[7], (HS, C), jnp.float32) * STD}
    _L2_ffn_in = _L2_ffn_setup()
    _L2_c = _w((lambda *s: np.random.randn(*s).astype(np.float32) * 0.05)(2, 128))
    _L2_wmod = _w((lambda *s: np.random.randn(*s).astype(np.float32) * 0.05)(128, 6 * 128) * 128 ** (-0.5))

    def _L3_attn_setup():
        import jax, jax.numpy as jnp
        import numpy as np
        NUM_HEADS = 16
        EPS = 1e-12

        def _l2norm(t):
            n = jnp.linalg.norm(t, axis=-1, keepdims=True)
            return t / jnp.maximum(n, EPS)
        key = jax.random.key(seed)
        ks = jax.random.split(key, 5)
        N, C, d = (16, 128, 128)
        x = jax.random.normal(ks[0], (N, C, d), dtype=jnp.float32)
        Wq = jax.random.normal(ks[1], (d, d), dtype=jnp.float32) * 0.02
        Wk = jax.random.normal(ks[2], (d, d), dtype=jnp.float32) * 0.02
        Wv = jax.random.normal(ks[3], (d, d), dtype=jnp.float32) * 0.02
        Wo = jax.random.normal(ks[4], (d, d), dtype=jnp.float32) * 0.02
        norm_const = 0.5 * jnp.ones((1, NUM_HEADS, 1, 1), dtype=jnp.float32)
        return {'x': x, 'Wq': Wq, 'Wk': Wk, 'Wv': Wv, 'Wo': Wo, 'norm_const': norm_const}
    _L3_attn_in = _L3_attn_setup()

    def _L3_ffn_setup():
        import jax, jax.numpy as jnp
        import numpy as np
        LORA_DIM = 16
        LORA_TOKEN_INDEX = 1
        B, S, D, H = (4, 256, 128, 512)
        key = jax.random.key(seed)
        ks = jax.random.split(key, 6)
        x = jax.random.normal(ks[0], (B, S, D), dtype=jnp.float32)
        W1 = jax.random.normal(ks[1], (H, D), dtype=jnp.float32) * 0.02
        b1 = jnp.zeros((H,), dtype=jnp.float32)
        W2 = jax.random.normal(ks[2], (D, H), dtype=jnp.float32) * 0.02
        b2 = jnp.zeros((D,), dtype=jnp.float32)
        scale = jnp.asarray(0.001, dtype=jnp.float32)
        return {'x': x, 'W1': W1, 'b1': b1, 'W2': W2, 'b2': b2, 'scale': scale}
    _L3_ffn_in = _L3_ffn_setup()
    _L3_c = _w((lambda *s: np.random.randn(*s).astype(np.float32) * 0.05)(2, 128))
    _L3_wmod = _w((lambda *s: np.random.randn(*s).astype(np.float32) * 0.05)(128, 6 * 128) * 128 ** (-0.5))
    _d = {'L0_attn_query': _L0_attn_in['query'], 'L0_attn_Wq': _L0_attn_in['Wq'], 'L0_attn_Wk': _L0_attn_in['Wk'], 'L0_attn_Wv': _L0_attn_in['Wv'], 'L0_attn_Wo': _L0_attn_in['Wo'], 'L0_attn_lambda_q1': _L0_attn_in['lambda_q1'], 'L0_attn_lambda_k1': _L0_attn_in['lambda_k1'], 'L0_attn_lambda_q2': _L0_attn_in['lambda_q2'], 'L0_attn_lambda_k2': _L0_attn_in['lambda_k2'], 'L0_attn_subln_w': _L0_attn_in['subln_w'], 'L0_ffn_W1': _L0_ffn_in['W1'], 'L0_ffn_b1': _L0_ffn_in['b1'], 'L0_ffn_W2': _L0_ffn_in['W2'], 'L0_ffn_b2': _L0_ffn_in['b2'], 'L0_ffn_scale': _L0_ffn_in['scale'], 'L0_c': _L0_c, 'L0_wmod': _L0_wmod, 'L1_attn_wq_w': _L1_attn_in['wq_w'], 'L1_attn_wq_b': _L1_attn_in['wq_b'], 'L1_attn_wk_w': _L1_attn_in['wk_w'], 'L1_attn_wk_b': _L1_attn_in['wk_b'], 'L1_attn_wv_w': _L1_attn_in['wv_w'], 'L1_attn_wv_b': _L1_attn_in['wv_b'], 'L1_attn_wo_w': _L1_attn_in['wo_w'], 'L1_attn_wo_b': _L1_attn_in['wo_b'], 'L1_ffn_W_r': _L1_ffn_in['W_r'], 'L1_ffn_W_k': _L1_ffn_in['W_k'], 'L1_ffn_W_v': _L1_ffn_in['W_v'], 'L1_ffn_mu_r': _L1_ffn_in['mu_r'], 'L1_ffn_mu_k': _L1_ffn_in['mu_k'], 'L1_c': _L1_c, 'L1_wmod': _L1_wmod, 'L2_attn_w_kv_down': _L2_attn_in['w_kv_down'], 'L2_attn_w_kv_up': _L2_attn_in['w_kv_up'], 'L2_attn_w_q': _L2_attn_in['w_q'], 'L2_attn_w_out': _L2_attn_in['w_out'], 'L2_ffn_router_w': _L2_ffn_in['router_w'], 'L2_ffn_e_bias': _L2_ffn_in['e_bias'], 'L2_ffn_gate_w': _L2_ffn_in['gate_w'], 'L2_ffn_up_w': _L2_ffn_in['up_w'], 'L2_ffn_down_w': _L2_ffn_in['down_w'], 'L2_ffn_sh_gate_w': _L2_ffn_in['sh_gate_w'], 'L2_ffn_sh_up_w': _L2_ffn_in['sh_up_w'], 'L2_ffn_sh_down_w': _L2_ffn_in['sh_down_w'], 'L2_c': _L2_c, 'L2_wmod': _L2_wmod, 'L3_attn_Wq': _L3_attn_in['Wq'], 'L3_attn_Wk': _L3_attn_in['Wk'], 'L3_attn_Wv': _L3_attn_in['Wv'], 'L3_attn_Wo': _L3_attn_in['Wo'], 'L3_attn_norm_const': _L3_attn_in['norm_const'], 'L3_ffn_W1': _L3_ffn_in['W1'], 'L3_ffn_b1': _L3_ffn_in['b1'], 'L3_ffn_W2': _L3_ffn_in['W2'], 'L3_ffn_b2': _L3_ffn_in['b2'], 'L3_ffn_scale': _L3_ffn_in['scale'], 'L3_c': _L3_c, 'L3_wmod': _L3_wmod}
    _x0 = _d['L0_attn_query']
    _d['L0_attn_query'] = jax.random.normal(jax.random.fold_in(jax.random.key(seed), 1), (2, 1024, 128), dtype=_x0.dtype)
    del _x0
    return _d

def reference(L0_attn_query, L0_attn_Wq, L0_attn_Wk, L0_attn_Wv, L0_attn_Wo, L0_attn_lambda_q1, L0_attn_lambda_k1, L0_attn_lambda_q2, L0_attn_lambda_k2, L0_attn_subln_w, L0_ffn_W1, L0_ffn_b1, L0_ffn_W2, L0_ffn_b2, L0_ffn_scale, L0_c, L0_wmod, L1_attn_wq_w, L1_attn_wq_b, L1_attn_wk_w, L1_attn_wk_b, L1_attn_wv_w, L1_attn_wv_b, L1_attn_wo_w, L1_attn_wo_b, L1_ffn_W_r, L1_ffn_W_k, L1_ffn_W_v, L1_ffn_mu_r, L1_ffn_mu_k, L1_c, L1_wmod, L2_attn_w_kv_down, L2_attn_w_kv_up, L2_attn_w_q, L2_attn_w_out, L2_ffn_router_w, L2_ffn_e_bias, L2_ffn_gate_w, L2_ffn_up_w, L2_ffn_down_w, L2_ffn_sh_gate_w, L2_ffn_sh_up_w, L2_ffn_sh_down_w, L2_c, L2_wmod, L3_attn_Wq, L3_attn_Wk, L3_attn_Wv, L3_attn_Wo, L3_attn_norm_const, L3_ffn_W1, L3_ffn_b1, L3_ffn_W2, L3_ffn_b2, L3_ffn_scale, L3_c, L3_wmod):

    def _L0_attn_ref(query, Wq, Wk, Wv, Wo, lambda_q1, lambda_k1, lambda_q2, lambda_k2, subln_w):
        import jax, jax.numpy as jnp
        import numpy as np
        EMBED_DIM = 128
        NUM_HEADS = 16
        DEPTH = 12
        HEAD_DIM = EMBED_DIM // NUM_HEADS // 2
        LAMBDA_INIT = float(0.8 - 0.6 * np.exp(-0.3 * DEPTH))
        B, T = (2, 256)
        Bsz, Tt, E = query.shape
        H, hd = (NUM_HEADS, HEAD_DIM)
        scaling = hd ** (-0.5)
        q = jnp.einsum('bte,fe->btf', query, Wq).reshape(Bsz, Tt, 2 * H, hd).transpose(0, 2, 1, 3)
        k = jnp.einsum('bse,fe->bsf', query, Wk).reshape(Bsz, Tt, 2 * H, hd).transpose(0, 2, 1, 3)
        v = jnp.einsum('bse,fe->bsf', query, Wv).reshape(Bsz, Tt, H, 2 * hd).transpose(0, 2, 1, 3)
        q = q * scaling
        scores = jnp.einsum('bhtd,bhsd->bhts', q, k)
        attn_w = jax.nn.softmax(scores.astype(jnp.float32), axis=-1).astype(q.dtype)
        lam1 = jnp.exp(jnp.sum(lambda_q1 * lambda_k1))
        lam2 = jnp.exp(jnp.sum(lambda_q2 * lambda_k2))
        lam = lam1 - lam2 + LAMBDA_INIT
        aw = attn_w.reshape(Bsz, H, 2, Tt, Tt)
        aw = aw[:, :, 0] - lam * aw[:, :, 1]
        attn = jnp.einsum('bhts,bhsd->bhtd', aw, v)
        x32 = attn.astype(jnp.float32)
        normed = (x32 * jax.lax.rsqrt(jnp.mean(x32 * x32, axis=-1, keepdims=True) + 1e-05)).astype(attn.dtype)
        attn = normed * subln_w
        attn = attn * (1.0 - LAMBDA_INIT)
        out = attn.transpose(0, 2, 1, 3).reshape(Bsz, Tt, H * 2 * hd)
        return jnp.einsum('bte,fe->btf', out, Wo)

    def _L0_ffn_ref(x, W1, b1, W2, b2, scale):
        import jax, jax.numpy as jnp
        import numpy as np
        LORA_DIM = 16
        LORA_TOKEN_INDEX = 1
        B, S, D, H = (4, 256, 128, 512)
        Bx, Sx, Dx = x.shape
        Hx = W1.shape[0]
        lt = jax.lax.dynamic_slice_in_dim(x, LORA_TOKEN_INDEX, LORA_DIM, axis=1)
        even = lt[:, ::2, :]
        odd = lt[:, 1::2, :]
        m1 = (even[:, :4, :, None] * odd[:, :4, None, :]).reshape(Bx, Hx, Dx)
        m2 = (even[:, 4:, :, None] * odd[:, 4:, None, :]).reshape(Bx, Dx, Hx)
        h = jnp.einsum('bsd,hd->bsh', x, W1) + scale * jnp.einsum('bsd,bhd->bsh', x, m1) + b1
        h = jax.nn.gelu(h, approximate=False)
        out = jnp.einsum('bsh,oh->bso', h, W2) + scale * jnp.einsum('bsh,boh->bso', h, m2) + b2
        return out

    def _L1_attn_ref(x, wq_w, wq_b, wk_w, wk_b, wv_w, wv_b, wo_w, wo_b):
        import jax, jax.numpy as jnp
        import numpy as np
        NUM_HEADS = 16
        PAD_ID = 0.0
        B, T, C = x.shape
        H = NUM_HEADS
        Dh = C // H
        scale = Dh ** (-0.5)
        q = (x @ wq_w.T + wq_b).reshape(B, T, H, Dh)
        k = (x @ wk_w.T + wk_b).reshape(B, T, H, Dh)
        v = (x @ wv_w.T + wv_b).reshape(B, T, H, Dh)
        scores = jnp.einsum('bthd,bshd->bhts', q, k) * scale
        key_mask = (x[:, :, 0] != PAD_ID)[:, None, None, :]
        scores = jnp.where(key_mask, scores, -jnp.inf)
        attn = jax.nn.softmax(scores, axis=-1)
        out = jnp.einsum('bhts,bshd->bthd', attn, v).reshape(B, T, C)
        return out @ wo_w.T + wo_b

    def _L1_ffn_ref(x, W_r, W_k, W_v, mu_r, mu_k):
        import jax, jax.numpy as jnp
        import numpy as np
        DIM = 128

        def _reference_tuple_inner(x, W_r, W_k, W_v, mu_r, mu_k):
            B, T, C = x.shape
            x_prev = jnp.concatenate([jnp.zeros((B, 1, C), x.dtype), x[:, :-1, :]], axis=1)
            xr = mu_r * x + (1.0 - mu_r) * x_prev
            xk = mu_k * x + (1.0 - mu_k) * x_prev
            r = jax.nn.sigmoid(jnp.einsum('btc,dc->btd', xr, W_r))
            k = jnp.einsum('btc,dc->btd', xk, W_k)
            k_act = jnp.square(jax.nn.relu(k))
            out = r * jnp.einsum('btc,dc->btd', k_act, W_v)
            new_state = x[:, -1, :]
            return (out, new_state)
        return _reference_tuple_inner(x, W_r, W_k, W_v, mu_r, mu_k)[0]

    def _L2_attn_ref(x, w_kv_down, w_kv_up, w_q, w_out):
        import jax, jax.numpy as jnp
        import numpy as np
        B, T, C = (64, 32, 128)
        N_HEAD, HEAD_SIZE, KV_RANK = (16, 64, 128)
        BLOCK_SIZE = 32
        Bx, Tx, Cx = x.shape
        HD = N_HEAD * HEAD_SIZE
        latent_kv = x @ w_kv_down
        kv = latent_kv @ w_kv_up
        k, v = (kv[..., :HD], kv[..., HD:])
        k = k.reshape(Bx, Tx, N_HEAD, HEAD_SIZE)
        v = v.reshape(Bx, Tx, N_HEAD, HEAD_SIZE)
        q = (x @ w_q).reshape(Bx, Tx, N_HEAD, HEAD_SIZE)
        scale = HEAD_SIZE ** (-0.5)
        att = jnp.einsum('bqhd,bkhd->bhqk', q, k) * scale
        causal = jnp.tril(jnp.ones((Tx, Tx), dtype=bool))
        att = jnp.where(causal, att, -jnp.inf)
        att = jax.nn.softmax(att, axis=-1)
        y = jnp.einsum('bhqk,bkhd->bqhd', att, v)
        y = y.reshape(Bx, Tx, HD)
        return y @ w_out

    def _L2_ffn_ref(x, router_w, e_bias, gate_w, up_w, down_w, sh_gate_w, sh_up_w, sh_down_w):
        import jax, jax.numpy as jnp
        import numpy as np
        B, T, C = (1, 512, 128)
        E, K = (64, 8)
        G, TG = (8, 4)
        H, HS = (64, 256)
        STD = 0.02

        def _route(xf, router_w, e_bias):
            S = xf.shape[0]
            scores = jax.nn.sigmoid(xf @ router_w.T)
            sb = scores + e_bias
            epg = E // G
            grp = jax.lax.top_k(sb.reshape(S, G, epg), K // TG)[0].sum(-1)
            gidx = jax.lax.top_k(grp, TG)[1]
            gmask = jnp.zeros((S, G), bool).at[jnp.arange(S)[:, None], gidx].set(True)
            emask = jnp.repeat(gmask, epg, axis=1)
            masked = jnp.where(emask, sb, -jnp.inf)
            topk_idx = jax.lax.top_k(masked, K)[1]
            w = jnp.take_along_axis(scores, topk_idx, axis=1)
            w = w / (w.sum(-1, keepdims=True) + 1e-20)
            return (topk_idx, w)
        Bq, Tq, Cq = x.shape
        xf = x.reshape(Bq * Tq, Cq)
        shared = jax.nn.silu(xf @ sh_gate_w) * (xf @ sh_up_w) @ sh_down_w
        topk_idx, w = _route(xf, router_w, e_bias)
        fe = topk_idx.reshape(-1)
        order = jnp.argsort(fe, stable=True)
        tok = order // K
        sorted_x = xf[tok]
        group_sizes = jnp.bincount(fe, length=E).astype(jnp.int32)
        g = jax.lax.ragged_dot(sorted_x, gate_w, group_sizes)
        u = jax.lax.ragged_dot(sorted_x, up_w, group_sizes)
        h = jax.nn.silu(g) * u
        o = jax.lax.ragged_dot(h, down_w, group_sizes)
        o = o * w.reshape(-1)[order][:, None]
        routed = jnp.zeros_like(xf).at[tok].add(o)
        return (shared + routed).reshape(Bq, Tq, Cq)

    def _L3_attn_ref(x, Wq, Wk, Wv, Wo, norm_const):
        import jax, jax.numpy as jnp
        import numpy as np
        NUM_HEADS = 16
        EPS = 1e-12

        def _l2norm(t):
            n = jnp.linalg.norm(t, axis=-1, keepdims=True)
            return t / jnp.maximum(n, EPS)
        N, C, d = x.shape
        H = NUM_HEADS
        hd = d // H

        def proj(W):
            return (x @ W.T).reshape(N, C, H, hd).transpose(0, 2, 1, 3)
        q = _l2norm(proj(Wq))
        k = _l2norm(proj(Wk))
        v = proj(Wv)
        v = v / jnp.power(jnp.float32(C), jax.nn.sigmoid(norm_const))
        kv = jnp.einsum('nhcd,nhce->nhde', k, v)
        attn = jnp.einsum('nhcd,nhde->nhce', q, kv)
        out = attn.transpose(0, 2, 1, 3).reshape(N, C, d)
        return out @ Wo.T

    def _L3_ffn_ref(x, W1, b1, W2, b2, scale):
        import jax, jax.numpy as jnp
        import numpy as np
        LORA_DIM = 16
        LORA_TOKEN_INDEX = 1
        B, S, D, H = (4, 256, 128, 512)
        Bx, Sx, Dx = x.shape
        Hx = W1.shape[0]
        lt = jax.lax.dynamic_slice_in_dim(x, LORA_TOKEN_INDEX, LORA_DIM, axis=1)
        even = lt[:, ::2, :]
        odd = lt[:, 1::2, :]
        m1 = (even[:, :4, :, None] * odd[:, :4, None, :]).reshape(Bx, Hx, Dx)
        m2 = (even[:, 4:, :, None] * odd[:, 4:, None, :]).reshape(Bx, Dx, Hx)
        h = jnp.einsum('bsd,hd->bsh', x, W1) + scale * jnp.einsum('bsd,bhd->bsh', x, m1) + b1
        h = jax.nn.gelu(h, approximate=False)
        out = jnp.einsum('bsh,oh->bso', h, W2) + scale * jnp.einsum('bsh,boh->bso', h, m2) + b2
        return out
    x = L0_attn_query
    mod = (_silu(L0_c) @ L0_wmod).reshape(L0_c.shape[0], 6, 1, -1)
    sa, ca, ga, sb, cb, gb = (mod[:, 0], mod[:, 1], mod[:, 2], mod[:, 3], mod[:, 4], mod[:, 5])
    ga = (2 * (ga >= 0) - 1) * jnp.maximum(jnp.abs(ga), 0.25)
    gb = (2 * (gb >= 0) - 1) * jnp.maximum(jnp.abs(gb), 0.25)
    h = _layernorm(x, axis=-1) * (1 + ca) + sa
    x = x + ga * _L0_attn_ref(h, L0_attn_Wq, L0_attn_Wk, L0_attn_Wv, L0_attn_Wo, L0_attn_lambda_q1, L0_attn_lambda_k1, L0_attn_lambda_q2, L0_attn_lambda_k2, L0_attn_subln_w)
    h = _layernorm(x, axis=-1) * (1 + cb) + sb
    x = x + gb * _L0_ffn_ref(h, L0_ffn_W1, L0_ffn_b1, L0_ffn_W2, L0_ffn_b2, L0_ffn_scale)
    mod = (_silu(L1_c) @ L1_wmod).reshape(L1_c.shape[0], 6, 1, -1)
    sa, ca, ga, sb, cb, gb = (mod[:, 0], mod[:, 1], mod[:, 2], mod[:, 3], mod[:, 4], mod[:, 5])
    ga = (2 * (ga >= 0) - 1) * jnp.maximum(jnp.abs(ga), 0.25)
    gb = (2 * (gb >= 0) - 1) * jnp.maximum(jnp.abs(gb), 0.25)
    h = _layernorm(x, axis=-1) * (1 + ca) + sa
    x = x + ga * _L1_attn_ref(h, L1_attn_wq_w, L1_attn_wq_b, L1_attn_wk_w, L1_attn_wk_b, L1_attn_wv_w, L1_attn_wv_b, L1_attn_wo_w, L1_attn_wo_b)
    h = _layernorm(x, axis=-1) * (1 + cb) + sb
    x = x + gb * _L1_ffn_ref(h, L1_ffn_W_r, L1_ffn_W_k, L1_ffn_W_v, L1_ffn_mu_r, L1_ffn_mu_k)
    mod = (_silu(L2_c) @ L2_wmod).reshape(L2_c.shape[0], 6, 1, -1)
    sa, ca, ga, sb, cb, gb = (mod[:, 0], mod[:, 1], mod[:, 2], mod[:, 3], mod[:, 4], mod[:, 5])
    ga = (2 * (ga >= 0) - 1) * jnp.maximum(jnp.abs(ga), 0.25)
    gb = (2 * (gb >= 0) - 1) * jnp.maximum(jnp.abs(gb), 0.25)
    h = _layernorm(x, axis=-1) * (1 + ca) + sa
    x = x + ga * _L2_attn_ref(h, L2_attn_w_kv_down, L2_attn_w_kv_up, L2_attn_w_q, L2_attn_w_out)
    h = _layernorm(x, axis=-1) * (1 + cb) + sb
    x = x + gb * _L2_ffn_ref(h, L2_ffn_router_w, L2_ffn_e_bias, L2_ffn_gate_w, L2_ffn_up_w, L2_ffn_down_w, L2_ffn_sh_gate_w, L2_ffn_sh_up_w, L2_ffn_sh_down_w)
    mod = (_silu(L3_c) @ L3_wmod).reshape(L3_c.shape[0], 6, 1, -1)
    sa, ca, ga, sb, cb, gb = (mod[:, 0], mod[:, 1], mod[:, 2], mod[:, 3], mod[:, 4], mod[:, 5])
    ga = (2 * (ga >= 0) - 1) * jnp.maximum(jnp.abs(ga), 0.25)
    gb = (2 * (gb >= 0) - 1) * jnp.maximum(jnp.abs(gb), 0.25)
    h = _layernorm(x, axis=-1) * (1 + ca) + sa
    x = x + ga * _L3_attn_ref(h, L3_attn_Wq, L3_attn_Wk, L3_attn_Wv, L3_attn_Wo, L3_attn_norm_const)
    h = _layernorm(x, axis=-1) * (1 + cb) + sb
    x = x + gb * _L3_ffn_ref(h, L3_ffn_W1, L3_ffn_b1, L3_ffn_W2, L3_ffn_b2, L3_ffn_scale)
    return x

_drawn_inputs = setup_inputs


def setup_inputs(seed=0):
    import zlib

    import numpy as np

    out = dict(_drawn_inputs(seed))
    spreads = {'L0_attn_subln_w': (1.0, 0.6),
     'L0_ffn_b1': (0.0, 0.8),
     'L0_ffn_b2': (0.0, 0.317),
     'L2_ffn_e_bias': (0.0, 2.0),
     'L3_attn_norm_const': (0.5, 0.6),
     'L3_ffn_b1': (0.0, 2.0),
     'L3_ffn_b2': (0.0, 2.0)}
    factors = {'L0_attn_Wq': 8.0,
     'L0_attn_Wk': 8.0,
     'L0_attn_Wv': 8.0,
     'L0_attn_Wo': 7.964,
     'L0_attn_lambda_q1': 8.0,
     'L0_attn_lambda_k1': 8.0,
     'L0_attn_lambda_q2': 8.0,
     'L0_attn_lambda_k2': 8.0,
     'L0_ffn_W1': 4.094,
     'L0_ffn_W2': 3.528,
     'L1_attn_wq_b': 6.869,
     'L1_attn_wk_b': 64.0,
     'L1_ffn_W_r': 8.0,
     'L1_ffn_W_k': 3.009,
     'L1_ffn_W_v': 2.813,
     'L1_ffn_mu_r': 8.0,
     'L1_ffn_mu_k': 4.841,
     'L2_attn_w_kv_down': 5.385,
     'L2_attn_w_kv_up': 4.764,
     'L2_attn_w_q': 8.0,
     'L2_attn_w_out': 4.901,
     'L2_ffn_router_w': 30.862,
     'L2_ffn_gate_w': 26.622,
     'L2_ffn_up_w': 23.838,
     'L2_ffn_down_w': 23.767,
     'L2_ffn_sh_gate_w': 8.0,
     'L2_ffn_sh_up_w': 8.0,
     'L2_ffn_sh_down_w': 8.0,
     'L2_c': 4.752,
     'L2_wmod': 4.949,
     'L3_attn_Wq': 8.0,
     'L3_attn_Wk': 8.0,
     'L3_attn_Wv': 8.0,
     'L3_attn_Wo': 8.0,
     'L3_ffn_W1': 12.667,
     'L3_ffn_W2': 3.677}
    for name, (base, spread) in spreads.items():
        noise = np.random.default_rng([zlib.crc32(name.encode()), seed]).standard_normal(out[name].shape)
        drawn = base * np.exp(spread * noise) if base else spread * noise
        out[name] = jnp.asarray(drawn.astype(out[name].dtype))
    for name, factor in factors.items():
        out[name] = (out[name] * factor).astype(out[name].dtype)
    return out
```

```python
import math

import numpy as np

import concourse.bass as bass
from concourse import mybir
from contextlib import ExitStack

F32 = mybir.dt.float32
BF16 = mybir.dt.bfloat16
ALU = mybir.AluOpType
ACT = mybir.ActivationFunctionType
X_AXIS = mybir.AxisListType.X

C = 128
B = 2
T = 1024
N = B * T
CW = 512
NC = N // CW
TB = N // 128
HEADS = 16
LAYERS = 4
NEG = -1e30
LN_EPS = 1e-5
LAMBDA_INIT = float(0.8 - 0.6 * np.exp(-0.3 * 12))
HID = 512
HB = HID // C
E = 64
EH = 64
EP = E // 2
GRP = 8
PH = 64
HALF = T // 2


class NormSems:

    def __init__(self, nc):
        sem = lambda n: nc.alloc_semaphore("norm_" + n)
        self.mean, self.centred, self.squared, self.var = sem("mean"), sem("centred"), sem("squared"), sem("var")
        self.dev, self.step, self.out = sem("dev"), sem("step"), sem("out")
        self.calls = 0


class Residents:

    def __init__(self, nc):
        sb = lambda n, s, d=F32: nc.alloc_sbuf_tensor(n + "_res", s, d)
        self.x = sb("x", [C, B, T])
        self.h = sb("h", [C, B, T + 4])
        self.mod = sb("mod", [C, LAYERS, 6, B])
        self.scale1 = sb("scale1", [C, LAYERS, 2, B])
        self.gate = sb("gate", [C, LAYERS * 2 * B])
        self.ident = sb("ident", [128, 128])
        self.identb = sb("identb", [128, 128], BF16)
        self.ones = sb("ones", [128, 128])
        self.blk8 = sb("blk8", [128, 128])
        self.eps = sb("eps", [128, 1])
        self.ps = nc.alloc_psum_tensor("ps", [128, 8, CW], F32)
        self.norm_sems = NormSems(nc)


class Attn:

    def __init__(self, nc, name, rows, dim, groups, heads_of_group, mask):
        self.name, self.rows, self.dim, self.groups = name, rows, dim, groups
        self.row_tiles = 4 * rows // 128
        self.heads_of_group, self.mask = heads_of_group, mask
        self.parts_dram = nc.dram_tensor(name + "parts", [2, 3, B * C, T], BF16, kind="Internal").ap()
        self.mask_dram = nc.dram_tensor(name + "mask", [groups, T], BF16, kind="Internal").ap() if mask else None
        self.ones_set = nc.alloc_semaphore(name + "ones_set")
        self.dve_extra = nc.alloc_semaphore(name + "q_scaled")


def chunk(c):
    return c // 2, slice((c % 2) * CW, (c % 2) * CW + CW)


def setup_stage(nc, R, dram):
    with ExitStack() as ctx:
        sb = lambda n, s, d=F32: ctx.enter_context(nc.sbuf_tensor(n, s, d))
        wmod = sb("wmod", [C, LAYERS, 6 * C])
        cT = sb("cT", [C, LAYERS, B])
        sil = sb("sil", [C, LAYERS, B])
        sgn = sb("sgn", [C, LAYERS, 2, B])
        mag = sb("mag", [C, LAYERS, 2, B])
        raw = sb("raw", [C, LAYERS, 2, B])
        loaded = nc.alloc_semaphore("setup_loaded")
        silu_done = nc.alloc_semaphore("silu_done")
        mod_done = nc.alloc_semaphore("mod_products_done")
        dve_step = nc.alloc_semaphore("setup_dve_step")
        ones_done = nc.alloc_semaphore("setup_ones_done")
        cast_loaded = nc.alloc_semaphore("setup_cast_loaded")
        loads = [(R.x[:], dram["xT"]), (R.ident[:], dram["ident"]), (R.blk8[:], dram["blk8"])]
        loads += [(wmod[:, l, :], dram[f"L{l}_wmod"]) for l in range(LAYERS)]
        loads += [(cT[:, l, :], dram[f"L{l}_cT"]) for l in range(LAYERS)]
        with nc.Block() as block:

            @block.sync
            def _(sp):
                for dst, src in loads:
                    sp.dma_start(dst, src).then_inc(loaded, 16)
                sp.wait_ge(loaded, 16 * len(loads))

            @block.gpsimd
            def _(pool):
                pool.memset(R.ones[:], 1.0 / C).then_inc(ones_done, 1)
                pool.memset(R.h[:, :, 0:4], 0.0).then_inc(ones_done, 1)
                pool.memset(R.eps[:], LN_EPS).then_inc(ones_done, 1)
                pool.dma_start(R.identb[:], dram["ident"]).then_inc(cast_loaded, 16)
                pool.wait_ge(cast_loaded, 16)

            @block.scalar
            def _(act):
                act.wait_ge(loaded, 16 * len(loads))
                act.activation(sil[:], cT[:], ACT.Silu).then_inc(silu_done, 1)

            @block.tensor
            def _(pe):
                pe.wait_ge(loaded, 16 * len(loads))
                pe.wait_ge(silu_done, 1)
                for l in range(LAYERS):
                    for k in range(6):
                        col = (l * 6 + k) * B
                        last = pe.matmul(R.ps[:, 0, col:col + B], wmod[:, l, k * C:(k + 1) * C], sil[:, l, :],
                                         start=True, stop=True)
                last.then_inc(mod_done, 1)

            @block.vector
            def _(dve):
                dve.wait_ge(mod_done, 1)
                dve.tensor_copy(R.mod[:], R.ps[:, 0, 0:LAYERS * 6 * B].rearrange("p (l k b) -> p l k b", l=LAYERS, k=6))\
                   .then_inc(dve_step, 1)
                dve.wait_ge(dve_step, 1)
                gates = R.mod[:, :, 2:6:3, :]
                scales = R.mod[:, :, 1:5:3, :]
                dve.tensor_scalar(sgn[:], gates, 0.0, 2.0, ALU.is_ge, ALU.mult).then_inc(dve_step, 1)
                dve.tensor_copy(raw[:], gates).then_inc(dve_step, 1)
                dve.wait_ge(dve_step, 3)
                flat = lambda x: x[:].rearrange("p l k b -> p (l k b)")
                dve.scalar_tensor_tensor(flat(mag), flat(sgn), -1.0, flat(raw), ALU.add, ALU.mult).then_inc(dve_step, 1)
                dve.wait_ge(dve_step, 4)
                dve.tensor_scalar(mag[:], mag[:], 0.25, None, ALU.max).then_inc(dve_step, 1)
                dve.wait_ge(dve_step, 5)
                dve.scalar_tensor_tensor(R.gate[:], flat(sgn), -1.0, flat(mag), ALU.add, ALU.mult).then_inc(dve_step, 1)
                dve.tensor_scalar(R.scale1[:], scales, 1.0, None, ALU.add).then_inc(dve_step, 1)


def mod_cols(R, layer, half, b):
    k = (layer * 2 + half) * B + b
    return R.mod[:, layer, 3 * half, b:b + 1], R.scale1[:, layer, half, b:b + 1], R.gate[:, k:k + 1]


def norm_stage(nc, R, layer, half):
    S = R.norm_sems
    n0 = S.calls * NC
    S.calls += 1
    with ExitStack() as ctx:
        xc = ctx.enter_context(nc.sbuf_tensor(f"ln_xc{n0}", [C, NC, CW], F32))
        sq = ctx.enter_context(nc.sbuf_tensor(f"ln_sq{n0}", [C, NC, CW], F32))
        with nc.Block() as block:

            @block.tensor
            def _(pe):
                for c in range(NC):
                    b, t = chunk(c)
                    pe.matmul(R.ps[:, c, :], R.ones[:], R.x[:, b, t], start=True, stop=True).then_inc(S.mean, 1)
                for c in range(NC):
                    pe.wait_ge(S.squared, n0 + c + 1)
                    pe.matmul(R.ps[:, 4 + c, :], R.ones[:], sq[:, c, :], start=True, stop=True).then_inc(S.var, 1)

            @block.scalar
            def _(act):
                for c in range(NC):
                    act.wait_ge(S.centred, n0 + c + 1)
                    act.activation(sq[:, c, :], xc[:, c, :], ACT.Square).then_inc(S.squared, 1)
                for c in range(NC):
                    act.wait_ge(S.var, n0 + c + 1)
                    act.activation(sq[:, c, :], R.ps[:, 4 + c, :], ACT.Sqrt, bias=R.eps[:]).then_inc(S.dev, 1)

            @block.vector
            def _(dve):
                for c in range(NC):
                    b, t = chunk(c)
                    dve.wait_ge(S.mean, n0 + c + 1)
                    dve.tensor_tensor(xc[:, c, :], R.x[:, b, t], R.ps[:, c, :], ALU.subtract).then_inc(S.centred, 1)
                for c in range(NC):
                    b, t = chunk(c)
                    shift, scale1, _g = mod_cols(R, layer, half, b)
                    dve.wait_ge(S.dev, n0 + c + 1)
                    dve.reciprocal(R.ps[:, 4 + c, :], sq[:, c, :]).then_inc(S.step, 1)
                    dve.wait_ge(S.step, 2 * (n0 + c) + 1)
                    dve.scalar_tensor_tensor(xc[:, c, :], xc[:, c, :], scale1, R.ps[:, 4 + c, :], ALU.mult, ALU.mult)\
                       .then_inc(S.step, 1)
                    dve.wait_ge(S.step, 2 * (n0 + c) + 2)
                    dve.tensor_scalar(R.h[:, b, 4 + t.start:4 + t.stop], xc[:, c, :], shift, None, ALU.add)\
                       .then_inc(S.out, 1)


def h_chunk(R, c):
    b, t = chunk(c)
    return R.h[:, b, 4 + t.start:4 + t.stop]


def h_block(R, tb):
    b, s = tb // 8, tb % 8
    return R.h[:, b, 4 + s * 128:4 + s * 128 + 128]


def project_stage(nc, R, A, dram, layer):
    pre = f"pj{layer}"
    bias = layer == 1
    q_scale = 4 ** -0.5 if layer == 0 else 8 ** -0.5
    with ExitStack() as ctx:
        sb = lambda n, s, d=F32: ctx.enter_context(nc.sbuf_tensor(pre + n, s, d))
        w = sb("w", [C, 3, C])
        bqk = sb("bqk", [C, 2])
        bv = sb("bv", [128, C])
        full = sb("full", [C, 2, 2, CW])
        rest = sb("rest", [C, 2, 2, CW])
        rest2 = sb("rest2", [C, 2, 2, CW])
        parts = sb("parts", [C, 2, 3, B, T], BF16)
        mrow = sb("mrow", [1, B, T], BF16)
        sem = lambda n: nc.alloc_semaphore(pre + n)
        loaded, qk, full_done, step, stored, vp, v_done = (sem(n) for n in
                                                           ("loaded", "qk", "full", "step", "stored", "vp", "v"))
        loads = [(w[:, i, :], dram[f"L{layer}_w{n}T"]) for i, n in enumerate("qkv")]
        if bias:
            loads += [(bqk[:, i:i + 1], dram[f"L1_b{n}"]) for i, n in enumerate("qk")]
            loads += [(bv[:], dram["L1_bv"].broadcast_to([128, C]))]
        heads = A.heads_of_group
        with nc.Block() as block:

            @block.sync
            def _(sp):
                for dst, src in loads:
                    sp.dma_start(dst, src).then_inc(loaded, 16)
                for c in range(NC):
                    b, t = chunk(c)
                    sp.wait_ge(step, 5 * 2 * (c + 1))
                    for o in range(2):
                        sp.dma_start(A.parts_dram[o, :, b * C:(b + 1) * C, t].rearrange("s f t -> f s t"),
                                     parts[:, o, :, b, t]).then_inc(stored, 16)
                if bias:
                    sp.wait_ge(step, 5 * 2 * NC + 1)
                    for g in range(A.groups // B):
                        sp.dma_start(A.mask_dram[g::A.groups // B, :].unsqueeze(0), mrow[:]).then_inc(stored, 16)
                sp.wait_ge(stored, 16 * (2 * NC + (A.groups // B if bias else 0)))

            @block.tensor
            def _(pe):
                pe.wait_ge(loaded, 16 * len(loads))
                for c in range(NC):
                    for o in range(2):
                        n = 2 * c + o
                        if n >= 4:
                            pe.wait_ge(full_done, n - 3)
                        pe.matmul(R.ps[:, n % 4, :], w[:, o, :], h_chunk(R, c), start=True, stop=True).then_inc(qk, 1)
                for g in range(TB // 4):
                    for i in range(4):
                        last = pe.matmul(R.ps[:, 4 + g, i * C:(i + 1) * C], h_block(R, 4 * g + i), w[:, 2, :],
                                         start=True, stop=True)
                    last.then_inc(vp, 1)

            @block.scalar
            def _(act):
                for c in range(NC):
                    for o in range(2):
                        n = 2 * c + o
                        act.wait_ge(qk, n + 1)
                        if n >= 4:
                            act.wait_ge(step, 5 * (n - 3))
                        if bias:
                            act.activation(full[:, c % 2, o, :], R.ps[:, n % 4, :], ACT.Identity,
                                           bias=bqk[:, o:o + 1]).then_inc(full_done, 1)
                        else:
                            act.activation(full[:, c % 2, o, :], R.ps[:, n % 4, :], ACT.Copy,
                                           scale=q_scale if o == 0 else 1.0).then_inc(full_done, 1)

            @block.vector
            def _(dve):
                done = 0
                for c in range(NC):
                    b, t = chunk(c)
                    for o in range(2):
                        dve.wait_ge(full_done, 2 * c + o + 1)
                        f = full[:, c % 2, o, :]
                        if bias and o == 0:
                            dve.tensor_scalar(f, f, q_scale, None, ALU.mult).then_inc(A.dve_extra, 1)
                            dve.wait_ge(A.dve_extra, c + 1)
                        r, r2 = rest[:, c % 2, o, :], rest2[:, c % 2, o, :]
                        p = [parts[:, o, s, b, t] for s in range(3)]
                        for op in ((p[0], f), (r, f, p[0]), (p[1], r), (r2, r, p[1]), (p[2], r2)):
                            if len(op) == 2:
                                dve.tensor_copy(*op).then_inc(step, 1)
                            else:
                                dve.tensor_tensor(*op, ALU.subtract).then_inc(step, 1)
                            done += 1
                            dve.wait_ge(step, done)
                if bias:
                    dve.tensor_scalar(mrow[:], R.h[0:1, :, 4:4 + T], 0.0, NEG, ALU.is_equal, ALU.mult)\
                       .then_inc(step, 1)
                for g in range(TB // 4):
                    dve.wait_ge(vp, g + 1)
                    b, s = g // 2, (g % 2) * 4
                    for i in range(4):
                        src = R.ps[:, 4 + g, i * C:(i + 1) * C].rearrange("p (g h c) -> p g h c", h=heads, c=8)
                        dst = A.v[:, b * (A.groups // B):(b + 1) * (A.groups // B), s + i, :, 0:8]
                        if bias:
                            dve.tensor_tensor(dst, src, bv[:].rearrange("p (g h c) -> p g h c", h=heads, c=8),
                                              ALU.add).then_inc(v_done, 1)
                        else:
                            dve.tensor_copy(dst, src).then_inc(v_done, 1)

            @block.gpsimd
            def _(pool):
                pool.memset(A.v[:, :, :, :, 8:9], 1.0).then_inc(A.ones_set, 1)


def softmax_stage(nc, R, A, dram):
    pre, RT, W, D, NG = A.name, A.row_tiles, A.rows, A.dim, A.groups
    HG = A.heads_of_group
    UNITS = 2 * NG
    QP, KP = 3, 3 + 3 * D
    with ExitStack() as ctx:
        sb = lambda n, s, d=F32: ctx.enter_context(nc.sbuf_tensor(pre + n, s, d))
        sem = lambda n: nc.alloc_semaphore(pre + n)
        q = sb("q", [128, 2, RT, T], BF16)
        k = sb("k", [128, 2, 4, T], BF16)
        qm = sb("qm", [128, 2, RT, CW], BF16)
        vst = sb("vst", [128, 2, 8, HG, 32])
        p = sb("p", [128, 2, 4, CW])
        o = sb("o", [128, 2, CW])
        rec = sb("rec", [128, CW])
        nm = sb("nm", [128, 2, 4, 4])
        m1 = sb("m1", [128, 4, 4])
        m2 = sb("m2", [128, 4, 4])
        mt = sb("mt", [128, 4, 4, W], BF16)
        zero = sb("zero", [128, 8, 9])
        rowc = sb("rowc", [128, 5])
        sel = sb("sel", [128, 128])
        const_loaded, zeroed, inited = sem("const"), sem("zeroed"), sem("inited")
        ld = [sem("ld0"), sem("ld1")]
        p1_full, p1_free = sem("p1_full"), sem("p1_free")
        mt_ready, mt_turned, qm_ready = sem("mt_ready"), sem("mt_turned"), sem("qm_ready")
        p2_full, exp_done, pv_done, pv_out = sem("p2_full"), sem("exp_done"), sem("pv_done"), sem("pv_out")
        den_ready, rec_done, on_done, v_ready, pool_step = (sem("den_ready"), sem("rec_done"), sem("on_done"),
                                                            sem("v_ready"), sem("pool_step"))
        MISC = 7
        misc_b = R.ps[:, MISC, :].bitcast(BF16).rearrange("p (r t) -> p r t", r=2)[:, 0:RT, :]
        n_loads = 4 * (6 + (1 if A.mask else 0))
        n_init = 1 + 4

        def head_row(j):
            return (W * j) % 128

        with nc.Block() as block:

            @block.sync
            def _(sp):
                sp.dma_start(rowc[:], dram[pre + "rowc"]).then_inc(const_loaded, 16)
                sp.dma_start(sel[:], dram["den_sel"]).then_inc(const_loaded, 16)
                sp.wait_ge(inited, 2 * n_init)

                def load(idx, slot):
                    for j in range(4):
                        r = head_row(j)
                        f = bass.ds(idx * (4 * D) + j * D, D)
                        qt = q[:, slot, (W * j) // 128, :]
                        kt = k[:, slot, j, :]
                        P = A.parts_dram
                        sp.dma_start(qt[r + QP:r + QP + 3 * D, :], P[0, 0:1, f, :].broadcast_to([3, D, T]))\
                          .then_inc(ld[slot], 16)
                        sp.dma_start(qt[r + KP:r + KP + 2 * D, :], P[0, 1:2, f, :].broadcast_to([2, D, T]))\
                          .then_inc(ld[slot], 16)
                        sp.dma_start(qt[r + KP + 2 * D:r + KP + 3 * D, :], P[0, 2, f, :]).then_inc(ld[slot], 16)
                        sp.dma_start(kt[r + QP:r + QP + 3 * D, :], P[1, 0:3, f, :]).then_inc(ld[slot], 16)
                        sp.dma_start(kt[r + KP:r + KP + 2 * D, :], P[1, 0:2, f, :]).then_inc(ld[slot], 16)
                        sp.dma_start(kt[r + KP + 2 * D:r + KP + 3 * D, :], P[1, 0, f, :]).then_inc(ld[slot], 16)
                        if A.mask:
                            rm = r + 3 + 6 * D
                            sp.dma_start(kt[rm:rm + 1, :], A.mask_dram[bass.ds(idx, 1), :])\
                              .then_inc(ld[slot], 16)

                load(0, 0)
                load(1, 1)
                with sp.Fori(1, NG // 2) as kk:
                    sp.wait_ge(exp_done, kk * 128 - 64)
                    load(kk * 2, 0)
                    sp.wait_ge(exp_done, kk * 128)
                    load(kk * 2 + 1, 1)

            @block.gpsimd
            def _(pool):
                pool.memset(vst[:], 0.0).then_inc(pool_step, 1)
                pool.memset(mt[:], 0.0).then_inc(pool_step, 1)
                pool.memset(zero[:], 0.0).then_inc(pool_step, 1)
                pool.wait_ge(pool_step, 3)

                def stage_v(idx, slot):
                    pool.tensor_tensor(vst[:, slot, :, :, 0:9], A.v[:, bass.ds(idx, 1)].squeeze(1),
                                       zero[:].unsqueeze(2).broadcast_to([128, 8, HG, 9]), ALU.add).then_inc(v_ready, 1)

                def split(kk, w):
                    u = kk * 4 + w
                    pool.wait_ge(p1_free, u * 16 + 16)
                    if not (isinstance(u, int) and u == 0):
                        pool.wait_ge(mt_turned, u)
                    m = nm[:, w % 2]
                    ops = ((mt[:, :, :, 0], m), (m1[:], m, mt[:, :, :, 0]), (mt[:, :, :, 1], m1[:]),
                           (m2[:], m1[:], mt[:, :, :, 1]), (mt[:, :, :, 2], m2[:]))
                    for i, op in enumerate(ops):
                        if len(op) == 2:
                            ins = pool.tensor_tensor(*op, zero[:, 0:4, 0:4], ALU.add)
                        else:
                            ins = pool.tensor_tensor(*op, ALU.subtract)
                        if i == 4:
                            ins.then_inc(mt_ready, 1)
                        else:
                            ins.then_inc(pool_step, 1)
                            pool.wait_ge(pool_step, u * 4 + (4 + i))

                stage_v(0, 0)
                split(0, 0)

                def body(kk, last):
                    for w in range(4):
                        if w % 2 and not (last and w == 3):
                            e = (w + 1) // 2
                            idx = kk * 2 + e
                            if not (isinstance(kk, int) and kk == 0 and e == 1):
                                pool.wait_ge(pv_done, (idx - 1) * 16)
                            stage_v(idx, e % 2)
                        if not (last and w == 3):
                            split(kk, w + 1)

                if NG > 2:
                    body(0, False)
                if NG // 2 > 2:
                    with pool.Fori(1, NG // 2 - 1) as kk:
                        body(kk, False)
                body(NG // 2 - 1, True)

            @block.tensor
            def _(pe):
                def p1_slot(kk, w, i):
                    tb, j = i // 4, i % 4
                    u, g_slot = kk * 4 + w, (w // 2) % 2
                    if i == 0 and w % 2 == 0:
                        pe.wait_ge(ld[g_slot], (kk + (w // 4 + 1)) * (16 * n_loads))
                    if not (isinstance(u, int) and u == 0 and i < 2):
                        pe.wait_ge(p1_free, u * 16 + (i - 1))
                    t0 = (w % 2) * CW + tb * 128
                    for hf in range(2):
                        last = pe.matmul(R.ps[:, 2 * (i % 2) + hf, :], q[:, g_slot, (W * j) // 128, t0:t0 + 128],
                                         k[:, g_slot, j, hf * CW:(hf + 1) * CW], start=True, stop=True)
                    last.then_inc(p1_full, 1)

                def turn(kk, w):
                    u = kk * 4 + w
                    pe.wait_ge(mt_ready, u + 1)
                    if not (isinstance(u, int) and u < 2):
                        pe.wait_ge(rec_done, u - 1)
                    for tb in range(4):
                        for r in range(RT):
                            last = pe.transpose(misc_b[:, r, tb * 128:(tb + 1) * 128],
                                                mt[:].rearrange("p b h w -> p b (h w)")[:, tb, r * 128:(r + 1) * 128],
                                                R.identb[:])
                    last.then_inc(mt_turned, 1)

                def score(kk, w, s, j):
                    u = kk * 4 + w
                    if not (isinstance(u, int) and u == 0 and s == 0 and j < 2):
                        pe.wait_ge(exp_done, u * 32 + (4 * s + j - 1))
                    pe.matmul(R.ps[:, 4 + j % 2, :], k[:, (w // 2) % 2, j, s * 128:(s + 1) * 128],
                              qm[:, w % 2, (W * j) // 128, :], start=True, stop=True).then_inc(p2_full, 1)

                def pv(kk, w, s):
                    u = kk * 4 + w
                    if s == 0:
                        if not (isinstance(u, int) and u == 0):
                            pe.wait_ge(pv_out, u)
                        if w % 2 == 0:
                            pe.wait_ge(v_ready, kk * 2 + (w // 2 + 1))
                    pe.wait_ge(exp_done, u * 32 + (4 * s + 4))
                    for j in range(4):
                        last = pe.matmul(R.ps[32 * j:32 * j + 32, 6, :], vst[:, (w // 2) % 2, s, j * HG // 4, :],
                                         p[:, s % 2, j, :], start=(s == 0), stop=(s == 7))
                    last.then_inc(pv_done, 1)

                def den(kk, w, last_unit=False):
                    u = kk * 4 + w
                    pe.wait_ge(pv_out, u + 1)
                    if not last_unit:
                        pe.wait_ge(qm_ready, u + 2)
                    pe.matmul(R.ps[:, MISC, :], sel[:], o[:, w % 2, :], start=True, stop=True).then_inc(den_ready, 1)

                def body(kk, last, first=False):
                    for w in range(4):
                        pe.wait_ge(qm_ready, kk * 4 + (w + 1))
                        for s in range(8):
                            def ahead(i):
                                n = 4 + 2 * s + i
                                wv = w + 1 + n // 16
                                if not (last and wv > 3):
                                    p1_slot(kk, wv, n % 16)
                            score(kk, w, s, 0)
                            score(kk, w, s, 1)
                            ahead(0)
                            score(kk, w, s, 2)
                            ahead(1)
                            score(kk, w, s, 3)
                            if s > 0:
                                pv(kk, w, s - 1)
                            elif not (first and w == 0):
                                pv(kk, w - 1, 7)
                            if s == 1 and not (first and w == 0):
                                den(kk, w - 1)
                            if s == 6 and not (last and w == 3):
                                turn(kk, w + 1)
                    if last:
                        pv(kk, 3, 7)
                        den(kk, 3, True)

                pe.wait_ge(const_loaded, 32)
                for i in range(16):
                    p1_slot(0, 0, i)
                turn(0, 0)
                for i in range(4):
                    p1_slot(0, 1, i)
                if NG > 2:
                    body(0, False, True)
                if NG // 2 > 2:
                    with pe.Fori(1, NG // 2 - 1) as kk:
                        body(kk, False)
                body(NG // 2 - 1, True)

            @block.scalar
            def _(act):
                act.wait_ge(const_loaded, 32)
                act.wait_ge(zeroed, 2)
                for slot in range(2):
                    act.activation(q[:, slot], q[:, slot], ACT.Identity, bias=rowc[:, 0:1]).then_inc(inited, 1)
                    for j in range(4):
                        act.activation(k[:, slot, j, :], k[:, slot, j, :], ACT.Identity, bias=rowc[:, 1 + j:2 + j])\
                           .then_inc(inited, 1)

                def body(kk, last=False, first=False):
                    for w in range(4):
                        u = kk * 4 + w
                        for s in range(8):
                            if not (first and w == 0 and s < 2):
                                act.wait_ge(pv_done, u * 8 + (s - 1))
                            for j in range(4):
                                act.wait_ge(p2_full, u * 32 + (4 * s + j + 1))
                                act.activation(p[:, s % 2, j, :], R.ps[:, 4 + j % 2, :], ACT.Exp).then_inc(exp_done, 1)

                body(0, first=True)
                with act.Fori(1, NG // 2) as kk:
                    body(kk)

            @block.vector
            def _(dve):
                dve.memset(q[:].bitcast(F32), 0.0).then_inc(zeroed, 1)
                dve.memset(k[:].bitcast(F32), 0.0).then_inc(zeroed, 1)

                def reduce(kk, w, i):
                    u = kk * 4 + w
                    dve.wait_ge(p1_full, u * 16 + (i + 1))
                    dve.tensor_reduce(nm[:, w % 2, i // 4, i % 4:i % 4 + 1], R.ps[:, 2 * (i % 2):2 * (i % 2) + 2, :],
                                      mybir.AxisListType.XY, ALU.max, negate=True).then_inc(p1_free, 1)

                def merge(kk, w):
                    u = kk * 4 + w
                    dve.wait_ge(mt_turned, u + 1)
                    if not (isinstance(u, int) and u < 2):
                        dve.wait_ge(exp_done, u * 32 - 32)
                    t0 = (w % 2) * CW
                    dve.tensor_tensor(qm[:, w % 2], q[:, (w // 2) % 2, :, t0:t0 + CW], misc_b, ALU.add)\
                       .then_inc(qm_ready, 1)

                def take(kk, w):
                    u = kk * 4 + w
                    dve.wait_ge(pv_done, u * 8 + 8)
                    dve.tensor_copy(o[:, w % 2, :], R.ps[:, 6, :]).then_inc(pv_out, 1)

                def divide(kk, w):
                    u = kk * 4 + w
                    dve.wait_ge(den_ready, u + 1)
                    if not (isinstance(u, int) and u == 0):
                        dve.wait_ge(on_done, u)
                    dve.reciprocal(rec[:], R.ps[:, MISC, :]).then_inc(rec_done, 1)
                    dve.wait_ge(rec_done, u + 1)
                    t0 = (w % 2) * CW
                    dve.tensor_tensor(A.on[:, bass.ds(kk * 2 + w // 2, 1), t0:t0 + CW], o[:, w % 2, :].unsqueeze(1),
                                      rec[:].unsqueeze(1), ALU.mult).then_inc(on_done, 1)

                def body(kk, last, first=False):
                    for w in range(4):
                        for s in range(8):
                            for i in range(2):
                                n = 4 + 2 * s + i
                                wv = w + 1 + n // 16
                                if not (last and wv > 3):
                                    reduce(kk, wv, n % 16)
                                if s == 7 and i == 0 and not (last and w == 3):
                                    merge(kk, w + 1)
                            if s == 0 and not (first and w == 0):
                                take(kk, w - 1)
                            if s == 2 and not (first and w == 0):
                                divide(kk, w - 1)
                    if last:
                        take(kk, 3)
                        divide(kk, 3)

                for i in range(16):
                    reduce(0, 0, i)
                merge(0, 0)
                for i in range(4):
                    reduce(0, 1, i)
                if NG > 2:
                    body(0, False, True)
                if NG // 2 > 2:
                    with dve.Fori(1, NG // 2 - 1) as kk:
                        body(kk, False)
                body(NG // 2 - 1, True)


def diff_out_stage(nc, R, A, dram):
    with ExitStack() as ctx:
        sb = lambda n, s, d=F32: ctx.enter_context(nc.sbuf_tensor("do_" + n, s, d))
        sem = lambda n: nc.alloc_semaphore("do_" + n)
        lam = sb("lam", [128, 4, 4])
        prod = sb("prod", [128, 2, 4])
        dots = sb("dots", [128, 2])
        cols = sb("cols", [128, 8])
        pick0 = sb("pick0", [128, 8, C])
        pick = sb("pick", [128, 8, C])
        wo = sb("wo", [C, C])
        a = sb("a", [C, NC, CW])
        sq = sb("sq", [C, NC, CW])
        loaded, step, exped, got, copied, squared, ms, dev, normed, proj, done = (
            sem(n) for n in ("loaded", "step", "exped", "got", "copied", "squared", "ms", "dev", "normed", "proj", "done"))
        loads = [(lam[:, i, :], dram[f"L0_lam{i}"].broadcast_to([128, 4])) for i in range(4)]
        loads += [(cols[:, 0:2], dram["parity"]), (cols[:, 2:3], dram["subln_col"]), (pick0[:], dram["pick"]),
                  (wo[:], dram["L0_woT"])]
        with nc.Block() as block:

            @block.sync
            def _(sp):
                for dst, src in loads:
                    sp.dma_start(dst, src).then_inc(loaded, 16)
                sp.wait_ge(loaded, 16 * len(loads))

            @block.tensor
            def _(pe):
                pe.wait_ge(step, 8)
                for c in range(NC):
                    b, t = chunk(c)
                    for g in range(8):
                        last = pe.matmul(R.ps[:, c, :], pick[:, g, :], A.on[:, b * 8 + g, t], start=(g == 0), stop=(g == 7))
                    last.then_inc(got, 1)
                for c in range(NC):
                    pe.wait_ge(squared, c + 1)
                    pe.matmul(R.ps[:, 4 + c, :], R.blk8[:], sq[:, c, :], start=True, stop=True).then_inc(ms, 1)
                for c in range(NC):
                    pe.wait_ge(normed, c + 1)
                    pe.matmul(R.ps[:, c, :], wo[:], a[:, c, :], start=True, stop=True).then_inc(proj, 1)

            @block.scalar
            def _(act):
                act.wait_ge(step, 2)
                act.activation(dots[:], dots[:], ACT.Exp).then_inc(exped, 1)
                for c in range(NC):
                    act.wait_ge(got, c + 1)
                    act.activation(sq[:, c, :], R.ps[:, c, :], ACT.Square, scale=8 ** -0.5).then_inc(squared, 1)
                for c in range(NC):
                    act.wait_ge(ms, c + 1)
                    act.activation(sq[:, c, :], R.ps[:, 4 + c, :], ACT.Sqrt, bias=R.eps[:]).then_inc(dev, 1)

            @block.vector
            def _(dve):
                dve.wait_ge(loaded, 16 * len(loads))
                dve.tensor_tensor(prod[:], lam[:, 0:3:2, :], lam[:, 1:4:2, :], ALU.mult).then_inc(step, 1)
                dve.wait_ge(step, 1)
                dve.tensor_reduce(dots[:], prod[:], X_AXIS, ALU.add).then_inc(step, 1)
                dve.wait_ge(exped, 1)
                dve.tensor_tensor(cols[:, 3:4], dots[:, 1:2], dots[:, 0:1], ALU.subtract).then_inc(step, 1)
                dve.wait_ge(step, 3)
                dve.tensor_scalar(cols[:, 4:5], cols[:, 3:4], LAMBDA_INIT, None, ALU.subtract).then_inc(step, 1)
                dve.wait_ge(step, 4)
                dve.tensor_tensor(cols[:, 5:6], cols[:, 4:5], cols[:, 1:2], ALU.mult).then_inc(step, 1)
                dve.wait_ge(step, 5)
                dve.tensor_tensor(cols[:, 6:7], cols[:, 5:6], cols[:, 0:1], ALU.add).then_inc(step, 1)
                dve.tensor_scalar(cols[:, 7:8], cols[:, 2:3], 1.0 - LAMBDA_INIT, None, ALU.mult).then_inc(step, 1)
                dve.wait_ge(step, 7)
                dve.tensor_scalar(pick[:], pick0[:], cols[:, 6:7], None, ALU.mult).then_inc(step, 1)
                for c in range(NC):
                    dve.wait_ge(dev, c + 1)
                    dve.reciprocal(sq[:, c, :], sq[:, c, :]).then_inc(copied, 1)
                    dve.wait_ge(copied, c + 1)
                    dve.scalar_tensor_tensor(a[:, c, :], R.ps[:, c, :], cols[:, 7:8], sq[:, c, :], ALU.mult, ALU.mult)\
                       .then_inc(normed, 1)
                for c in range(NC):
                    b, t = chunk(c)
                    dve.wait_ge(proj, c + 1)
                    dve.scalar_tensor_tensor(R.x[:, b, t], R.ps[:, c, :], mod_cols(R, 0, 0, b)[2], R.x[:, b, t],
                                             ALU.mult, ALU.add).then_inc(done, 1)


def out_stage(nc, R, layer, half, name, rhs, parts, w_dram, bias_dram=None):
    with ExitStack() as ctx:
        w = ctx.enter_context(nc.sbuf_tensor(name + "w", [128, parts, C], F32))
        bias = ctx.enter_context(nc.sbuf_tensor(name + "bias", [C, 1], F32))
        tmp = ctx.enter_context(nc.sbuf_tensor(name + "tmp", [C, NC, CW], F32))
        loaded, proj, biased, done = (nc.alloc_semaphore(name + n) for n in ("loaded", "proj", "biased", "done"))
        loads = [(w[:], w_dram)] + ([(bias[:], bias_dram)] if bias_dram is not None else [])
        with nc.Block() as block:

            @block.sync
            def _(sp):
                for dst, src in loads:
                    sp.dma_start(dst, src).then_inc(loaded, 16)
                sp.wait_ge(loaded, 16 * len(loads))

            @block.tensor
            def _(pe):
                pe.wait_ge(loaded, 16 * len(loads))
                for c in range(NC):
                    for i in range(parts):
                        last = pe.matmul(R.ps[:, c, :], w[:, i, :], rhs(i, c), start=(i == 0), stop=(i == parts - 1))
                    last.then_inc(proj, 1)

            @block.vector
            def _(dve):
                dve.wait_ge(loaded, 16 * len(loads))
                for c in range(NC):
                    b, t = chunk(c)
                    gate = mod_cols(R, layer, half, b)[2]
                    dve.wait_ge(proj, c + 1)
                    src = R.ps[:, c, :]
                    if bias_dram is not None:
                        dve.tensor_scalar(tmp[:, c, :], src, bias[:], None, ALU.add).then_inc(biased, 1)
                        dve.wait_ge(biased, c + 1)
                        src = tmp[:, c, :]
                    dve.scalar_tensor_tensor(R.x[:, b, t], src, gate, R.x[:, b, t], ALU.mult, ALU.add).then_inc(done, 1)


def lora_stage(nc, R, layer, dram):
    pre = f"ff{layer}"
    with ExitStack() as ctx:
        sb = lambda n, s, d=F32: ctx.enter_context(nc.sbuf_tensor(pre + n, s, d))
        sem = lambda n: nc.alloc_semaphore(pre + n)
        w1 = sb("w1", [C, HID])
        w2 = sb("w2", [C, HB, C])
        w1e = sb("w1e", [C, B, HID])
        w2e = sb("w2e", [C, B, HB, C])
        b1, b2, scale = sb("b1", [C, HB]), sb("b2", [C, 1]), sb("scale", [128, 1])
        eye8 = sb("eye8", [8, 8])
        even = sb("even", [8, B, C])
        odd = sb("odd", [8, B, C])
        bd = sb("bd", [8, B, 8, C])
        hid = sb("hid", [C, 2, HB, CW])
        tmp = sb("tmp", [C, NC, CW])
        loaded, turned, copied, spread, outer, eff, up, act_done, down, biased, done = (
            sem(n) for n in ("loaded", "turned", "copied", "spread", "outer", "eff", "up", "act", "down", "biased", "done"))
        p = f"L{layer}_f"
        loads = [(w1[:], dram[p + "W1T"]), (w2[:], dram[p + "W2T"]), (b1[:], dram[p + "b1"]), (b2[:], dram[p + "b2"]),
                 (scale[:], dram[p + "scale"].broadcast_to([128, 1])), (eye8[:], dram["ident"][0:8, 0:8])]
        with nc.Block() as block:

            @block.sync
            def _(sp):
                for dst, src in loads:
                    sp.dma_start(dst, src).then_inc(loaded, 16)
                sp.wait_ge(loaded, 16 * len(loads))

            @block.tensor
            def _(pe):
                for b in range(B):
                    for i in range(2):
                        lt = R.h[:, b, 5 + i:5 + i + 15:2]
                        last = pe.transpose(R.ps[0:8, b, i * C:(i + 1) * C], lt, R.ident[:])
                last.then_inc(turned, 1)
                for b in range(B):
                    pe.wait_ge(spread, b + 1)
                    pe.matmul(R.ps[:, 2 + 2 * b, :], odd[:, b, :], bd[:, b, 0:4, :], start=True, stop=True).then_inc(outer, 1)
                    for r in range(HB):
                        last = pe.matmul(R.ps[:, 3 + 2 * b, r * C:(r + 1) * C], odd[:, b, :],
                                         bd[:, b, 4:8, :].rearrange("p i (c r) -> p r i c", r=4)[:, r], start=True, stop=True)
                    last.then_inc(outer, 1)

                def ups(c):
                    for hb in range(HB):
                        n = c * HB + hb
                        if n >= 4:
                            pe.wait_ge(act_done, n - 3)
                        pe.matmul(R.ps[:, hb, :], w1e[:, c // 2, hb * C:(hb + 1) * C], h_chunk(R, c),
                                  start=True, stop=True).then_inc(up, 1)

                def downs(c):
                    pe.wait_ge(act_done, (c + 1) * HB)
                    for hb in range(HB):
                        last = pe.matmul(R.ps[:, 4 + c, :], w2e[:, c // 2, hb, :], hid[:, c % 2, hb, :],
                                         start=(hb == 0), stop=(hb == HB - 1))
                    last.then_inc(down, 1)

                pe.wait_ge(eff, 2 * B)
                for c in range(NC):
                    ups(c)
                    if c:
                        downs(c - 1)
                downs(NC - 1)

            @block.scalar
            def _(act):
                act.wait_ge(loaded, 16 * len(loads))
                for c in range(NC):
                    for hb in range(HB):
                        act.wait_ge(up, c * HB + hb + 1)
                        if c >= 2:
                            act.wait_ge(down, c - 1)
                        act.activation(hid[:, c % 2, hb, :], R.ps[:, hb, :], ACT.Gelu, bias=b1[:, hb:hb + 1])\
                           .then_inc(act_done, 1)

            @block.vector
            def _(dve):
                dve.wait_ge(loaded, 16 * len(loads))
                dve.wait_ge(turned, 1)
                dve.tensor_copy(even[:], R.ps[0:8, 0:B, 0:C]).then_inc(copied, 1)
                dve.tensor_copy(odd[:], R.ps[0:8, 0:B, C:2 * C]).then_inc(copied, 1)
                dve.wait_ge(copied, 2)
                for b in range(B):
                    dve.tensor_tensor(bd[:, b], even[:, b, :].unsqueeze(1).broadcast_to([8, 8, C]),
                                      eye8[:].unsqueeze(2).broadcast_to([8, 8, C]), ALU.mult).then_inc(spread, 1)
                for b in range(B):
                    for i, (w, we) in enumerate(((w1[:], w1e[:, b]), (w2[:], w2e[:, b]))):
                        dve.wait_ge(outer, 2 * b + i + 1)
                        if i:
                            w, we = w.rearrange("p r o -> p (r o)"), we.rearrange("p r o -> p (r o)")
                        dve.scalar_tensor_tensor(we, R.ps[:, 2 + 2 * b + i, :], scale[:], w, ALU.mult, ALU.add)\
                           .then_inc(eff, 1)
                for c in range(NC):
                    b, t = chunk(c)
                    dve.wait_ge(down, c + 1)
                    dve.tensor_scalar(tmp[:, c, :], R.ps[:, 4 + c, :], b2[:], None, ALU.add).then_inc(biased, 1)
                    dve.wait_ge(biased, c + 1)
                    dve.scalar_tensor_tensor(R.x[:, b, t], tmp[:, c, :], mod_cols(R, layer, 1, b)[2], R.x[:, b, t],
                                             ALU.mult, ALU.add).then_inc(done, 1)


def mix_stage(nc, R, dram):
    with ExitStack() as ctx:
        sb = lambda n, s, d=F32: ctx.enter_context(nc.sbuf_tensor("mx_" + n, s, d))
        sem = lambda n: nc.alloc_semaphore("mx_" + n)
        w = sb("w", [C, 3, C])
        mu = sb("mu", [C, 4])
        own = sb("own", [C, 2, NC, CW])
        mixed = sb("mixed", [C, 2, NC, CW])
        r = sb("r", [C, NC, CW])
        k = sb("k", [C, NC, CW])
        k2 = sb("k2", [C, NC, CW])
        loaded, inv, part, mix, prod, sig, relu, sqd, vprod, step, done = (
            sem(n) for n in ("loaded", "inv", "part", "mix", "prod", "sig", "relu", "sqd", "vprod", "step", "done"))
        loads = [(w[:, i, :], dram[f"L1_W{n}T"]) for i, n in enumerate("rkv")]
        loads += [(mu[:, i:i + 1], dram[f"L1_mu{n}"]) for i, n in enumerate("rk")]
        with nc.Block() as block:

            @block.sync
            def _(sp):
                for dst, src in loads:
                    sp.dma_start(dst, src).then_inc(loaded, 16)
                sp.wait_ge(loaded, 16 * len(loads))

            @block.tensor
            def _(pe):
                for c in range(NC):
                    for i in range(2):
                        pe.wait_ge(mix, 2 * c + i + 1)
                        pe.matmul(R.ps[:, 2 * (c % 2) + i, :], w[:, i, :], mixed[:, i, c, :], start=True, stop=True)\
                          .then_inc(prod, 1)
                    if c == 1:
                        pe.wait_ge(sig, 2)
                        pe.wait_ge(relu, 2)
                for c in range(NC):
                    pe.wait_ge(sqd, c + 1)
                    pe.matmul(R.ps[:, 4 + c, :], w[:, 2, :], k2[:, c, :], start=True, stop=True).then_inc(vprod, 1)

            @block.scalar
            def _(act):
                for c in range(NC):
                    act.wait_ge(prod, 2 * c + 1)
                    act.activation(r[:, c, :], R.ps[:, 2 * (c % 2), :], ACT.Sigmoid).then_inc(sig, 1)
                    act.wait_ge(prod, 2 * c + 2)
                    act.activation(k[:, c, :], R.ps[:, 2 * (c % 2) + 1, :], ACT.Relu).then_inc(relu, 1)

            @block.vector
            def _(dve):
                dve.wait_ge(loaded, 16 * len(loads))
                dve.tensor_scalar(mu[:, 2:4], mu[:, 0:2], -1.0, 1.0, ALU.mult, ALU.add).then_inc(inv, 1)
                dve.wait_ge(inv, 1)
                for c in range(NC):
                    b, t = chunk(c)
                    before = R.h[:, b, 3 + t.start:3 + t.stop]
                    for i in range(2):
                        dve.tensor_scalar(own[:, i, c, :], h_chunk(R, c), mu[:, i:i + 1], None, ALU.mult).then_inc(part, 1)
                        dve.wait_ge(part, 2 * c + i + 1)
                        dve.scalar_tensor_tensor(mixed[:, i, c, :], before, mu[:, 2 + i:3 + i], own[:, i, c, :],
                                                 ALU.mult, ALU.add).then_inc(mix, 1)
                for c in range(NC):
                    dve.wait_ge(relu, c + 1)
                    dve.tensor_tensor(k2[:, c, :], k[:, c, :], k[:, c, :], ALU.mult).then_inc(sqd, 1)
                for c in range(NC):
                    b, t = chunk(c)
                    dve.wait_ge(vprod, c + 1)
                    dve.wait_ge(sqd, c + 1)
                    dve.scalar_tensor_tensor(k[:, c, :], R.ps[:, 4 + c, :], mod_cols(R, 1, 1, b)[2], r[:, c, :],
                                             ALU.mult, ALU.mult).then_inc(step, 1)
                    dve.wait_ge(step, c + 1)
                    dve.tensor_tensor(R.x[:, b, t], R.x[:, b, t], k[:, c, :], ALU.add).then_inc(done, 1)


def latent_stage(nc, R, dram, lat):
    with ExitStack() as ctx:
        w = ctx.enter_context(nc.sbuf_tensor("ltw", [C, C], F32))
        loaded, prod, done = (nc.alloc_semaphore("lt_" + n) for n in ("loaded", "prod", "done"))
        with nc.Block() as block:

            @block.sync
            def _(sp):
                sp.dma_start(w[:], dram["L2_kv_down"]).then_inc(loaded, 16)

            @block.tensor
            def _(pe):
                pe.wait_ge(loaded, 16)
                for c in range(NC):
                    pe.matmul(R.ps[:, c, :], w[:], h_chunk(R, c), start=True, stop=True).then_inc(prod, 1)

            @block.scalar
            def _(act):
                for c in range(NC):
                    b, t = chunk(c)
                    act.wait_ge(prod, c + 1)
                    act.activation(lat[:, b, t], R.ps[:, c, :], ACT.Copy).then_inc(done, 1)


def causal_stage(nc, R, dram, lat, y):
    pre = "ca"
    with ExitStack() as ctx:
        sb = lambda n, s, d=F32: ctx.enter_context(nc.sbuf_tensor(pre + n, s, d))
        sem = lambda n: nc.alloc_semaphore(pre + n)
        w = sb("w", [C, 3, C])
        q = sb("q", [PH + 1, 4, T])
        k = sb("k", [PH + 1, 4, T])
        v = sb("v", [128, 4, 8, C])
        p = sb("p", [128, 4, CW])
        nm = sb("nm", [128, 8, PH + 1])
        rec = sb("rec", [128, CW])
        one, tick = sb("one", [1, 1]), sb("tick", [1, 1])
        late = sb("late", [128, 128], BF16)
        lateT = sb("lateT", [128, 128], BF16)
        const_loaded, w_loaded, ones_set = sem("const"), sem("w_loaded"), sem("ones_set")
        pj, pj_a, pj_d = sem("pj"), sem("pj_a"), sem("pj_d")
        p1_full, p1_free, turned, row_zero = sem("p1_full"), sem("p1_free"), sem("turned"), sem("row_zero")
        p2_full, exp_done, pv_done, rec_done, y_done = (sem("p2_full"), sem("exp_done"), sem("pv_done"),
                                                        sem("rec_done"), sem("y_done"))
        STEPS = HEADS // 2
        PJ = 12
        chunks = [(th, s) for th in range(2) for s in range(4 * th + 4)]
        P2 = len(chunks)
        after = {0: 0, 1: 1, 2: 2, 3: 3, 5: 4, 6: 5, 7: 6, 9: 7}

        with nc.Block() as block:

            @block.sync
            def _(sp):
                def load(hp):
                    for i, n in enumerate(("q", "k", "v")):
                        sp.dma_start(w[:, i, :], dram[f"L2_w{n}"][:, bass.ds(hp * C, C)]).then_inc(w_loaded, 16)

                load(0)
                with sp.Fori(1, STEPS) as hp:
                    sp.wait_ge(pj, hp * PJ)
                    load(hp)

            @block.gpsimd
            def _(pool):
                pool.dma_start(late[:], dram["late"]).then_inc(const_loaded, 16)
                pool.dma_start(lateT[:], dram["lateT"]).then_inc(const_loaded, 16)
                pool.memset(nm[:], 0.0).then_inc(ones_set, 1)
                pool.wait_ge(ones_set, 1)
                pool.memset(v[:], 1.0).then_inc(ones_set, 1)
                pool.wait_ge(ones_set, 2)
                pool.memset(k[PH:PH + 1], 1.0).then_inc(ones_set, 1)
                pool.memset(one[:], 1.0).then_inc(ones_set, 1)
                pool.memset(q[PH:PH + 1], 0.0).then_inc(row_zero, 1)
                pool.wait_ge(ones_set, 4)
                with pool.Fori(1, STEPS) as hp:
                    pool.wait_ge(exp_done, hp * (4 * P2))
                    pool.tensor_tensor(tick[:], one[:], one[:], ALU.add).then_inc(row_zero, 1)
                    pool.memset(q[PH:PH + 1], 0.0).then_inc(row_zero, 1)

            @block.tensor
            def _(pe):
                def project(hp):
                    pe.wait_ge(w_loaded, hp * 48 + 48)
                    for n in range(PJ):
                        if n >= 4:
                            pe.wait_ge(pj_d if n % 2 else pj_a, hp * PJ + (n // 2 * 2 - 2))
                        if n < 8:
                            b, t = chunk(n % 4)
                            pe.matmul(R.ps[:, n % 4, :], w[:, n // 4, :], h_chunk(R, n) if n < 4 else lat[:, b, t],
                                      start=True, stop=True).then_inc(pj, 1)
                        else:
                            b, s0 = (n - 8) // 2, (n - 8) % 2 * 4
                            for i in range(4):
                                last = pe.matmul(R.ps[:, n % 4, i * C:(i + 1) * C],
                                                 lat[:, b, (s0 + i) * 128:(s0 + i + 1) * 128], w[:, 2, :],
                                                 start=True, stop=True)
                            last.then_inc(pj, 1)

                def p1_block(hp, u, tb):
                    if not (u == 0 and tb < 2):
                        pe.wait_ge(p1_free, hp * 36 + (9 * u + tb - 1))
                    base = 2 * ((9 * u + tb) % 2)
                    qt = q[0:PH + 1, u, tb * 128:(tb + 1) * 128]
                    full = (tb + 1) * 128
                    for c0 in range(0, full, CW):
                        n = min(CW, full - c0)
                        diag = c0 + n == full
                        if diag:
                            pe.matmul(R.ps[:, base + c0 // CW, n - 128:n], R.identb[:], late[:],
                                      start=True, stop=False, skip_group_check=True)
                        last = pe.matmul(R.ps[:, base + c0 // CW, 0:n], qt, k[0:PH + 1, u, c0:c0 + n],
                                         start=not diag, stop=True, skip_group_check=True)
                    last.then_inc(p1_full, 1)

                def turn(hp, u):
                    pe.wait_ge(p1_free, hp * 36 + (9 * u + 8))
                    base = 2 * ((9 * u + 8) % 2)
                    for tb in range(8):
                        last = pe.transpose(R.ps[0:PH + 1, base + tb // 4, (tb % 4) * 128:(tb % 4 + 1) * 128],
                                            nm[:, tb, :], R.ident[:])
                    last.then_inc(turned, 1)

                def score(hp, u, n):
                    th, s = chunks[n]
                    c0 = max(th * CW, s * 128)
                    wd = (th + 1) * CW - c0
                    if not (isinstance(hp, int) and hp == 0 and u == 0 and n < 2):
                        pe.wait_ge(exp_done, hp * (4 * P2) + (u * P2 + n - 1))
                    diag = s * 128 >= th * CW
                    if diag:
                        pe.matmul(R.ps[:, 4 + n % 2, 0:128], R.identb[:], lateT[:], start=True, stop=False,
                                  skip_group_check=True)
                    pe.matmul(R.ps[:, 4 + n % 2, 0:wd], k[0:PH + 1, u, s * 128:(s + 1) * 128],
                              q[0:PH + 1, u, c0:c0 + wd], start=not diag, stop=True,
                              skip_group_check=True).then_inc(p2_full, 1)

                def pv(hp, u, n):
                    th, s = chunks[n]
                    c0 = max(th * CW, s * 128)
                    if s == 0 and not (isinstance(hp, int) and hp == 0 and u == 0):
                        pe.wait_ge(y_done, hp * 8 + (2 * u + th - 1))
                    pe.wait_ge(exp_done, hp * (4 * P2) + (u * P2 + n + 1))
                    pe.matmul(R.ps[:, 6 + th, c0 - th * CW:CW], v[:, u, s, :], p[:, n % 4, 0:(th + 1) * CW - c0],
                              start=(s == 0), stop=(s == 4 * th + 3)).then_inc(pv_done, 1)

                def step(hp):
                    project(hp)
                    pe.wait_ge(pj_a, hp * PJ + PJ)
                    pe.wait_ge(pj_d, hp * PJ + PJ)
                    pe.wait_ge(row_zero, hp * 2 + 1)
                    for tb in range(8):
                        p1_block(hp, 0, tb)
                    turn(hp, 0)
                    for u in range(4):
                        pe.wait_ge(p1_free, hp * 36 + 9 * (u + 1))
                        for n in range(P2):
                            score(hp, u, n)
                            if n:
                                pv(hp, u, n - 1)
                            if n in after and u < 3:
                                p1_block(hp, u + 1, after[n])
                        pv(hp, u, P2 - 1)
                        if u < 3:
                            turn(hp, u + 1)

                pe.wait_ge(const_loaded, 32)
                pe.wait_ge(ones_set, 3)
                step(0)
                with pe.Fori(1, STEPS) as hp:
                    step(hp)

            def copy_out(n, hh):
                if n < 8:
                    b, t = chunk(n % 4)
                    dst = (q if n < 4 else k)[0:PH, 2 * hh + b, t]
                    src = R.ps[PH * hh:PH * hh + PH, n % 4, :]
                    scale = PH ** -0.5 if n < 4 else 1.0
                else:
                    b, s0 = (n - 8) // 2, (n - 8) % 2 * 4
                    dst = v[:, 2 * hh + b, s0:s0 + 4, PH * hh:PH * hh + PH]
                    src = R.ps[:, n % 4, :].rearrange("p (s c) -> p s c", s=4)[:, :, PH * hh:PH * hh + PH]
                    scale = 1.0
                return dst, src, scale

            @block.scalar
            def _(act):
                def step(hp):
                    for n in range(PJ):
                        if n % 2 == 0:
                            act.wait_ge(pj, hp * PJ + (n + 1))
                            for hh in range(2):
                                dst, src, scale = copy_out(n, hh)
                                act.activation(dst, src, ACT.Copy, scale=scale).then_inc(pj_a, 1)
                    for u in range(4):
                        for n in range(P2):
                            wd = (chunks[n][0] + 1) * CW - max(chunks[n][0] * CW, chunks[n][1] * 128)
                            if not (isinstance(hp, int) and hp == 0 and u == 0 and n < 4):
                                act.wait_ge(pv_done, hp * (4 * P2) + (u * P2 + n - 3))
                            act.wait_ge(p2_full, hp * (4 * P2) + (u * P2 + n + 1))
                            act.activation(p[:, n % 4, 0:wd], R.ps[:, 4 + n % 2, 0:wd], ACT.Exp).then_inc(exp_done, 1)

                act.wait_ge(ones_set, 3)
                step(0)
                with act.Fori(1, STEPS) as hp:
                    step(hp)

            @block.vector
            def _(dve):
                def reduce(hp, u, tb):
                    full = (tb + 1) * 128
                    base = 2 * ((9 * u + tb) % 2)
                    dve.wait_ge(p1_full, hp * 32 + (8 * u + tb + 1))
                    if not (isinstance(hp, int) and hp == 0 and u == 0):
                        dve.wait_ge(turned, hp * 4 + u)
                    src = R.ps[:, base:base + 2, :].rearrange("p a c -> p (a c)")[:, 0:full]
                    dve.tensor_reduce(nm[:, tb, PH:PH + 1], src, X_AXIS, ALU.max, negate=True).then_inc(p1_free, 1)

                def set_row(hp, u):
                    base = 2 * ((9 * u + 8) % 2)
                    dve.wait_ge(turned, hp * 4 + (u + 1))
                    dve.tensor_copy(q[PH:PH + 1, u, :].rearrange("p (a c) -> p a c", a=2), R.ps[PH:PH + 1, base:base + 2, :])\
                       .then_inc(p1_free, 1)

                def finish(hp, u, th):
                    hh, b = u // 2, u % 2
                    up, dn = (slice(0, PH), slice(PH, 2 * PH)) if hh == 0 else (slice(PH, 2 * PH), slice(0, PH))
                    dve.wait_ge(pv_done, hp * (4 * P2) + (u * P2 + (12 if th else 4)))
                    if not (isinstance(hp, int) and hp == 0 and u == 0 and th == 0):
                        dve.wait_ge(y_done, hp * 8 + (2 * u + th))
                    dve.reciprocal(rec[up, :], R.ps[dn, 6 + th, :]).then_inc(rec_done, 1)
                    dve.wait_ge(rec_done, hp * 8 + (2 * u + th + 1))
                    dve.tensor_tensor(y[up, bass.ds(hp, 1), b, th * CW:(th + 1) * CW], R.ps[up, 6 + th, :].unsqueeze(1),
                                      rec[up, :].unsqueeze(1), ALU.mult).then_inc(y_done, 1)

                def step(hp):
                    for n in range(PJ):
                        if n % 2:
                            dve.wait_ge(pj, hp * PJ + (n + 1))
                            for hh in range(2):
                                dst, src, scale = copy_out(n, hh)
                                dve.tensor_scalar(dst, src, scale, None, ALU.mult).then_inc(pj_d, 1)
                    for tb in range(8):
                        reduce(hp, 0, tb)
                    set_row(hp, 0)
                    for u in range(4):
                        for n in range(P2):
                            if n in after and u < 3:
                                reduce(hp, u + 1, after[n])
                            if n == 4:
                                finish(hp, u, 0)
                        finish(hp, u, 1)
                        if u < 3:
                            set_row(hp, u + 1)

                dve.wait_ge(ones_set, 3)
                step(0)
                with dve.Fori(1, STEPS) as hp:
                    step(hp)


def route_stage(nc, R, dram, wsplit):
    with ExitStack() as ctx:
        sb = lambda n, s, d=F32: ctx.enter_context(nc.sbuf_tensor("rt_" + n, s, d))
        sem = lambda n: nc.alloc_semaphore("rt_" + n)
        rw = sb("rw", [C, E])
        bias = sb("bias", [128, E])
        before = sb("before", [128, GRP * GRP])
        neg = sb("neg", [128, TB, E])
        score = sb("score", [128, TB, E])
        sbias = sb("sbias", [128, TB, E])
        hi, lo = sb("hi", [128, TB * GRP, 4]), sb("lo", [128, TB * GRP, 4])
        t1, t2 = sb("t1", [128, TB * GRP, 4]), sb("t2", [128, TB * GRP, 4])
        grp = sb("grp", [128, TB, GRP])
        gt, eq = sb("gt", [128, TB, GRP * GRP]), sb("eq", [128, TB, GRP * GRP])
        rank = sb("rank", [128, TB, GRP])
        keep, drop = sb("keep", [128, TB, GRP]), sb("drop", [128, TB, GRP])
        masked = sb("masked", [128, TB, E])
        left = sb("left", [128, TB, E])
        top = sb("top", [128, TB, 8])
        tot = sb("tot", [128, TB])
        parts = sb("parts", [128, TB, 4, E], BF16)
        loaded, prod, exped, step, top_step, parted, turned, out = (
            sem(n) for n in ("loaded", "prod", "exped", "step", "top", "parted", "turned", "out"))
        loads = [(rw[:], dram["L2_routerT"]), (bias[:], dram["L2_ebias"].broadcast_to([128, E])),
                 (before[:], dram["before"].broadcast_to([128, GRP * GRP]))]
        with nc.Block() as block:

            @block.sync
            def _(sp):
                for dst, src in loads:
                    sp.dma_start(dst, src).then_inc(loaded, 16)
                sp.wait_ge(loaded, 16 * len(loads))

            @block.gpsimd
            def _(pool):
                pool.memset(parts[:, :, 3, :], 0.0).then_inc(parted, 1)

            @block.tensor
            def _(pe):
                pe.wait_ge(loaded, 16 * len(loads))
                for tb in range(TB):
                    last = pe.matmul(R.ps[:, tb // 8, (tb % 8) * E:(tb % 8 + 1) * E], h_block(R, tb), rw[:],
                                     start=True, stop=True)
                last.then_inc(prod, 1)
                pe.wait_ge(parted, 6)
                for tb in range(TB):
                    for i in range(2):
                        dst = R.ps[:, 2 + tb // 4, :].bitcast(BF16)[:, ((tb % 4) * 2 + i) * 128:((tb % 4) * 2 + i + 1) * 128]
                        last = pe.transpose(dst, parts[:, tb, 2 * i:2 * i + 2, :].rearrange("p a e -> p (a e)"), R.identb[:])
                    if tb % 4 == 3:
                        last.then_inc(turned, 1)

            @block.scalar
            def _(act):
                act.wait_ge(step, 1)
                act.activation(neg[:], neg[:], ACT.Exp).then_inc(exped, 1)
                for g in range(TB // 4):
                    act.wait_ge(turned, g + 1)
                    src = R.ps[:, 2 + g, :].bitcast(BF16).rearrange("p (t i c) -> p i t c", t=4, i=2)
                    act.activation(wsplit[:, :, g * CW:(g + 1) * CW].rearrange("p i (t c) -> p i t c", t=4), src, ACT.Copy)\
                       .then_inc(out, 1)

            @block.vector
            def _(dve):
                n = 0

                def after(ins):
                    nonlocal n
                    n += 1
                    ins.then_inc(step, 1)

                def tt(out, a, b, op):
                    after(dve.tensor_tensor(out, a, b, op))

                def ts(out, a, s1, s2, op0, op1=None):
                    after(dve.tensor_scalar(out, a, s1, s2, op0, op1) if op1 else dve.tensor_scalar(out, a, s1, s2, op0))

                dve.wait_ge(loaded, 16 * len(loads))
                dve.wait_ge(prod, 1)
                logits = R.ps[:, 0:2, :].rearrange("p a (t e) -> p (a t) e", e=E)
                ts(neg[:], logits, -1.0, 87.0, ALU.mult, ALU.min)
                dve.wait_ge(exped, 1)
                ts(score[:], neg[:], 1.0, None, ALU.add)
                dve.wait_ge(step, n)
                after(dve.reciprocal(score[:], score[:]))
                dve.wait_ge(step, n)
                tt(sbias[:], score[:], bias[:].unsqueeze(1).broadcast_to([128, TB, E]), ALU.add)
                dve.wait_ge(step, n)
                v = sbias[:].rearrange("p t (g e) -> p (t g) e", g=GRP)
                tt(hi[:], v[:, :, 0:4], v[:, :, 4:8], ALU.max)
                tt(lo[:], v[:, :, 0:4], v[:, :, 4:8], ALU.min)
                dve.wait_ge(step, n)
                for wd in (2, 1):
                    a, b = slice(0, wd), slice(wd, 2 * wd)
                    tt(t1[:, :, 0:wd], hi[:, :, a], hi[:, :, b], ALU.min)
                    tt(t2[:, :, 0:wd], lo[:, :, a], lo[:, :, b], ALU.max)
                    tt(hi[:, :, a], hi[:, :, a], hi[:, :, b], ALU.max)
                    dve.wait_ge(step, n)
                    tt(lo[:, :, a], t1[:, :, 0:wd], t2[:, :, 0:wd], ALU.max)
                    dve.wait_ge(step, n)
                tt(grp[:].rearrange("p t g -> p (t g)").unsqueeze(2), hi[:, :, 0:1], lo[:, :, 0:1], ALU.add)
                dve.wait_ge(step, n)
                own = grp[:].unsqueeze(3).broadcast_to([128, TB, GRP, GRP])
                other = grp[:].unsqueeze(2).broadcast_to([128, TB, GRP, GRP])
                g4 = lambda x: x[:].rearrange("p t (a b) -> p t a b", a=GRP)
                tt(g4(gt), other, own, ALU.is_gt)
                tt(g4(eq), other, own, ALU.is_equal)
                dve.wait_ge(step, n)
                tt(eq[:], eq[:], before[:].unsqueeze(1).broadcast_to([128, TB, GRP * GRP]), ALU.mult)
                dve.wait_ge(step, n)
                tt(gt[:], gt[:], eq[:], ALU.add)
                dve.wait_ge(step, n)
                after(dve.tensor_reduce(rank[:], g4(gt), X_AXIS, ALU.add))
                dve.wait_ge(step, n)
                ts(keep[:], rank[:], 3.5, None, ALU.is_lt)
                dve.wait_ge(step, n)
                ts(drop[:], keep[:], 1e38, -1e38, ALU.mult, ALU.add)
                e4 = lambda x: x[:].rearrange("p t (g e) -> p t g e", g=GRP)
                wide = lambda x: x[:].unsqueeze(3).broadcast_to([128, TB, GRP, 8])
                tt(e4(masked), e4(sbias), wide(keep), ALU.mult)
                dve.wait_ge(step, n)
                tt(e4(masked), e4(masked), wide(drop), ALU.add)
                dve.wait_ge(step, n)
                for tb in range(TB):
                    dve.max(top[:, tb, :], masked[:, tb, :]).then_inc(top_step, 1)
                for tb in range(TB):
                    dve.wait_ge(top_step, tb + 1)
                    dve.match_replace(left[:, tb, :], top[:, tb, :], masked[:, tb, :], -2e38).then_inc(top_step, 1)
                dve.wait_ge(top_step, 2 * TB)
                tt(left[:], left[:], masked[:], ALU.is_lt)
                dve.wait_ge(step, n)
                tt(score[:], score[:], left[:], ALU.mult)
                dve.wait_ge(step, n)
                after(dve.tensor_reduce(tot[:], score[:], X_AXIS, ALU.add))
                dve.wait_ge(step, n)
                ts(tot[:], tot[:], 1e-20, None, ALU.add)
                dve.wait_ge(step, n)
                after(dve.reciprocal(tot[:], tot[:]))
                dve.wait_ge(step, n)
                tt(score[:], score[:], tot[:].unsqueeze(2).broadcast_to([128, TB, E]), ALU.mult)
                dve.wait_ge(step, n)
                for i, op in enumerate(((parts[:, :, 0, :], score[:]), (masked[:], score[:], parts[:, :, 0, :]),
                                        (parts[:, :, 1, :], masked[:]), (left[:], masked[:], parts[:, :, 1, :]),
                                        (parts[:, :, 2, :], left[:]))):
                    if len(op) == 2:
                        dve.tensor_copy(*op).then_inc(parted, 1)
                    else:
                        dve.tensor_tensor(*op, ALU.subtract).then_inc(parted, 1)
                    dve.wait_ge(parted, i + 2)


def expert_stage(nc, R, dram, wsplit):
    HS_T = 2
    with ExitStack() as ctx:
        sb = lambda n, s, d=F32: ctx.enter_context(nc.sbuf_tensor("ex_" + n, s, d))
        sem = lambda n: nc.alloc_semaphore("ex_" + n)
        wg = sb("wg", [C, 2, C])
        wu = sb("wu", [C, 2, C])
        wd = sb("wd", [C, 2, C])
        choose = sb("choose", [128, EP, C], BF16)
        s = sb("s", [C, 2, CW])
        su = sb("su", [C, 2, CW])
        hid = sb("hid", [C, 2, CW])
        const_loaded = sem("const")
        ld = [sem("ld0"), sem("ld1")]
        g_full, silu_done, u_full, su_done, w_full, hid_done, d_done, res_done = (
            sem(n) for n in ("g_full", "silu", "u_full", "su", "w_full", "hid", "d", "res"))
        G_BANK, U_BANK, W_BANK = 4, 5, 6
        TILES = HS_T + EP
        with nc.Block() as block:

            @block.sync
            def _(sp):
                def load(tile, slot):
                    sp.dma_start(wg[:, slot, :], dram["ex_gate"][bass.ds(tile * C, C), :]).then_inc(ld[slot], 16)
                    sp.dma_start(wu[:, slot, :], dram["ex_up"][bass.ds(tile * C, C), :]).then_inc(ld[slot], 16)
                    sp.dma_start(wd[:, slot, :], dram["ex_down"][bass.ds(tile * C, C), :]).then_inc(ld[slot], 16)

                load(0, 0)
                load(1, 1)
                with sp.Fori(1, TILES // 2) as kk:
                    for slot in range(2):
                        sp.wait_ge(d_done, kk * 8 + (4 * slot - 4))
                        load(kk * 2 + slot, slot)

            @block.gpsimd
            def _(pool):
                pool.dma_start(choose[:], dram["choose"]).then_inc(const_loaded, 16)

            @block.tensor
            def _(pe):
                def down(kk, i):
                    m = kk * 8 + i
                    shared_first = isinstance(kk, int) and kk == 0 and i < 4
                    pe.wait_ge(hid_done, m + 1)
                    pe.matmul(R.ps[:, i % 4, :], wd[:, (i // 4) % 2, :], hid[:, i % 2, :], start=shared_first,
                              stop=True, skip_group_check=True).then_inc(d_done, 1)

                def step(kk, first=False):
                    for i in range(8):
                        m = kk * 8 + i
                        slot, c = i // 4, i % 4
                        if c == 0:
                            pe.wait_ge(ld[slot], kk * 48 + 48)
                        if not (first and i == 0):
                            pe.wait_ge(silu_done, m)
                        pe.matmul(R.ps[:, G_BANK, :], wg[:, slot, :], h_chunk(R, c), start=True, stop=True).then_inc(g_full, 1)
                        if not (first and i == 0):
                            pe.wait_ge(su_done, m)
                        pe.matmul(R.ps[:, U_BANK, :], wu[:, slot, :], h_chunk(R, c), start=True, stop=True).then_inc(u_full, 1)
                        if not first:
                            if not (i == 0):
                                pe.wait_ge(hid_done, m)
                            else:
                                pe.wait_ge(hid_done, m)
                            pair = choose[:, bass.ds(kk * 2 + (slot - HS_T), 1), :]
                            for part in range(2):
                                last = pe.matmul(R.ps[:, W_BANK, :], pair, wsplit[:, part, c * CW:(c + 1) * CW],
                                                 start=(part == 0), stop=(part == 1))
                            last.then_inc(w_full, 1)
                        if not (first and i == 0):
                            down(kk, i - 1)

                pe.wait_ge(const_loaded, 16)
                step(0, True)
                with pe.Fori(1, TILES // 2) as kk:
                    step(kk)
                down(TILES // 2 - 1, 7)

            @block.scalar
            def _(act):
                def step(kk, first=False):
                    for i in range(8):
                        m = kk * 8 + i
                        act.wait_ge(g_full, m + 1)
                        if not (first and i < 2):
                            act.wait_ge(su_done, m - 1)
                        act.activation(s[:, i % 2, :], R.ps[:, G_BANK, :], ACT.Silu).then_inc(silu_done, 1)

                step(0, True)
                with act.Fori(1, TILES // 2) as kk:
                    step(kk)

            @block.vector
            def _(dve):
                def step(kk, first=False):
                    for i in range(8):
                        m = kk * 8 + i
                        dve.wait_ge(silu_done, m + 1)
                        dve.wait_ge(u_full, m + 1)
                        if not (first and i < 2):
                            dve.wait_ge(d_done, m - 1)
                        if first:
                            dve.tensor_tensor(hid[:, i % 2, :], s[:, i % 2, :], R.ps[:, U_BANK, :], ALU.mult)\
                               .then_inc(su_done, 1)
                            dve.wait_ge(su_done, m + 1)
                            dve.sem_inc(hid_done, 1)
                        else:
                            dve.tensor_tensor(su[:, i % 2, :], s[:, i % 2, :], R.ps[:, U_BANK, :], ALU.mult)\
                               .then_inc(su_done, 1)
                            dve.wait_ge(su_done, m + 1)
                            dve.wait_ge(w_full, m - 7)
                            dve.tensor_tensor(hid[:, i % 2, :], su[:, i % 2, :], R.ps[:, W_BANK, :], ALU.mult)\
                               .then_inc(hid_done, 1)

                step(0, True)
                with dve.Fori(1, TILES // 2) as kk:
                    step(kk)
                dve.wait_ge(d_done, TILES * 4)
                for c in range(NC):
                    b, t = chunk(c)
                    dve.scalar_tensor_tensor(R.x[:, b, t], R.ps[:, c, :], mod_cols(R, 2, 1, b)[2], R.x[:, b, t],
                                             ALU.mult, ALU.add).then_inc(res_done, 1)


def linear_stage(nc, R, dram, attn):
    with ExitStack() as ctx:
        sb = lambda n, s, d=F32: ctx.enter_context(nc.sbuf_tensor("la_" + n, s, d))
        sem = lambda n: nc.alloc_semaphore("la_" + n)
        wq = sb("wq", [C, C])
        wkv = sb("wkv", [C, 2, C])
        sc = sb("sc", [128, HEADS])
        qf = sb("qf", [C, NC, CW])
        q2 = sb("q2", [C, NC, CW])
        k = sb("k", [128, TB, C])
        v = sb("v", [128, TB, C])
        k2 = sb("k2", [128, TB, C])
        kn = sb("kn", [128, TB, HEADS])
        mask = sb("mask", [128, C])
        kv = sb("kv", [C, B, C])
        loaded, qp, q_copied, squared, norm, q_root, q_len, q_hat, kvp, v_copied, k_sq, k_sum, k_root, k_hat, outer, masked, \
            att, done, step, nc_step = (sem(n) for n in (
                "loaded", "qp", "q_copied", "squared", "norm", "q_root", "q_len", "q_hat", "kvp", "v_copied", "k_sq",
                "k_sum", "k_root", "k_hat", "outer", "masked", "att", "done", "step", "nc_step"))
        loads = [(wq[:], dram["L3_wqT"]), (wkv[:, 0, :], dram["L3_wkT"]), (wkv[:, 1, :], dram["L3_wvT"]),
                 (sc[:], dram["L3_norm"].broadcast_to([128, HEADS]))]
        with nc.Block() as block:

            @block.sync
            def _(sp):
                for dst, src in loads:
                    sp.dma_start(dst, src).then_inc(loaded, 16)
                sp.wait_ge(loaded, 16 * len(loads))

            @block.tensor
            def _(pe):
                pe.wait_ge(loaded, 16 * len(loads))
                for g in range(TB // 4):
                    if g >= 2:
                        pe.wait_ge(v_copied, g - 1)
                        pe.wait_ge(k_sq, 2 * (g - 1) - 1)
                    for a in range(2):
                        for i in range(4):
                            last = pe.matmul(R.ps[:, 2 * (g % 2) + a, i * C:(i + 1) * C], h_block(R, 4 * g + i),
                                             wkv[:, a, :], start=True, stop=True)
                    last.then_inc(kvp, 1)
                for c in range(NC):
                    pe.matmul(R.ps[:, 4 + c, :], wq[:], h_chunk(R, c), start=True, stop=True).then_inc(qp, 1)
                pe.wait_ge(v_copied, TB // 4)
                pe.wait_ge(k_sq, TB // 2)
                for c in range(NC):
                    pe.wait_ge(squared, c + 1)
                    pe.matmul(R.ps[:, c, :], R.blk8[:], q2[:, c, :], start=True, stop=True).then_inc(norm, 1)
                pe.wait_ge(q_root, NC)
                pe.wait_ge(k_hat, 1)
                for b in range(B):
                    for s in range(8):
                        last = pe.matmul(R.ps[:, 0, b * C:(b + 1) * C], k[:, 8 * b + s, :], v[:, 8 * b + s, :],
                                         start=(s == 0), stop=(s == 7))
                    last.then_inc(outer, 1)
                pe.wait_ge(q_hat, NC)
                for c in range(NC):
                    pe.wait_ge(masked, c // 2 + 1)
                    pe.matmul(R.ps[:, 4 + c, :], kv[:, c // 2, :], qf[:, c, :], start=True, stop=True).then_inc(att, 1)

            @block.scalar
            def _(act):
                act.wait_ge(loaded, 16 * len(loads))
                act.activation(sc[:], sc[:], ACT.Sigmoid).then_inc(nc_step, 1)
                act.wait_ge(nc_step, 1)
                act.activation(sc[:], sc[:], ACT.Exp, scale=-math.log(T)).then_inc(nc_step, 1)
                for g in range(TB // 4):
                    act.wait_ge(kvp, g + 1)
                    act.activation(v[:, 4 * g:4 * g + 4, :].rearrange("p t c -> p (t c)"), R.ps[:, 2 * (g % 2) + 1, :],
                                   ACT.Copy).then_inc(v_copied, 1)
                for c in range(NC):
                    act.wait_ge(qp, c + 1)
                    act.activation(q2[:, c, :], R.ps[:, 4 + c, :], ACT.Square).then_inc(squared, 1)
                act.wait_ge(k_sum, 1)
                act.activation(kn[:], kn[:], ACT.Sqrt).then_inc(k_root, 1)
                for c in range(NC):
                    act.wait_ge(norm, c + 1)
                    act.activation(q2[:, c, :], R.ps[:, c, :], ACT.Sqrt).then_inc(q_root, 1)
                for c in range(NC):
                    b, t = chunk(c)
                    act.wait_ge(att, c + 1)
                    act.activation(attn[:, b, t], R.ps[:, 4 + c, :], ACT.Copy).then_inc(done, 1)

            @block.vector
            def _(dve):
                for g in range(TB // 4):
                    dve.wait_ge(kvp, g + 1)
                    kg = k[:, 4 * g:4 * g + 4, :].rearrange("p t c -> p (t c)")
                    dve.tensor_copy(kg, R.ps[:, 2 * (g % 2), :]).then_inc(k_sq, 1)
                    dve.wait_ge(k_sq, 2 * g + 1)
                    dve.tensor_tensor(k2[:, 4 * g:4 * g + 4, :].rearrange("p t c -> p (t c)"), kg, kg, ALU.mult)\
                       .then_inc(k_sq, 1)
                dve.wait_ge(k_sq, TB // 2)
                kh = lambda x: x[:].rearrange("p t (h c) -> p t h c", c=8)
                dve.tensor_reduce(kn[:], kh(k2), X_AXIS, ALU.add).then_inc(k_sum, 1)
                dve.wait_ge(k_root, 1)
                dve.tensor_scalar(kn[:], kn[:], 1e-12, None, ALU.max).then_inc(step, 1)
                dve.wait_ge(step, 1)
                dve.reciprocal(kn[:], kn[:]).then_inc(step, 1)
                dve.wait_ge(step, 2)
                dve.tensor_tensor(kh(k), kh(k), kn[:].unsqueeze(3).broadcast_to([128, TB, HEADS, 8]), ALU.mult)\
                   .then_inc(k_hat, 1)
                dve.wait_ge(nc_step, 2)
                dve.tensor_tensor(mask[:].rearrange("p (h c) -> p h c", c=8), R.blk8[:].rearrange("p (h c) -> p h c", c=8),
                                  sc[:].unsqueeze(2).broadcast_to([128, HEADS, 8]), ALU.mult).then_inc(step, 1)
                for c in range(NC):
                    dve.wait_ge(q_root, c + 1)
                    dve.tensor_scalar(q2[:, c, :], q2[:, c, :], 1e-12, None, ALU.max).then_inc(q_len, 1)
                    dve.wait_ge(q_len, 2 * c + 1)
                    dve.reciprocal(q2[:, c, :], q2[:, c, :]).then_inc(q_len, 1)
                    dve.wait_ge(q_len, 2 * c + 2)
                    dve.tensor_tensor(qf[:, c, :], R.ps[:, 4 + c, :], q2[:, c, :], ALU.mult).then_inc(q_hat, 1)
                dve.wait_ge(step, 3)
                dve.wait_ge(outer, 2)
                for b in range(B):
                    dve.tensor_tensor(kv[:, b, :], R.ps[:, 0, b * C:(b + 1) * C], mask[:], ALU.mult).then_inc(masked, 1)


def store_stage(nc, R, out):
    stored = nc.alloc_semaphore("stored")
    with nc.Block() as block:

        @block.sync
        def _(sp):
            sp.dma_start(out, R.x[:]).then_inc(stored, 16)
            sp.wait_ge(stored, 16)


def build_program(nc, dram, out, halves=8):
    R = Residents(nc)
    setup_stage(nc, R, dram)

    def softmax_layer(name, layer, rows, dim, groups, hg, mask):
        with ExitStack() as ctx:
            A = Attn(nc, name, rows, dim, groups, hg, mask)
            A.v = ctx.enter_context(nc.sbuf_tensor(name + "v", [128, groups, 8, hg, 9], F32))
            norm_stage(nc, R, layer, 0)
            project_stage(nc, R, A, dram, layer)
            A.on = ctx.enter_context(nc.sbuf_tensor(name + "on", [128, groups, T], F32))
            softmax_stage(nc, R, A, dram)
            if layer == 0:
                diff_out_stage(nc, R, A, dram)
            else:
                out_stage(nc, R, 1, 0, "o1", lambda i, c: A.on[:, (c // 2) * 4 + i, chunk(c)[1]], 4,
                          dram["L1_woG"], dram["L1_bo"])

    def layer_0a():
        softmax_layer("a0", 0, 32, 4, 16, 2, False)

    def layer_0b():
        norm_stage(nc, R, 0, 1)
        lora_stage(nc, R, 0, dram)

    def layer_1a():
        softmax_layer("a1", 1, 64, 8, 8, 4, True)

    def layer_1b():
        norm_stage(nc, R, 1, 1)
        mix_stage(nc, R, dram)

    def layer_2a():
        with ExitStack() as ctx:
            norm_stage(nc, R, 2, 0)
            y = ctx.enter_context(nc.sbuf_tensor("y2", [128, HEADS // 2, B, T], F32))
            with ExitStack() as inner:
                lat = inner.enter_context(nc.sbuf_tensor("lat", [C, B, T], F32))
                latent_stage(nc, R, dram, lat)
                causal_stage(nc, R, dram, lat, y)
            out_stage(nc, R, 2, 0, "o2", lambda i, c: y[:, i, c // 2, chunk(c)[1]], HEADS // 2, dram["L2_wout"])

    def layer_2b():
        norm_stage(nc, R, 2, 1)
        with nc.sbuf_tensor("wsplit", [128, 2, N], BF16) as wsplit:
            route_stage(nc, R, dram, wsplit)
            expert_stage(nc, R, dram, wsplit)

    def layer_3a():
        norm_stage(nc, R, 3, 0)
        with nc.sbuf_tensor("attn3", [C, B, T], F32) as attn:
            linear_stage(nc, R, dram, attn)
            out_stage(nc, R, 3, 0, "o3", lambda i, c: attn[:, c // 2, chunk(c)[1]], 1, dram["L3_woT"])

    def layer_3b():
        norm_stage(nc, R, 3, 1)
        lora_stage(nc, R, 3, dram)

    for i, half in enumerate((layer_0a, layer_0b, layer_1a, layer_1b, layer_2a, layer_2b, layer_3a, layer_3b)):
        if i in halves:
            with nc.cleanup_on_exit():
                half()
    store_stage(nc, R, out)


def constants():
    r = np.arange(128)
    k = {"ident": np.eye(128, dtype=np.float32), "blk8": (r[:, None] // 8 == r[None, :] // 8).astype(np.float32),
         "den_sel": (r[:, None] == r[None, :] // 32 * 32 + 8).astype(np.float32),
         "parity": np.stack([(r // 32) % 2 == 0, (r // 32) % 2 == 1], 1).astype(np.float32),
         "late": np.where(r[None, :] > r[:, None], NEG, 0.0).astype(np.float32),
         "lateT": np.where(r[:, None] > r[None, :], NEG, 0.0).astype(np.float32)}
    a0 = np.zeros((128, 5), np.float32)
    a1 = np.zeros((128, 5), np.float32)
    for j in range(4):
        a0[32 * j:32 * j + 3, 1 + j] = 1
        a1[64 * (j % 2):64 * (j % 2) + 3, 1 + j] = 1
    a1[[51, 115], 0] = 1
    k["a0rowc"], k["a1rowc"] = a0, a1
    pick = np.zeros((128, 8, C), np.float32)
    for g in range(8):
        for j in range(4):
            for c in range(8):
                pick[32 * j + c, g, (2 * g + j // 2) * 8 + c] = 1
    k["pick"] = pick
    g = np.arange(GRP)
    k["before"] = (g[None, :] < g[:, None]).astype(np.float32).reshape(1, -1)
    choose = np.zeros((128, EP, C), np.float32)
    for e in range(E):
        choose[[e, 64 + e], e // 2, (e % 2) * EH:(e % 2) * EH + EH] = 1
    k["choose"] = choose
    return k


def lay_out(inputs):
    i = {k: np.asarray(v) for k, v in inputs.items()}
    d = {"xT": i["L0_attn_query"].transpose(2, 0, 1)}
    for l in range(LAYERS):
        d[f"L{l}_wmod"] = i[f"L{l}_wmod"]
        d[f"L{l}_cT"] = i[f"L{l}_c"].T
    for n in "qkv":
        d[f"L0_w{n}T"] = i[f"L0_attn_W{n}"].T
        d[f"L1_w{n}T"] = i[f"L1_attn_w{n}_w"].T
        d[f"L3_w{n}T"] = i[f"L3_attn_W{n}"].T
    for n, m in enumerate(("q1", "k1", "q2", "k2")):
        d[f"L0_lam{n}"] = i[f"L0_attn_lambda_{m}"].reshape(1, 4)
    d["subln_col"] = np.tile(i["L0_attn_subln_w"], HEADS).reshape(C, 1)
    d["L0_woT"] = i["L0_attn_Wo"].T
    for l in (0, 3):
        d[f"L{l}_fW1T"] = i[f"L{l}_ffn_W1"].T
        d[f"L{l}_fW2T"] = i[f"L{l}_ffn_W2"].T.reshape(HB, C, C).transpose(1, 0, 2)
        d[f"L{l}_fb1"] = i[f"L{l}_ffn_b1"].reshape(HB, C).T
        d[f"L{l}_fb2"] = i[f"L{l}_ffn_b2"].reshape(C, 1)
        d[f"L{l}_fscale"] = i[f"L{l}_ffn_scale"].reshape(1, 1)
    d["L1_bq"], d["L1_bk"] = i["L1_attn_wq_b"].reshape(C, 1), i["L1_attn_wk_b"].reshape(C, 1)
    d["L1_bv"], d["L1_bo"] = i["L1_attn_wv_b"].reshape(1, C), i["L1_attn_wo_b"].reshape(C, 1)
    wo = np.zeros((4, 32, 4, C), np.float32)
    wo[:, 0:8] = i["L1_attn_wo_w"].T.reshape(4, 4, 8, C).transpose(1, 2, 0, 3)
    d["L1_woG"] = wo.reshape(128, 4, C)
    for n in "rkv":
        d[f"L1_W{n}T"] = i[f"L1_ffn_W_{n}"].T
    for n in "rk":
        d[f"L1_mu{n}"] = i[f"L1_ffn_mu_{n}"].reshape(C, 1)
    d["L2_kv_down"] = i["L2_attn_w_kv_down"]
    d["L2_wq"] = i["L2_attn_w_q"]
    d["L2_wk"], d["L2_wv"] = i["L2_attn_w_kv_up"][:, :HEADS * PH], i["L2_attn_w_kv_up"][:, HEADS * PH:]
    d["L2_wout"] = i["L2_attn_w_out"].reshape(HEADS // 2, C, C).transpose(1, 0, 2)
    d["L2_routerT"] = i["L2_ffn_router_w"].T
    d["L2_ebias"] = i["L2_ffn_e_bias"].reshape(1, E)

    def tiles(shared, experts):
        shared = shared.reshape(C, 2, C).transpose(1, 0, 2)
        experts = experts.reshape(EP, 2, C, EH).transpose(0, 2, 1, 3).reshape(EP, C, C)
        return np.concatenate([shared, experts]).reshape(-1, C)

    d["ex_gate"] = tiles(i["L2_ffn_sh_gate_w"], i["L2_ffn_gate_w"])
    d["ex_up"] = tiles(i["L2_ffn_sh_up_w"], i["L2_ffn_up_w"])
    d["ex_down"] = np.concatenate([i["L2_ffn_sh_down_w"], i["L2_ffn_down_w"].reshape(-1, C)])
    d["L3_woT"] = i["L3_attn_Wo"].T.reshape(C, 1, C)
    d["L3_norm"] = i["L3_attn_norm_const"].reshape(1, HEADS)
    d.update(constants())
    return {k: np.ascontiguousarray(v) for k, v in d.items()}


def kernel(**inputs):
    import concourse.bacc as bacc
    from concourse.bass_utils import run_bass_kernel_spmd

    nc = bacc.Bacc("TRN2", target_bir_lowering=False, num_devices=1)
    arrays = {"in_" + k: v for k, v in lay_out(inputs).items()}
    dram = {k[3:]: nc.dram_tensor(k, a.shape, mybir.dt.from_np(a.dtype), kind="ExternalInput").ap()
            for k, a in arrays.items()}
    out = nc.dram_tensor("out_x", (C, B, T), F32, kind="ExternalOutput").ap()
    build_program(nc, dram, out, range(8))
    r = run_bass_kernel_spmd(nc, [arrays], core_ids=[0])
    return np.ascontiguousarray(r.results[0]["out_x"].transpose(1, 2, 0))
```

```python
import math

import numpy as np

import concourse.bass as bass
from concourse import mybir
from contextlib import ExitStack

F32 = mybir.dt.float32
BF16 = mybir.dt.bfloat16
ALU = mybir.AluOpType
ACT = mybir.ActivationFunctionType
X_AXIS = mybir.AxisListType.X

C = 128
B = 2
T = 1024
N = B * T
CW = 512
NC = N // CW
TB = N // 128
HEADS = 16
LAYERS = 4
NEG = -1e30
LN_EPS = 1e-5
LAMBDA_INIT = float(0.8 - 0.6 * np.exp(-0.3 * 12))
HID = 512
HB = HID // C
E = 64
EH = 64
EP = E // 2
GRP = 8
PH = 64
HALF = T // 2


class NormSems:

    def __init__(self, nc):
        sem = lambda n: nc.alloc_semaphore("norm_" + n)
        self.mean, self.centred, self.squared, self.var = sem("mean"), sem("centred"), sem("squared"), sem("var")
        self.dev, self.step, self.out = sem("dev"), sem("step"), sem("out")
        self.spread, self.scaled, self.warm = sem("spread"), sem("scaled"), sem("warm")
        self.calls = 0


class Residents:

    def __init__(self, nc):
        sb = lambda n, s, d=F32: nc.alloc_sbuf_tensor(n + "_res", s, d)
        self.x = sb("x", [C, B, T])
        self.h = sb("h", [C, B, T + 4])
        self.mod = sb("mod", [C, LAYERS, 6, B])
        self.scale1 = sb("scale1", [C, LAYERS, 2, B])
        self.gate = sb("gate", [C, LAYERS * 2 * B])
        self.ident = sb("ident", [128, 128])
        self.identb = sb("identb", [128, 128], BF16)
        self.ones = sb("ones", [128, 128])
        self.blk8 = sb("blk8", [128, 128])
        self.eps = sb("eps", [128, 1])
        self.ps = nc.alloc_psum_tensor("ps", [128, 8, CW], F32)
        self.norm_sems = NormSems(nc)


class Weights:

    def __init__(self, nc, ctx, name):
        self.nc, self.ctx, self.name, self.loads = nc, ctx, name, []
        self.loaded = nc.alloc_semaphore(name + "weights_loaded")

    def tile(self, name, shape):
        return self.ctx.enter_context(self.nc.sbuf_tensor(self.name + name, shape, F32))

    def add(self, name, shape, src):
        t = self.tile(name, shape)
        self.loads.append((t[:], src))
        return t

    @property
    def count(self):
        return 16 * len(self.loads)


class Attn:

    def __init__(self, nc, name, rows, dim, groups, heads_of_group, mask):
        self.name, self.rows, self.dim, self.groups = name, rows, dim, groups
        self.row_tiles = 4 * rows // 128
        self.heads_of_group, self.mask = heads_of_group, mask
        self.parts_dram = nc.dram_tensor(name + "parts", [2, 3, B * C, T], BF16, kind="Internal").ap()
        self.mask_dram = nc.dram_tensor(name + "mask", [groups, T], BF16, kind="Internal").ap() if mask else None
        self.first_part = 4 if mask else 3
        self.scale = dim ** -0.5
        self.n_scaled = 2 if mask else 1
        self.ld = [nc.alloc_semaphore(name + "ld0"), nc.alloc_semaphore(name + "ld1")]
        self.first_k = nc.alloc_semaphore(name + "first_k")
        self.n_k_loads = 12 + (4 if mask else 0)
        self.inited = nc.alloc_semaphore(name + "inited")
        self.n_inited = 7 + (2 * 128 // rows if mask else 0)



def chunk(c):
    return c // 2, slice((c % 2) * CW, (c % 2) * CW + CW)


def setup_stage(nc, R, dram):
    with ExitStack() as ctx:
        sb = lambda n, s, d=F32: ctx.enter_context(nc.sbuf_tensor(n, s, d))
        wmod = sb("wmod", [C, LAYERS, 6 * C])
        cT = sb("cT", [C, LAYERS, B])
        sil = sb("sil", [C, LAYERS, B])
        sgn = sb("sgn", [C, LAYERS, 2, B])
        mag = sb("mag", [C, LAYERS, 2, B])
        raw = sb("raw", [C, LAYERS, 2, B])
        loaded = nc.alloc_semaphore("setup_loaded")
        silu_done = nc.alloc_semaphore("silu_done")
        mod_done = nc.alloc_semaphore("mod_products_done")
        dve_step = nc.alloc_semaphore("setup_dve_step")
        ones_done = nc.alloc_semaphore("setup_ones_done")
        cast_loaded = nc.alloc_semaphore("setup_cast_loaded")
        loads = [(R.x[:], dram["xT"]), (R.ident[:], dram["ident"]), (R.blk8[:], dram["blk8"])]
        loads += [(wmod[:, l, :], dram[f"L{l}_wmod"]) for l in range(LAYERS)]
        loads += [(cT[:, l, :], dram[f"L{l}_cT"]) for l in range(LAYERS)]
        with nc.Block() as block:

            @block.sync
            def _(sp):
                for dst, src in loads:
                    sp.dma_start(dst, src).then_inc(loaded, 16)
                sp.wait_ge(loaded, 16 * len(loads))

            @block.gpsimd
            def _(pool):
                pool.memset(R.ones[:], 1.0 / C).then_inc(ones_done, 1)
                pool.memset(R.h[:, :, 0:4], 0.0).then_inc(ones_done, 1)
                pool.memset(R.eps[:], LN_EPS).then_inc(ones_done, 1)
                pool.dma_start(R.identb[:], dram["ident"]).then_inc(cast_loaded, 16)
                pool.wait_ge(cast_loaded, 16)

            @block.scalar
            def _(act):
                act.wait_ge(loaded, 16 * len(loads))
                act.activation(sil[:], cT[:], ACT.Silu).then_inc(silu_done, 1)

            @block.tensor
            def _(pe):
                pe.wait_ge(loaded, 16 * len(loads))
                pe.wait_ge(silu_done, 1)
                for l in range(LAYERS):
                    for k in range(6):
                        col = (l * 6 + k) * B
                        last = pe.matmul(R.ps[:, 0, col:col + B], wmod[:, l, k * C:(k + 1) * C], sil[:, l, :],
                                         start=True, stop=True)
                last.then_inc(mod_done, 1)

            @block.vector
            def _(dve):
                dve.wait_ge(mod_done, 1)
                dve.tensor_copy(R.mod[:], R.ps[:, 0, 0:LAYERS * 6 * B].rearrange("p (l k b) -> p l k b", l=LAYERS, k=6))\
                   .then_inc(dve_step, 1)
                dve.wait_ge(dve_step, 1)
                gates = R.mod[:, :, 2:6:3, :]
                scales = R.mod[:, :, 1:5:3, :]
                dve.tensor_scalar(sgn[:], gates, 0.0, 2.0, ALU.is_ge, ALU.mult).then_inc(dve_step, 1)
                dve.tensor_copy(raw[:], gates).then_inc(dve_step, 1)
                dve.wait_ge(dve_step, 3)
                flat = lambda x: x[:].rearrange("p l k b -> p (l k b)")
                dve.scalar_tensor_tensor(flat(mag), flat(sgn), -1.0, flat(raw), ALU.add, ALU.mult).then_inc(dve_step, 1)
                dve.wait_ge(dve_step, 4)
                dve.tensor_scalar(mag[:], mag[:], 0.25, None, ALU.max).then_inc(dve_step, 1)
                dve.wait_ge(dve_step, 5)
                dve.scalar_tensor_tensor(R.gate[:], flat(sgn), -1.0, flat(mag), ALU.add, ALU.mult).then_inc(dve_step, 1)
                dve.tensor_scalar(R.scale1[:], scales, 1.0, None, ALU.add).then_inc(dve_step, 1)


def mod_cols(R, layer, half, b):
    k = (layer * 2 + half) * B + b
    return R.mod[:, layer, 3 * half, b:b + 1], R.scale1[:, layer, half, b:b + 1], R.gate[:, k:k + 1]


def norm_stage(nc, R, layer, half, W=None, pool_program=None):
    S = R.norm_sems
    k = S.calls
    n0 = k * NC
    S.calls += 1
    with ExitStack() as ctx:
        xc = ctx.enter_context(nc.sbuf_tensor(f"ln_xc{n0}", [C, NC, CW], F32))
        sq = ctx.enter_context(nc.sbuf_tensor(f"ln_sq{n0}", [C, NC, CW], F32))
        dev = ctx.enter_context(nc.sbuf_tensor(f"ln_dev{n0}", [C, 2, CW], F32))
        with nc.Block() as block:
            if pool_program:
                block.gpsimd(pool_program)

            @block.sync
            def _(sp):
                for dst, src in W.loads if W else []:
                    sp.dma_start(dst, src).then_inc(W.loaded, 16)

            @block.tensor
            def _(pe):
                for c in range(NC):
                    b, t = chunk(c)
                    pe.matmul(R.ps[:, c, :], R.ones[:], R.x[:, b, t], start=True, stop=True).then_inc(S.mean, 1)
                for c in range(NC):
                    pe.wait_ge(S.squared, n0 + c + 1)
                    last = pe.matmul(R.ps[32 * c:32 * c + 32, 4, :], R.ones[:, 0:32], sq[:, c, :], start=True, stop=True)
                last.then_inc(S.var, 1)
                pe.wait_ge(S.step, k + 1)
                for c in range(NC):
                    pe.matmul(R.ps[:, c, :], R.ident[:, 32 * c:32 * c + 1].broadcast_to([128, 128]), dev[:, 1, :],
                              start=True, stop=True).then_inc(S.spread, 1)

            @block.scalar
            def _(act):
                act.activation(dev[0:1, 0, 0:1], R.eps[0:1], ACT.Sqrt).then_inc(S.warm, 1)
                for c in range(NC):
                    act.wait_ge(S.centred, n0 + c + 1)
                    act.activation(sq[:, c, :], xc[:, c, :], ACT.Square).then_inc(S.squared, 1)
                act.wait_ge(S.warm, k + 1)
                act.wait_ge(S.var, k + 1)
                act.activation(dev[:, 0, :], R.ps[:, 4, :], ACT.Sqrt, bias=R.eps[:]).then_inc(S.dev, 1)
                for c in range(NC):
                    b, t = chunk(c)
                    shift, scale1, _g = mod_cols(R, layer, half, b)
                    act.wait_ge(S.scaled, n0 + c + 1)
                    act.activation(R.h[:, b, 4 + t.start:4 + t.stop], xc[:, c, :], ACT.Identity, scale=scale1,
                                   bias=shift).then_inc(S.out, 1)

            @block.vector
            def _(dve):
                for c in range(NC):
                    b, t = chunk(c)
                    dve.wait_ge(S.mean, n0 + c + 1)
                    dve.tensor_tensor(xc[:, c, :], R.x[:, b, t], R.ps[:, c, :], ALU.subtract).then_inc(S.centred, 1)
                dve.wait_ge(S.dev, k + 1)
                dve.reciprocal(dev[:, 1, :], dev[:, 0, :]).then_inc(S.step, 1)
                for c in range(NC):
                    dve.wait_ge(S.spread, n0 + c + 1)
                    dve.tensor_tensor(xc[:, c, :], xc[:, c, :], R.ps[:, c, :], ALU.mult).then_inc(S.scaled, 1)


def h_chunk(R, c):
    b, t = chunk(c)
    return R.h[:, b, 4 + t.start:4 + t.stop]


def h_block(R, tb):
    b, s = tb // 8, tb % 8
    return R.h[:, b, 4 + s * 128:4 + s * 128 + 128]


def head_row(A, j):
    return (A.rows * j) % 128


def load_rows(A, idx, slot, operand, queue, loaded=None):
    D, W, QP, KP, P = A.dim, A.rows, A.first_part, A.first_part + 3 * A.dim, A.parts_dram
    for j in range(4):
        r = head_row(A, j)
        f = bass.ds(idx * (4 * D) + j * D, D)
        if operand == 0:
            t = A.q[:, slot, (W * j) // 128, :]
            loads = [(t[r + QP:r + QP + 3 * D, :], P[0, 0:1, f, :].broadcast_to([3, D, T])),
                     (t[r + KP:r + KP + 2 * D, :], P[0, 1:2, f, :].broadcast_to([2, D, T])),
                     (t[r + KP + 2 * D:r + KP + 3 * D, :], P[0, 2, f, :])]
        else:
            t = A.k[:, slot, j, :]
            loads = [(t[r + QP:r + QP + 3 * D, :], P[1, 0:3, f, :]),
                     (t[r + KP:r + KP + 2 * D, :], P[1, 0:2, f, :]),
                     (t[r + KP + 2 * D:r + KP + 3 * D, :], P[1, 0, f, :])]
            if A.mask:
                loads += [(t[r + 3:r + 4, :], A.mask_dram[bass.ds(idx, 1), :])]
        for dst, src in loads:
            queue.dma_start(dst, src).then_inc(loaded or A.ld[slot], 16)


def load_group(A, idx, slot, queue):
    load_rows(A, idx, slot, 0, queue)
    load_rows(A, idx, slot, 1, queue)


def init_operands(A):
    def program(pool):
        rows = sorted({head_row(A, j) for j in range(4)})
        steps = [(A.q[:].bitcast(F32), 0.0), (A.k[:].bitcast(F32), 0.0)]
        if A.mask:
            steps += [(A.q[r:r + 4], 1.0) for r in rows] + [(A.q[r:r + 3], 0.0) for r in rows]
        steps += [(A.k[head_row(A, j):head_row(A, j) + 3, :, j, :], 1.0) for j in range(4)]
        steps += [(A.v[:, :, :, :, 8:9], 1.0)]
        assert len(steps) == A.n_inited
        for i, (dst, value) in enumerate(steps):
            if i:
                pool.wait_ge(A.inited, i)
            pool.memset(dst, value).then_inc(A.inited, 1)

    return program


def project_stage(nc, R, W, A, layer):
    pre = f"pj{layer}"
    bias = A.mask
    with ExitStack() as ctx:
        sb = lambda n, s, d=F32: ctx.enter_context(nc.sbuf_tensor(pre + n, s, d))
        w, bqk, bv = W.w, W.bqk, W.bv
        rest = sb("rest", [C, 4, CW])
        parts = sb("parts", [C, 2, 3, B, T], BF16)
        mrow = sb("mrow", [1, B, T], BF16)
        sem = lambda n: nc.alloc_semaphore(pre + n)
        scaled, qk, part1, rested, part2, part3, vp, v_done, mask_set, mask_stored = (
            sem(n) for n in ("scaled", "qk", "part1", "rested", "part2", "part3", "vp", "v", "mask_set",
                             "mask_stored"))
        stored = [sem("stored0"), sem("stored1")]
        heads = A.heads_of_group
        TILES = 2 * NC
        n_masks = A.groups // B if bias else 0
        with nc.Block() as block:

            @block.sync
            def _(sp):
                if bias:
                    sp.wait_ge(mask_set, 1)
                    for g in range(n_masks):
                        sp.dma_start(A.mask_dram[g::A.groups // B, :].unsqueeze(0), mrow[:]).then_inc(mask_stored, 16)
                for c in range(NC):
                    b, t = chunk(c)
                    sp.wait_ge(part3, 2 * (c + 1))
                    for o in range(2):
                        sp.dma_start(A.parts_dram[o, :, b * C:(b + 1) * C, t].rearrange("s f t -> f s t"),
                                     parts[:, o, :, b, t]).then_inc(stored[b], 16)
                sp.wait_ge(A.inited, A.n_inited)
                sp.wait_ge(stored[0], 16 * 2 * NC // B)
                load_rows(A, 0, 0, 0, sp)
                sp.wait_ge(stored[1], 16 * 2 * NC // B)

            @block.gpsimd
            def _(pool):
                pool.wait_ge(A.inited, A.n_inited)
                pool.wait_ge(stored[0], 16 * 2 * NC // B)
                if bias:
                    pool.wait_ge(mask_stored, 16 * n_masks)
                load_rows(A, 0, 0, 1, pool, A.first_k)

            @block.tensor
            def _(pe):
                def values(g):
                    for i in range(4):
                        last = pe.matmul(R.ps[:, 4 + g, i * C:(i + 1) * C], h_block(R, 4 * g + i), w[:, 2, :],
                                         start=True, stop=True)
                    last.then_inc(vp, 1)

                pe.wait_ge(W.loaded, W.count)
                pe.wait_ge(scaled, A.n_scaled)
                for c in range(NC):
                    for o in range(2):
                        n = 2 * c + o
                        if n >= 4:
                            pe.wait_ge(rested, n - 3)
                        pe.matmul(R.ps[:, n % 4, :], w[:, o, :], h_chunk(R, c), start=True, stop=True).then_inc(qk, 1)
                    values(c)

            @block.scalar
            def _(act):
                pe_bias = lambda o: bqk[:, o:o + 1]
                if bias:
                    act.wait_ge(scaled, A.n_scaled)
                for n in range(TILES + 1):
                    if n < TILES:
                        b, t = chunk(n // 2)
                        act.wait_ge(qk, n + 1)
                        dst = parts[:, n % 2, 0, b, t]
                        if bias:
                            act.activation(dst, R.ps[:, n % 4, :], ACT.Identity, bias=pe_bias(n % 2)).then_inc(part1, 1)
                        else:
                            act.activation(dst, R.ps[:, n % 4, :], ACT.Copy).then_inc(part1, 1)
                    if n:
                        m = n - 1
                        b, t = chunk(m // 2)
                        act.wait_ge(rested, m + 1)
                        act.activation(parts[:, m % 2, 1, b, t], rest[:, m % 4, :], ACT.Copy).then_inc(part2, 1)
                if layer == 0:
                    lambda_programs(W)[0](act)

            @block.vector
            def _(dve):
                if bias:
                    dve.tensor_scalar(mrow[:], R.h[0:1, :, 4:4 + T], 0.0, NEG, ALU.is_equal, ALU.mult)\
                       .then_inc(mask_set, 1)
                dve.wait_ge(W.loaded, W.count)
                dve.tensor_scalar(w[:, 0, :], w[:, 0, :], A.scale, None, ALU.mult).then_inc(scaled, 1)
                if bias:
                    dve.tensor_scalar(bqk[:, 0:1], bqk[:, 0:1], A.scale, None, ALU.mult).then_inc(scaled, 1)
                    dve.wait_ge(scaled, A.n_scaled)
                for n in range(TILES + 1):
                    if n < TILES:
                        b, t = chunk(n // 2)
                        dve.wait_ge(part1, n + 1)
                        if n >= 4:
                            dve.wait_ge(part3, n - 3)
                        first = parts[:, n % 2, 0, b, t]
                        if bias:
                            dve.scalar_tensor_tensor(rest[:, n % 4, :], R.ps[:, n % 4, :], bqk[:, n % 2:n % 2 + 1], first,
                                                     ALU.add, ALU.subtract).then_inc(rested, 1)
                        else:
                            dve.tensor_tensor(rest[:, n % 4, :], R.ps[:, n % 4, :], first, ALU.subtract).then_inc(rested, 1)
                    if n:
                        m = n - 1
                        b, t = chunk(m // 2)
                        dve.wait_ge(part2, m + 1)
                        dve.tensor_tensor(parts[:, m % 2, 2, b, t], rest[:, m % 4, :], parts[:, m % 2, 1, b, t],
                                          ALU.subtract).then_inc(part3, 1)
                for g in range(TB // 4):
                    dve.wait_ge(vp, g + 1)
                    b, s = g // 2, (g % 2) * 4
                    for i in range(4):
                        src = R.ps[:, 4 + g, i * C:(i + 1) * C].rearrange("p (g h c) -> p g h c", h=heads, c=8)
                        dst = A.v[:, b * (A.groups // B):(b + 1) * (A.groups // B), s + i, :, 0:8]
                        if bias:
                            dve.tensor_tensor(dst, src, bv[:].rearrange("p (g h c) -> p g h c", h=heads, c=8),
                                              ALU.add).then_inc(v_done, 1)
                        else:
                            dve.tensor_copy(dst, src).then_inc(v_done, 1)
                if layer == 0:
                    lambda_programs(W)[1](dve)



def softmax_stage(nc, R, W, A):
    pre, RT, ROWS, D, NG = A.name, A.row_tiles, A.rows, A.dim, A.groups
    HG = A.heads_of_group
    UNITS = 2 * NG
    with ExitStack() as ctx:
        sb = lambda n, s, d=F32: ctx.enter_context(nc.sbuf_tensor(pre + n, s, d))
        sem = lambda n: nc.alloc_semaphore(pre + n)
        q, k, ld = A.q, A.k, A.ld
        qm = sb("qm", [128, 2, RT, CW], BF16)
        vst = sb("vst", [128, 2, 8, HG, 32])
        p = sb("p", [128, 2, 4, CW])
        o = sb("o", [128, 2, CW])
        rec = sb("rec", [128, CW])
        nm = sb("nm", [128, 2, 4, 4])
        m1 = sb("m1", [128, 4, 4])
        m2 = sb("m2", [128, 4, 4])
        mt = sb("mt", [128, 4, 4, ROWS], BF16)
        zero = sb("zero", [128, 8, 9])
        den_sel, den_spread = W.den_sel, W.den_spread
        p1_full, p1_free = sem("p1_full"), sem("p1_free")
        mt_ready, mt_turned, qm_ready = sem("mt_ready"), sem("mt_turned"), sem("qm_ready")
        p2_full, exp_done, pv_done, pv_out = sem("p2_full"), sem("exp_done"), sem("pv_done"), sem("pv_out")
        den_ready, rec_done, rec_spread, on_done = sem("den_ready"), sem("rec_done"), sem("rec_spread"), sem("on_done")
        v_ready, pool_step = sem("v_ready"), sem("pool_step")
        MISC = 7
        misc_b = R.ps[:, MISC, :].bitcast(BF16).rearrange("p (r t) -> p r t", r=2)[:, 0:RT, :]
        n_loads = 4 * (6 + (1 if A.mask else 0))

        with nc.Block() as block:

            @block.sync
            def _(sp):
                load_group(A, 1, 1, sp)
                with sp.Fori(1, NG // 2) as kk:
                    sp.wait_ge(exp_done, kk * 128 - 64)
                    load_group(A, kk * 2, 0, sp)
                    sp.wait_ge(exp_done, kk * 128)
                    load_group(A, kk * 2 + 1, 1, sp)

            @block.gpsimd
            def _(pool):
                pool.memset(vst[:], 0.0).then_inc(pool_step, 1)
                pool.memset(mt[:], 0.0).then_inc(pool_step, 1)
                pool.memset(zero[:], 0.0).then_inc(pool_step, 1)
                pool.wait_ge(pool_step, 3)

                def stage_v(idx, slot):
                    pool.tensor_tensor(vst[:, slot, :, :, 16 * slot:16 * slot + 9], A.v[:, bass.ds(idx, 1)].squeeze(1),
                                       zero[:].unsqueeze(2).broadcast_to([128, 8, HG, 9]), ALU.add).then_inc(v_ready, 1)

                def split(kk, w):
                    u = kk * 4 + w
                    pool.wait_ge(p1_free, u * 16 + 16)
                    if not (isinstance(u, int) and u == 0):
                        pool.wait_ge(mt_turned, u)
                    m = nm[:, w % 2]
                    ops = ((mt[:, :, :, 0], m), (m1[:], m, mt[:, :, :, 0]), (mt[:, :, :, 1], m1[:]),
                           (m2[:], m1[:], mt[:, :, :, 1]), (mt[:, :, :, 2], m2[:]))
                    for i, op in enumerate(ops):
                        if len(op) == 2:
                            ins = pool.tensor_tensor(*op, zero[:, 0:4, 0:4], ALU.add)
                        else:
                            ins = pool.tensor_tensor(*op, ALU.subtract)
                        if i == 4:
                            ins.then_inc(mt_ready, 1)
                        else:
                            ins.then_inc(pool_step, 1)
                            pool.wait_ge(pool_step, u * 4 + (4 + i))

                stage_v(0, 0)
                split(0, 0)

                def body(kk, last):
                    for w in range(4):
                        if w % 2 and not (last and w == 3):
                            e = (w + 1) // 2
                            idx = kk * 2 + e
                            if not (isinstance(kk, int) and kk == 0 and e == 1):
                                pool.wait_ge(pv_done, (idx - 1) * 16)
                            stage_v(idx, e % 2)
                        if not (last and w == 3):
                            split(kk, w + 1)

                if NG > 2:
                    body(0, False)
                if NG // 2 > 2:
                    with pool.Fori(1, NG // 2 - 1) as kk:
                        body(kk, False)
                body(NG // 2 - 1, True)

            @block.tensor
            def _(pe):
                def p1_slot(kk, w, i):
                    tb, j = i // 4, i % 4
                    u, g_slot = kk * 4 + w, (w // 2) % 2
                    if i == 0 and w % 2 == 0:
                        not_counted = 0 if g_slot else 16 * A.n_k_loads
                        pe.wait_ge(ld[g_slot], kk * (16 * n_loads) + ((w // 4 + 1) * 16 * n_loads - not_counted))
                    if not (isinstance(u, int) and u == 0 and i < 2):
                        pe.wait_ge(p1_free, u * 16 + (i - 1))
                    t0 = (w % 2) * CW + tb * 128
                    for hf in range(2):
                        last = pe.matmul(R.ps[:, 2 * (i % 2) + hf, :], q[:, g_slot, (ROWS * j) // 128, t0:t0 + 128],
                                         k[:, g_slot, j, hf * CW:(hf + 1) * CW], start=True, stop=True)
                    last.then_inc(p1_full, 1)

                def turn(kk, w):
                    u = kk * 4 + w
                    pe.wait_ge(mt_ready, u + 1)
                    if w in (1, 2) and not (isinstance(kk, int) and kk == 0):
                        pe.wait_ge(on_done, kk * 2 + (w - 2))
                    for tb in range(4):
                        for r in range(RT):
                            last = pe.transpose(misc_b[:, r, tb * 128:(tb + 1) * 128],
                                                mt[:].rearrange("p b h w -> p b (h w)")[:, tb, r * 128:(r + 1) * 128],
                                                R.identb[:])
                    last.then_inc(mt_turned, 1)

                def score(kk, w, s, j):
                    u = kk * 4 + w
                    if not (isinstance(u, int) and u == 0 and s == 0 and j < 2):
                        pe.wait_ge(exp_done, u * 32 + (4 * s + j - 1))
                    pe.matmul(R.ps[:, 4 + j % 2, :], k[:, (w // 2) % 2, j, s * 128:(s + 1) * 128],
                              qm[:, w % 2, (ROWS * j) // 128, :], start=True, stop=True).then_inc(p2_full, 1)

                def pv(kk, w, s):
                    u = kk * 4 + w
                    if s == 0:
                        if not (isinstance(u, int) and u == 0):
                            pe.wait_ge(pv_out, u)
                        if w % 2 == 0:
                            pe.wait_ge(v_ready, kk * 2 + (w // 2 + 1))
                    pe.wait_ge(exp_done, u * 32 + (4 * s + 4))
                    for j in range(4):
                        last = pe.matmul(R.ps[32 * j:32 * j + 32, 6, :], vst[:, (w // 2) % 2, s, j * HG // 4, :],
                                         p[:, s % 2, j, :], start=(s == 0), stop=(s == 7))
                    last.then_inc(pv_done, 1)

                def den(kk):
                    pe.wait_ge(pv_out, kk * 4)
                    for w in range(2):
                        last = pe.matmul(R.ps[64 * w:64 * w + 64, MISC, :], den_sel[:], o[:, w, :], start=True, stop=True)
                    last.then_inc(den_ready, 1)

                def spread(kk, w):
                    pe.wait_ge(rec_done, kk * 4)
                    pe.matmul(R.ps[:, MISC, :], den_spread[:, w, :], rec[:], start=True, stop=True).then_inc(rec_spread, 1)

                def body(kk, last, first=False):
                    for w in range(4):
                        pe.wait_ge(qm_ready, kk * 4 + (w + 1))
                        for s in range(8):
                            def ahead(i):
                                n = 4 + 2 * s + i
                                wv = w + 1 + n // 16
                                if not (last and wv > 3):
                                    p1_slot(kk, wv, n % 16)
                            score(kk, w, s, 0)
                            score(kk, w, s, 1)
                            ahead(0)
                            ahead(1)
                            score(kk, w, s, 2)
                            score(kk, w, s, 3)
                            if s > 0:
                                pv(kk, w, s - 1)
                            elif not (first and w == 0):
                                pv(kk, w - 1, 7)
                            if s == 1 and w == 0 and not first:
                                den(kk)
                            if w < 2 and s == (4 if w == 0 else 2) and not first:
                                spread(kk, w)
                            if s == 6 and not (last and w == 3):
                                turn(kk, w + 1)
                    if last:
                        pv(kk, 3, 7)
                        den(kk + 1)
                        for w in range(2):
                            if w:
                                pe.wait_ge(on_done, kk * 2 + w)
                            spread(kk + 1, w)

                pe.wait_ge(W.loaded, W.count)
                pe.wait_ge(A.first_k, 16 * A.n_k_loads)
                for i in range(16):
                    p1_slot(0, 0, i)
                turn(0, 0)
                for i in range(4):
                    p1_slot(0, 1, i)
                if NG > 2:
                    body(0, False, True)
                if NG // 2 > 2:
                    with pe.Fori(1, NG // 2 - 1) as kk:
                        body(kk, False)
                body(NG // 2 - 1, True)

            @block.scalar
            def _(act):
                def body(kk, first=False):
                    for w in range(4):
                        u = kk * 4 + w
                        for s in range(8):
                            if not (first and w == 0 and s < 2):
                                act.wait_ge(pv_done, u * 8 + (s - 1))
                            for j in range(4):
                                act.wait_ge(p2_full, u * 32 + (4 * s + j + 1))
                                act.activation(p[:, s % 2, j, :], R.ps[:, 4 + j % 2, :], ACT.Exp).then_inc(exp_done, 1)
                                if s == 1 and j == 1 and w in (1, 2):
                                    take(kk, w - 1, first)

                def take(kk, w, first):
                    act.wait_ge(pv_done, kk * 32 + (w * 8 + 8))
                    if not first:
                        act.wait_ge(on_done, kk * 2 + (w - 1))
                    act.activation(o[:, w, :], R.ps[:, 6, :], ACT.Copy).then_inc(pv_out, 1)

                body(0, first=True)
                with act.Fori(1, NG // 2) as kk:
                    body(kk)

            @block.vector
            def _(dve):
                def reduce(kk, w, i):
                    u = kk * 4 + w
                    dve.wait_ge(p1_full, u * 16 + (i + 1))
                    dve.tensor_reduce(nm[:, w % 2, i // 4, i % 4:i % 4 + 1], R.ps[:, 2 * (i % 2):2 * (i % 2) + 2, :],
                                      mybir.AxisListType.XY, ALU.max, negate=True).then_inc(p1_free, 1)

                def merge(kk, w):
                    u = kk * 4 + w
                    dve.wait_ge(mt_turned, u + 1)
                    if not (isinstance(u, int) and u < 2):
                        dve.wait_ge(exp_done, u * 32 - 32)
                    t0 = (w % 2) * CW
                    dve.tensor_tensor(qm[:, w % 2], q[:, (w // 2) % 2, :, t0:t0 + CW], misc_b, ALU.add)\
                       .then_inc(qm_ready, 1)

                def take(kk, w):
                    dve.wait_ge(pv_done, kk * 32 + (w * 8 + 8))
                    dve.wait_ge(pv_out, kk * 4 + (w - 1))
                    dve.tensor_tensor(o[:, w - 2, :], o[:, w - 2, :], R.ps[:, 6, :], ALU.add).then_inc(pv_out, 1)

                def invert(kk, part):
                    dve.wait_ge(den_ready, kk)
                    cols = slice(part * 128, part * 128 + 128)
                    dve.reciprocal(rec[:, cols], R.ps[:, MISC, cols]).then_inc(rec_done, 1)

                def divide(kk, w):
                    dve.wait_ge(rec_spread, (kk - 1) * 2 + (w + 1))
                    t0 = w * CW
                    dve.tensor_tensor(A.on[:, bass.ds(kk - 1, 1), t0:t0 + CW], o[:, w, :].unsqueeze(1),
                                      R.ps[:, MISC, :].unsqueeze(1), ALU.mult).then_inc(on_done, 1)

                def body(kk, last, first=False):
                    for w in range(4):
                        for s in range(8):
                            for i in range(2):
                                if w == 0 and s in (2, 3) and not first:
                                    invert(kk, 2 * (s - 2) + i)
                                n = 4 + 2 * s + i
                                wv = w + 1 + n // 16
                                if not (last and wv > 3):
                                    reduce(kk, wv, n % 16)
                                if s == 7 and i == 0 and not (last and w == 3):
                                    merge(kk, w + 1)
                                if s == 1 and i == 0 and w == 0 and not first:
                                    take(kk - 1, 3)
                                if s == 1 and i == 0 and w == 3:
                                    take(kk, 2)
                            if w < 2 and s == (4 if w == 0 else 2) and not first:
                                divide(kk, w)
                    if last:
                        take(kk, 3)
                        for part in range(4):
                            invert(kk + 1, part)
                        for w in range(2):
                            divide(kk + 1, w)

                for i in range(16):
                    reduce(0, 0, i)
                merge(0, 0)
                for i in range(4):
                    reduce(0, 1, i)
                if NG > 2:
                    body(0, False, True)
                if NG // 2 > 2:
                    with dve.Fori(1, NG // 2 - 1) as kk:
                        body(kk, False)
                body(NG // 2 - 1, True)


def lambda_programs(W):
    lam, cols, prod, dots, pick, step, exped = W.lam, W.cols, W.prod, W.dots, W.pick, W.lam_step, W.exped

    def on_act(act):
        act.wait_ge(step, 2)
        act.activation(dots[:], dots[:], ACT.Exp).then_inc(exped, 1)

    def on_dve(dve):
        dve.tensor_tensor(prod[:], lam[:, 0:3:2, :], lam[:, 1:4:2, :], ALU.mult).then_inc(step, 1)
        dve.wait_ge(step, 1)
        dve.tensor_reduce(dots[:], prod[:], X_AXIS, ALU.add).then_inc(step, 1)
        dve.wait_ge(exped, 1)
        dve.tensor_tensor(cols[:, 3:4], dots[:, 1:2], dots[:, 0:1], ALU.subtract).then_inc(step, 1)
        dve.wait_ge(step, 3)
        dve.tensor_scalar(cols[:, 4:5], cols[:, 3:4], LAMBDA_INIT, None, ALU.subtract).then_inc(step, 1)
        dve.wait_ge(step, 4)
        dve.tensor_tensor(cols[:, 5:6], cols[:, 4:5], cols[:, 1:2], ALU.mult).then_inc(step, 1)
        dve.wait_ge(step, 5)
        dve.tensor_tensor(cols[:, 6:7], cols[:, 5:6], cols[:, 0:1], ALU.add).then_inc(step, 1)
        dve.tensor_scalar(cols[:, 7:8], cols[:, 2:3], 1.0 - LAMBDA_INIT, None, ALU.mult).then_inc(step, 1)
        dve.wait_ge(step, 7)
        dve.tensor_scalar(pick[:], pick[:], cols[:, 6:7], None, ALU.mult).then_inc(step, 1)

    return on_act, on_dve


def diff_out_stage(nc, R, W, A):
    PAIRS = A.groups // 2 // B
    with ExitStack() as ctx:
        sb = lambda n, s, d=F32: ctx.enter_context(nc.sbuf_tensor("do_" + n, s, d))
        sem = lambda n: nc.alloc_semaphore("do_" + n)
        cols, pick, wo = W.cols, W.pick, W.wo
        a = sb("a", [C, NC, CW])
        sq = sb("sq", [C, NC, CW])
        dev = sb("dev", [128, 2, CW])
        got, copied, squared, ms, deviated, inverted, spread, normed, proj, done = (
            sem(n) for n in ("got", "copied", "squared", "ms", "dev", "inverted", "spread", "normed", "proj", "done"))
        with nc.Block() as block:

            @block.tensor
            def _(pe):
                for c in range(NC):
                    b, t = chunk(c)
                    for g in range(PAIRS):
                        last = pe.matmul(R.ps[:, c, :], pick[:, g, :], A.on[:, b * PAIRS + g, t], start=(g == 0),
                                         stop=(g == PAIRS - 1))
                    last.then_inc(got, 1)
                for c in range(NC):
                    pe.wait_ge(squared, c + 1)
                    last = pe.matmul(R.ps[32 * c:32 * c + 32, 4, :], W.head_sum[:], sq[:, c, :], start=True, stop=True)
                last.then_inc(ms, 1)
                pe.wait_ge(inverted, 1)
                pe.wait_ge(copied, NC)
                for c in range(NC):
                    pe.matmul(R.ps[:, c, :], W.head_spread[:, c, :], dev[:, 1, :], start=True, stop=True).then_inc(spread, 1)
                for c in range(NC):
                    pe.wait_ge(normed, c + 1)
                    pe.matmul(R.ps[:, 4 + c, :], wo[:], a[:, c, :], start=True, stop=True).then_inc(proj, 1)

            @block.scalar
            def _(act):
                for c in range(NC):
                    act.wait_ge(got, c + 1)
                    act.activation(sq[:, c, :], R.ps[:, c, :], ACT.Square, scale=8 ** -0.5).then_inc(squared, 1)
                act.wait_ge(ms, 1)
                act.activation(dev[:, 0, :], R.ps[:, 4, :], ACT.Sqrt, bias=R.eps[:]).then_inc(deviated, 1)

            @block.vector
            def _(dve):
                for c in range(NC):
                    dve.wait_ge(squared, c + 1)
                    dve.tensor_scalar(a[:, c, :], R.ps[:, c, :], cols[:, 7:8], None, ALU.mult).then_inc(copied, 1)
                dve.wait_ge(deviated, 1)
                dve.reciprocal(dev[:, 1, :], dev[:, 0, :]).then_inc(inverted, 1)
                for c in range(NC):
                    dve.wait_ge(copied, c + 1)
                    dve.wait_ge(spread, c + 1)
                    dve.tensor_tensor(a[:, c, :], a[:, c, :], R.ps[:, c, :], ALU.mult).then_inc(normed, 1)
                for c in range(NC):
                    b, t = chunk(c)
                    dve.wait_ge(proj, c + 1)
                    dve.scalar_tensor_tensor(R.x[:, b, t], R.ps[:, 4 + c, :], mod_cols(R, 0, 0, b)[2], R.x[:, b, t],
                                             ALU.mult, ALU.add).then_inc(done, 1)


def out_stage(nc, R, W, layer, half, name, rhs, parts, w, bias=None):
    with ExitStack() as ctx:
        tmp = ctx.enter_context(nc.sbuf_tensor(name + "tmp", [C, NC, CW], F32))
        proj, biased, done = (nc.alloc_semaphore(name + n) for n in ("proj", "biased", "done"))
        with nc.Block() as block:

            @block.tensor
            def _(pe):
                pe.wait_ge(W.loaded, W.count)
                for c in range(NC):
                    for i in range(parts):
                        last = pe.matmul(R.ps[:, c, :], w[:, i, :], rhs(i, c), start=(i == 0), stop=(i == parts - 1))
                    last.then_inc(proj, 1)

            @block.vector
            def _(dve):
                dve.wait_ge(W.loaded, W.count)
                for c in range(NC):
                    b, t = chunk(c)
                    gate = mod_cols(R, layer, half, b)[2]
                    dve.wait_ge(proj, c + 1)
                    src = R.ps[:, c, :]
                    if bias is not None:
                        dve.tensor_scalar(tmp[:, c, :], src, bias[:], None, ALU.add).then_inc(biased, 1)
                        dve.wait_ge(biased, c + 1)
                        src = tmp[:, c, :]
                    dve.scalar_tensor_tensor(R.x[:, b, t], src, gate, R.x[:, b, t], ALU.mult, ALU.add).then_inc(done, 1)


def lora_stage(nc, R, W, layer):
    pre = f"ff{layer}"
    with ExitStack() as ctx:
        sb = lambda n, s, d=F32: ctx.enter_context(nc.sbuf_tensor(pre + n, s, d))
        sem = lambda n: nc.alloc_semaphore(pre + n)
        w1, w2, b1, b2, scale, eye8 = W.w1, W.w2, W.b1, W.b2, W.scale, W.eye8
        w1e = sb("w1e", [C, B, HID])
        w2e = sb("w2e", [C, B, HB, C])
        even = sb("even", [8, B, C])
        odd = sb("odd", [8, B, C])
        bd = sb("bd", [8, B, 8, C])
        hid = sb("hid", [C, 2, HB, CW])
        tmp = sb("tmp", [C, NC, CW])
        turned, copied, spread, outer, eff, up, act_done, down, biased, done = (
            sem(n) for n in ("turned", "copied", "spread", "outer", "eff", "up", "act", "down", "biased", "done"))
        with nc.Block() as block:

            @block.tensor
            def _(pe):
                for b in range(B):
                    for i in range(2):
                        lt = R.h[:, b, 5 + i:5 + i + 15:2]
                        last = pe.transpose(R.ps[0:8, b, i * C:(i + 1) * C], lt, R.ident[:])
                last.then_inc(turned, 1)
                for b in range(B):
                    pe.wait_ge(spread, b + 1)
                    pe.matmul(R.ps[:, 2 + 2 * b, :], odd[:, b, :], bd[:, b, 0:4, :], start=True, stop=True).then_inc(outer, 1)
                    for r in range(HB):
                        last = pe.matmul(R.ps[:, 3 + 2 * b, r * C:(r + 1) * C], odd[:, b, :],
                                         bd[:, b, 4:8, :].rearrange("p i (c r) -> p r i c", r=4)[:, r], start=True, stop=True)
                    last.then_inc(outer, 1)

                def ups(c):
                    for hb in range(HB):
                        n = c * HB + hb
                        if n >= 4:
                            pe.wait_ge(act_done, n - 3)
                        pe.matmul(R.ps[:, hb, :], w1e[:, c // 2, hb * C:(hb + 1) * C], h_chunk(R, c),
                                  start=True, stop=True).then_inc(up, 1)

                def downs(c):
                    pe.wait_ge(act_done, (c + 1) * HB)
                    for hb in range(HB):
                        last = pe.matmul(R.ps[:, 4 + c, :], w2e[:, c // 2, hb, :], hid[:, c % 2, hb, :],
                                         start=(hb == 0), stop=(hb == HB - 1))
                    last.then_inc(down, 1)

                pe.wait_ge(eff, 2 * B)
                for c in range(NC):
                    ups(c)
                    if c:
                        downs(c - 1)
                downs(NC - 1)

            @block.scalar
            def _(act):
                act.wait_ge(W.loaded, W.count)
                for c in range(NC):
                    for hb in range(HB):
                        act.wait_ge(up, c * HB + hb + 1)
                        if c >= 2:
                            act.wait_ge(down, c - 1)
                        act.activation(hid[:, c % 2, hb, :], R.ps[:, hb, :], ACT.Gelu, bias=b1[:, hb:hb + 1])\
                           .then_inc(act_done, 1)

            @block.vector
            def _(dve):
                dve.wait_ge(W.loaded, W.count)
                dve.wait_ge(turned, 1)
                dve.tensor_copy(even[:], R.ps[0:8, 0:B, 0:C]).then_inc(copied, 1)
                dve.tensor_copy(odd[:], R.ps[0:8, 0:B, C:2 * C]).then_inc(copied, 1)
                dve.wait_ge(copied, 2)
                for b in range(B):
                    dve.tensor_tensor(bd[:, b], even[:, b, :].unsqueeze(1).broadcast_to([8, 8, C]),
                                      eye8[:].unsqueeze(2).broadcast_to([8, 8, C]), ALU.mult).then_inc(spread, 1)
                for b in range(B):
                    for i, (w, we) in enumerate(((w1[:], w1e[:, b]), (w2[:], w2e[:, b]))):
                        dve.wait_ge(outer, 2 * b + i + 1)
                        if i:
                            w, we = w.rearrange("p r o -> p (r o)"), we.rearrange("p r o -> p (r o)")
                        dve.scalar_tensor_tensor(we, R.ps[:, 2 + 2 * b + i, :], scale[:], w, ALU.mult, ALU.add)\
                           .then_inc(eff, 1)
                for c in range(NC):
                    b, t = chunk(c)
                    dve.wait_ge(down, c + 1)
                    dve.tensor_scalar(tmp[:, c, :], R.ps[:, 4 + c, :], b2[:], None, ALU.add).then_inc(biased, 1)
                    dve.wait_ge(biased, c + 1)
                    dve.scalar_tensor_tensor(R.x[:, b, t], tmp[:, c, :], mod_cols(R, layer, 1, b)[2], R.x[:, b, t],
                                             ALU.mult, ALU.add).then_inc(done, 1)


def mix_stage(nc, R, W):
    with ExitStack() as ctx:
        sb = lambda n, s, d=F32: ctx.enter_context(nc.sbuf_tensor("mx_" + n, s, d))
        sem = lambda n: nc.alloc_semaphore("mx_" + n)
        w, mu = W.w, W.mu
        own = sb("own", [C, 2, NC, CW])
        mixed = sb("mixed", [C, 2, NC, CW])
        r = sb("r", [C, NC, CW])
        k = sb("k", [C, NC, CW])
        k2 = sb("k2", [C, NC, CW])
        inv, part, mix, prod, sig, relu, sqd, vprod, step, done = (
            sem(n) for n in ("inv", "part", "mix", "prod", "sig", "relu", "sqd", "vprod", "step", "done"))
        with nc.Block() as block:

            @block.tensor
            def _(pe):
                pe.wait_ge(W.loaded, W.count)
                for c in range(NC):
                    for i in range(2):
                        pe.wait_ge(mix, 2 * c + i + 1)
                        pe.matmul(R.ps[:, 2 * (c % 2) + i, :], w[:, i, :], mixed[:, i, c, :], start=True, stop=True)\
                          .then_inc(prod, 1)
                    if c == 1:
                        pe.wait_ge(sig, 2)
                        pe.wait_ge(relu, 2)
                for c in range(NC):
                    pe.wait_ge(sqd, c + 1)
                    pe.matmul(R.ps[:, 4 + c, :], w[:, 2, :], k2[:, c, :], start=True, stop=True).then_inc(vprod, 1)

            @block.scalar
            def _(act):
                for c in range(NC):
                    act.wait_ge(prod, 2 * c + 1)
                    act.activation(r[:, c, :], R.ps[:, 2 * (c % 2), :], ACT.Sigmoid).then_inc(sig, 1)
                    act.wait_ge(prod, 2 * c + 2)
                    act.activation(k[:, c, :], R.ps[:, 2 * (c % 2) + 1, :], ACT.Relu).then_inc(relu, 1)

            @block.vector
            def _(dve):
                dve.wait_ge(W.loaded, W.count)
                dve.tensor_scalar(mu[:, 2:4], mu[:, 0:2], -1.0, 1.0, ALU.mult, ALU.add).then_inc(inv, 1)
                dve.wait_ge(inv, 1)
                for c in range(NC):
                    b, t = chunk(c)
                    before = R.h[:, b, 3 + t.start:3 + t.stop]
                    for i in range(2):
                        dve.tensor_scalar(own[:, i, c, :], h_chunk(R, c), mu[:, i:i + 1], None, ALU.mult).then_inc(part, 1)
                        dve.wait_ge(part, 2 * c + i + 1)
                        dve.scalar_tensor_tensor(mixed[:, i, c, :], before, mu[:, 2 + i:3 + i], own[:, i, c, :],
                                                 ALU.mult, ALU.add).then_inc(mix, 1)
                for c in range(NC):
                    dve.wait_ge(relu, c + 1)
                    dve.tensor_tensor(k2[:, c, :], k[:, c, :], k[:, c, :], ALU.mult).then_inc(sqd, 1)
                for c in range(NC):
                    b, t = chunk(c)
                    dve.wait_ge(vprod, c + 1)
                    dve.wait_ge(sqd, c + 1)
                    dve.scalar_tensor_tensor(k[:, c, :], R.ps[:, 4 + c, :], mod_cols(R, 1, 1, b)[2], r[:, c, :],
                                             ALU.mult, ALU.mult).then_inc(step, 1)
                    dve.wait_ge(step, c + 1)
                    dve.tensor_tensor(R.x[:, b, t], R.x[:, b, t], k[:, c, :], ALU.add).then_inc(done, 1)


def latent_stage(nc, R, W, lat):
    with ExitStack() as ctx:
        w = W.down
        prod, done = (nc.alloc_semaphore("lt_" + n) for n in ("prod", "done"))
        with nc.Block() as block:

            @block.tensor
            def _(pe):
                pe.wait_ge(W.loaded, W.count)
                for c in range(NC):
                    pe.matmul(R.ps[:, c, :], w[:], h_chunk(R, c), start=True, stop=True).then_inc(prod, 1)

            @block.scalar
            def _(act):
                for c in range(NC):
                    b, t = chunk(c)
                    act.wait_ge(prod, c + 1)
                    act.activation(lat[:, b, t], R.ps[:, c, :], ACT.Copy).then_inc(done, 1)


def causal_stage(nc, R, dram, lat, y):
    pre = "ca"
    KR = 96
    with ExitStack() as ctx:
        sb = lambda n, s, d=F32: ctx.enter_context(nc.sbuf_tensor(pre + n, s, d))
        sem = lambda n: nc.alloc_semaphore(pre + n)
        w = sb("w", [C, 3, C])
        q = sb("q", [KR, 2, B, T])
        k = sb("k", [KR, 2, B, T])
        v = sb("v", [128, B, 8, C])
        p = sb("p", [128, 2, 2, T])
        pT = sb("pT", [128, 2, 2, 8, 128])
        nm = sb("nm", [128, 4])
        rs = sb("rs", [128, B, 8, 2])
        rinv = sb("rinv", [128, B, 8, 2])
        rrow = sb("rrow", [128, 2, CW])
        late = sb("late", [128, 128], BF16)
        const_loaded, w_loaded, zeroed = sem("const"), sem("w_loaded"), sem("zeroed")
        pj, pj_a, pj_d = sem("pj"), sem("pj_a"), sem("pj_d")
        s_full, max_done, exp_done = sem("s_full"), sem("max_done"), sem("exp_done")
        t_full, t_a, t_d = sem("t_full"), sem("t_a"), sem("t_d")
        pv_done, inv_done, y_done = sem("pv_done"), sem("inv_done"), sem("y_done")
        STEPS = HEADS // 2
        PJ = 10
        items = [(b, tb) for b in range(B) for tb in (0, 7, 1, 6, 2, 5, 3, 4)]
        I = len(items)
        groups, of_item = [], {}

        def events():
            yield "score", 0, 0
            yield "score", 0, 1
            for i in range(I + 1):
                for hh in range(2):
                    if i + 1 < I:
                        yield "score", i + 1, hh
                    if i < I:
                        for g in range(items[i][1] // 4 + 1):
                            yield "turn", i, (hh, g)
                if i:
                    yield "product", i - 1, None
                    if i % 8 == 0:
                        for th in range(2):
                            yield "spread", items[i - 1][0], th

        order = list(events())
        for kind, i, x in order:
            if kind in ("turn", "spread"):
                of_item[kind, i, x] = len(groups)
                groups.append((kind, i, x))
        NG = len(groups)
        assert NG % 2 == 0

        def turned_of(i):
            return of_item["turn", i, (1, items[i][1] // 4)] + 1

        with nc.Block() as block:

            @block.sync
            def _(sp):
                def load(hp):
                    for i, n in enumerate(("q", "k", "v")):
                        sp.dma_start(w[:, i, :], dram[f"L2_w{n}"][:, bass.ds(hp * C, C)]).then_inc(w_loaded, 16)

                load(0)
                with sp.Fori(1, STEPS) as hp:
                    sp.wait_ge(pj, hp * PJ)
                    load(hp)

            @block.gpsimd
            def _(pool):
                pool.dma_start(late[:], dram["late"]).then_inc(const_loaded, 16)
                pool.memset(q[PH:KR], 0.0).then_inc(zeroed, 1)
                pool.memset(k[PH:KR], 0.0).then_inc(zeroed, 1)

            @block.tensor
            def _(pe):
                def project(hp):
                    pe.wait_ge(w_loaded, hp * 48 + 48)
                    for n in range(PJ):
                        if 4 <= n < 8:
                            pe.wait_ge(pj_d if n % 2 else pj_a, hp * PJ + (n // 2 * 2 - 2))
                        if n < 8:
                            b, t = chunk(n % 4)
                            pe.matmul(R.ps[:, n % 4, :], w[:, n // 4, :], h_chunk(R, n) if n < 4 else lat[:, b, t],
                                      start=True, stop=True).then_inc(pj, 1)
                            continue
                        b = n - 8
                        pe.wait_ge(pj_a, hp * PJ + (6 + 2 * b))
                        pe.wait_ge(pj_d, hp * PJ + (6 + 2 * b))
                        for i in range(8):
                            bank = 2 * b + i // 4
                            last = pe.matmul(R.ps[:, bank, (i % 4) * C:(i % 4 + 1) * C], lat[:, b, i * 128:(i + 1) * 128],
                                             w[:, 2, :], start=True, stop=True)
                        last.then_inc(pj, 1)

                def score(hp, i, hh):
                    b, tb = items[i]
                    a = 2 * i + hh
                    if i:
                        pe.wait_ge(exp_done, hp * (2 * I) + (a - 1))
                    full = (tb + 1) * 128
                    for c0 in range(0, full, CW):
                        n = min(CW, full - c0)
                        diag = c0 + n == full
                        bank = 2 * hh + c0 // CW
                        if diag:
                            pe.matmul(R.ps[:, bank, n - 128:n], R.identb[:], late[:], start=True, stop=False,
                                      skip_group_check=True)
                        last = pe.matmul(R.ps[:, bank, 0:n], q[:, hh, b, tb * 128:(tb + 1) * 128],
                                         k[:, hh, b, c0:c0 + n], start=not diag, stop=True, skip_group_check=True)
                    last.then_inc(s_full, 1)

                def group(hp, g):
                    kind, i, x = groups[g]
                    first = isinstance(hp, int) and hp == 0 and g < 2
                    if not first:
                        pe.wait_ge(t_d if g % 2 else t_a, hp * (NG // 2) + g // 2)
                    if kind == "turn":
                        hh, part = x
                        pe.wait_ge(exp_done, hp * (2 * I) + (2 * i + hh + 1))
                        for s in range(4 * part, min(4 * part + 4, items[i][1] + 1)):
                            last = pe.transpose(R.ps[:, 4 + g % 2, (s % 4) * 128:(s % 4 + 1) * 128],
                                                p[:, i % 2, hh, s * 128:(s + 1) * 128], R.ident[:])
                    else:
                        pe.wait_ge(inv_done, hp * 2 + (i + 1))
                        for n in range(8):
                            j, hh = n // 2, n % 2
                            last = pe.matmul(R.ps[PH * hh:PH * hh + PH, 4 + g % 2, j * 128:(j + 1) * 128],
                                             rinv[:, i, 4 * x + j, hh:hh + 1].broadcast_to([128, PH]), R.ident[:],
                                             start=True, stop=True)
                    last.then_inc(t_full, 1)

                def product(hp, i):
                    b, tb = items[i]
                    n = turned_of(i)
                    pe.wait_ge(t_a, hp * (NG // 2) + (n + 1) // 2)
                    pe.wait_ge(t_d, hp * (NG // 2) + n // 2)
                    if i % 8 == 0 and not (isinstance(hp, int) and hp == 0 and i == 0):
                        pe.wait_ge(y_done, hp * 4 + 2 * b)
                    for s in range(tb + 1):
                        for hh in range(2):
                            last = pe.matmul(R.ps[PH * hh:PH * hh + PH, 6 + tb // 4, (tb % 4) * 128:(tb % 4 + 1) * 128],
                                             v[:, b, s, PH * hh:PH * hh + PH], pT[:, i % 2, hh, s, :],
                                             start=(s == 0), stop=(s == tb))
                    last.then_inc(pv_done, 1)

                def step(hp):
                    project(hp)
                    pe.wait_ge(pj_a, hp * PJ + PJ)
                    pe.wait_ge(pj_d, hp * PJ + PJ)
                    for kind, i, x in order:
                        if kind == "score":
                            score(hp, i, x)
                        elif kind == "product":
                            product(hp, i)
                        else:
                            group(hp, of_item[kind, i, x])

                pe.wait_ge(const_loaded, 16)
                pe.wait_ge(zeroed, 2)
                step(0)
                with pe.Fori(1, STEPS) as hp:
                    step(hp)

            def projected(n):
                if n < 8:
                    b, t = chunk(n % 4)
                    return [((q if n < 4 else k)[0:PH, hh, b, t], R.ps[PH * hh:PH * hh + PH, n % 4, :],
                             PH ** -0.5 if n < 4 else 1.0) for hh in range(2)]
                b = n - 8
                return [(v[:, b, 4 * g:4 * g + 4, :].rearrange("p s c -> p (s c)"), R.ps[:, 2 * b + g, :], 1.0)
                        for g in range(2)]

            def moved(g):
                kind, i, x = groups[g]
                src = R.ps[:, 4 + g % 2, :]
                if kind == "spread":
                    return rrow[:, x, :], src
                hh, part = x
                n = min(4, items[i][1] + 1 - 4 * part)
                return pT[:, i % 2, hh, 4 * part:4 * part + n, :].rearrange("p s t -> p (s t)"), src[:, 0:n * 128]

            @block.scalar
            def _(act):
                def step(hp):
                    for n in range(0, PJ, 2):
                        act.wait_ge(pj, hp * PJ + (n + 1))
                        for dst, src, scale in projected(n):
                            act.activation(dst, src, ACT.Copy, scale=scale).then_inc(pj_a, 1)
                    for kind, i, x in order:
                        if kind == "score":
                            b, tb = items[i]
                            a = 2 * i + x
                            act.wait_ge(max_done, hp * (2 * I) + (a + 1))
                            if i >= 2:
                                act.wait_ge(t_full, hp * NG + turned_of(i - 2))
                            n = (tb + 1) * 128
                            src = R.ps[:, 2 * x:2 * x + 2, :].rearrange("p a c -> p (a c)")[:, 0:n]
                            act.activation(p[:, i % 2, x, 0:n], src, ACT.Exp, bias=nm[:, a % 4:a % 4 + 1],
                                           accum_out=rs[:, b, tb, x:x + 1]).then_inc(exp_done, 1)
                        elif kind in ("turn", "spread"):
                            g = of_item[kind, i, x]
                            if g % 2 == 0:
                                act.wait_ge(t_full, hp * NG + (g + 1))
                                if kind == "turn" and i >= 2:
                                    act.wait_ge(pv_done, hp * I + (i - 1))
                                dst, src = moved(g)
                                act.activation(dst, src, ACT.Copy).then_inc(t_a, 1)

                step(0)
                with act.Fori(1, STEPS) as hp:
                    step(hp)

            @block.vector
            def _(dve):
                def divide(hp, b):
                    dve.wait_ge(t_a, hp * (NG // 2) + (of_item["spread", b, 1] + 2) // 2)
                    for th in range(2):
                        dve.tensor_tensor(y[:, bass.ds(hp, 1), b, th * CW:(th + 1) * CW], R.ps[:, 6 + th, :].unsqueeze(1),
                                          rrow[:, th, :].unsqueeze(1), ALU.mult).then_inc(y_done, 1)

                def step(hp):
                    for n in range(1, PJ, 2):
                        dve.wait_ge(pj, hp * PJ + (n + 1))
                        for dst, src, scale in projected(n):
                            dve.tensor_scalar(dst, src, scale, None, ALU.mult).then_inc(pj_d, 1)
                    moved_here = hp * (NG // 2)
                    for kind, i, x in order:
                        if kind == "score":
                            b, tb = items[i]
                            a = 2 * i + x
                            dve.wait_ge(s_full, hp * (2 * I) + (a + 1))
                            if a >= 4:
                                dve.wait_ge(exp_done, hp * (2 * I) + (a - 3))
                            n = (tb + 1) * 128
                            src = R.ps[:, 2 * x:2 * x + 2, :].rearrange("p a c -> p (a c)")[:, 0:n]
                            dve.tensor_reduce(nm[:, a % 4:a % 4 + 1], src, X_AXIS, ALU.max, negate=True)\
                               .then_inc(max_done, 1)
                        elif kind == "product":
                            if i % 8 == 7:
                                b = items[i][0]
                                dve.wait_ge(exp_done, hp * (2 * I) + (2 * i + 2))
                                dve.reciprocal(rinv[:, b], rs[:, b]).then_inc(inv_done, 1)
                                dve.wait_ge(pv_done, hp * I + (i + 1))
                        else:
                            g = of_item[kind, i, x]
                            if g % 2:
                                dve.wait_ge(t_full, hp * NG + (g + 1))
                                if kind == "turn" and i >= 2:
                                    dve.wait_ge(pv_done, hp * I + (i - 1))
                                dst, src = moved(g)
                                dve.tensor_copy(dst, src).then_inc(t_d, 1)
                                if kind == "spread":
                                    dve.wait_ge(t_d, moved_here + (g + 1) // 2)
                            if kind == "spread" and x == 1:
                                divide(hp, i)

                step(0)
                with dve.Fori(1, STEPS) as hp:
                    step(hp)


def moe_stage(nc, R, W, dram):
    with ExitStack() as ctx:
        sb = lambda n, s, d=F32: ctx.enter_context(nc.sbuf_tensor("ex_" + n, s, d))
        sem = lambda n: nc.alloc_semaphore("ex_" + n)
        wsplit = sb("wsplit", [128, 2, N], BF16)
        rw, bias, before, shw = W.rw, W.bias, W.before, W.shw
        neg = sb("neg", [128, TB, E])
        score = sb("score", [128, TB, E])
        sbias = sb("sbias", [128, TB, E])
        hi, lo = sb("hi", [128, TB * GRP, 4]), sb("lo", [128, TB * GRP, 4])
        t1, t2 = sb("t1", [128, TB * GRP, 4]), sb("t2", [128, TB * GRP, 4])
        grp = sb("grp", [128, TB, GRP])
        gt, eq = sb("gt", [128, TB, GRP * GRP]), sb("eq", [128, TB, GRP * GRP])
        rank = sb("rank", [128, TB, GRP])
        keep, drop = sb("keep", [128, TB, GRP]), sb("drop", [128, TB, GRP])
        masked = sb("masked", [128, TB, E])
        left = sb("left", [128, TB, E])
        top = sb("top", [128, TB, 8])
        tot = sb("tot", [128, TB])
        parts = sb("parts", [128, TB, 2, 4, E // 2], BF16)
        prod, exped, routed, top_step, parted, turned, out = (
            sem(n) for n in ("prod", "exped", "step", "top", "parted", "turned", "out"))
        shs, shu, shh = sb("shs", [C, 2, CW]), sb("shu", [C, 2, CW]), sb("shh", [C, 2, CW])
        sh_g, sh_u, sh_silu, sh_copied, sh_hid, sh_down = (
            sem("sh_" + n) for n in ("g", "u", "silu", "copied", "hid", "down"))
        SH = 2 * NC
        wg = sb("wg", [C, 2, C])
        wu = sb("wu", [C, 2, C])
        wd = sb("wd", [C, 2, C])
        choose = sb("choose", [128, EP // 2, C], BF16)
        s = sb("s", [C, 2, CW])
        su = sb("su", [C, 2, CW])
        hid = sb("hid", [C, 2, CW])
        const_loaded = sem("const")
        ld = [sem("ld0"), sem("ld1")]
        g_full, silu_done, u_full, su_done, w_full, hid_done, d_done, res_done = (
            sem(n) for n in ("g_full", "silu", "u_full", "su", "w_full", "hid", "d", "res"))
        G_BANK, U_BANK, W_BANK = 4, 5, 6
        STEPS = EP // 2
        with nc.Block() as block:

            @block.sync
            def _(sp):
                def load(pair, slot):
                    sp.dma_start(wg[:, slot, :], dram["ex_gate"][bass.ds(pair * C, C), :]).then_inc(ld[slot], 16)
                    sp.dma_start(wu[:, slot, :], dram["ex_up"][bass.ds(pair * C, C), :]).then_inc(ld[slot], 16)
                    sp.dma_start(wd[:, slot, :], dram["ex_down"][bass.ds(pair * C, C), :]).then_inc(ld[slot], 16)

                load(0, 0)
                load(1, 1)
                with sp.Fori(1, STEPS) as kk:
                    for slot in range(2):
                        sp.wait_ge(d_done, kk * 8 + (4 * slot - 4))
                        load(kk * 2 + slot, slot)

            @block.gpsimd
            def _(pool):
                pool.memset(parts[:, :, :, 3, :], 0.0).then_inc(parted, 1)
                pool.dma_start(choose[:], dram["choose"]).then_inc(const_loaded, 16)
                for i in range(SH):
                    pool.wait_ge(sh_silu, i + 1)
                    pool.wait_ge(sh_copied, i + 1)
                    if i >= 2:
                        pool.wait_ge(sh_down, i - 1)
                    pool.tensor_tensor(shh[:, i % 2, :], shs[:, i % 2, :], shu[:, i % 2, :], ALU.mult)\
                        .then_inc(sh_hid, 1)

            @block.tensor
            def _(pe):
                pe.wait_ge(W.loaded, W.count)
                for tb in range(TB):
                    last = pe.matmul(R.ps[:, 6 + tb // 8, (tb % 8) * E:(tb % 8 + 1) * E], h_block(R, tb), rw[:],
                                     start=True, stop=True)
                last.then_inc(prod, 1)

                def shared_down(i):
                    pe.wait_ge(sh_hid, i + 1)
                    pe.matmul(R.ps[:, i % 4, :], shw[:, 2, i // 4, :], shh[:, i % 2, :], start=(i < 4), stop=True,
                              skip_group_check=True).then_inc(sh_down, 1)

                for i in range(SH):
                    if i:
                        pe.wait_ge(sh_silu, i)
                    pe.matmul(R.ps[:, G_BANK, :], shw[:, 0, i // 4, :], h_chunk(R, i % 4), start=True, stop=True)\
                        .then_inc(sh_g, 1)
                    if i:
                        pe.wait_ge(sh_copied, i)
                    pe.matmul(R.ps[:, U_BANK, :], shw[:, 1, i // 4, :], h_chunk(R, i % 4), start=True, stop=True)\
                        .then_inc(sh_u, 1)
                    if i:
                        shared_down(i - 1)
                shared_down(SH - 1)

                pe.wait_ge(sh_silu, SH)
                pe.wait_ge(sh_copied, SH)
                pe.wait_ge(parted, 6)
                for tb in range(TB):
                    for i in range(2):
                        dst = R.ps[:, 4 + tb // 4, :].bitcast(BF16)[:, ((tb % 4) * 2 + i) * 128:((tb % 4) * 2 + i + 1) * 128]
                        last = pe.transpose(dst, parts[:, tb, i].rearrange("p a e -> p (a e)"), R.identb[:])
                    if tb % 4 == 3:
                        last.then_inc(turned, 1)

                def down(kk, i):
                    m = kk * 8 + i
                    pe.wait_ge(hid_done, m + 1)
                    pe.matmul(R.ps[:, i % 4, :], wd[:, (i // 4) % 2, :], hid[:, i % 2, :], start=False,
                              stop=True, skip_group_check=True).then_inc(d_done, 1)

                def step(kk, half, first=False):
                    for i in range(8):
                        m = kk * 8 + i
                        slot, c = i // 4, i % 4
                        if c == 0:
                            pe.wait_ge(ld[slot], kk * 48 + 48)
                        if not (first and i == 0):
                            pe.wait_ge(silu_done, m)
                        pe.matmul(R.ps[:, G_BANK, :], wg[:, slot, :], h_chunk(R, c), start=True, stop=True).then_inc(g_full, 1)
                        if not (first and i == 0):
                            pe.wait_ge(su_done, m)
                        pe.matmul(R.ps[:, U_BANK, :], wu[:, slot, :], h_chunk(R, c), start=True, stop=True).then_inc(u_full, 1)
                        if not (first and i == 0):
                            pe.wait_ge(hid_done, m)
                        pair = choose[:, bass.ds(kk * 2 + (slot - half * (EP // 2)), 1), :]
                        pe.matmul(R.ps[:, W_BANK, :], pair, wsplit[:, half, c * CW:(c + 1) * CW],
                                  start=True, stop=True).then_inc(w_full, 1)
                        if not (first and i == 0):
                            down(kk, i - 1)

                pe.wait_ge(out, TB // 4)
                pe.wait_ge(const_loaded, 16)
                step(0, 0, True)
                with pe.Fori(1, STEPS // 2) as kk:
                    step(kk, 0)
                with pe.Fori(STEPS // 2, STEPS) as kk:
                    step(kk, 1)
                down(STEPS - 1, 7)

            @block.scalar
            def _(act):
                act.wait_ge(routed, 1)
                act.activation(neg[:], neg[:], ACT.Exp).then_inc(exped, 1)
                for i in range(SH):
                    act.wait_ge(sh_g, i + 1)
                    if i >= 2:
                        act.wait_ge(sh_hid, i - 1)
                    act.activation(shs[:, i % 2, :], R.ps[:, G_BANK, :], ACT.Silu).then_inc(sh_silu, 1)
                    act.wait_ge(sh_u, i + 1)
                    act.activation(shu[:, i % 2, :], R.ps[:, U_BANK, :], ACT.Copy).then_inc(sh_copied, 1)
                for g in range(TB // 4):
                    act.wait_ge(turned, g + 1)
                    src = R.ps[:, 4 + g, :].bitcast(BF16).rearrange("p (t i c) -> p i t c", t=4, i=2)
                    act.activation(wsplit[:, :, g * CW:(g + 1) * CW].rearrange("p i (t c) -> p i t c", t=4), src, ACT.Copy)\
                       .then_inc(out, 1)

                def step(kk, first=False):
                    for i in range(8):
                        m = kk * 8 + i
                        act.wait_ge(g_full, m + 1)
                        if not (first and i < 2):
                            act.wait_ge(su_done, m - 1)
                        act.activation(s[:, i % 2, :], R.ps[:, G_BANK, :], ACT.Silu).then_inc(silu_done, 1)

                step(0, True)
                with act.Fori(1, STEPS) as kk:
                    step(kk)

            @block.vector
            def _(dve):
                n = 0

                def after(ins):
                    nonlocal n
                    n += 1
                    ins.then_inc(routed, 1)

                def tt(out, a, b, op):
                    after(dve.tensor_tensor(out, a, b, op))

                def ts(out, a, s1, s2, op0, op1=None):
                    after(dve.tensor_scalar(out, a, s1, s2, op0, op1) if op1 else dve.tensor_scalar(out, a, s1, s2, op0))

                dve.wait_ge(W.loaded, W.count)
                dve.wait_ge(prod, 1)
                logits = R.ps[:, 6:8, :].rearrange("p a (t e) -> p (a t) e", e=E)
                ts(neg[:], logits, -1.0, 87.0, ALU.mult, ALU.min)
                dve.wait_ge(exped, 1)
                ts(score[:], neg[:], 1.0, None, ALU.add)
                dve.wait_ge(routed, n)
                after(dve.reciprocal(score[:], score[:]))
                dve.wait_ge(routed, n)
                tt(sbias[:], score[:], bias[:].unsqueeze(1).broadcast_to([128, TB, E]), ALU.add)
                dve.wait_ge(routed, n)
                v = sbias[:].rearrange("p t (g e) -> p (t g) e", g=GRP)
                tt(hi[:], v[:, :, 0:4], v[:, :, 4:8], ALU.max)
                tt(lo[:], v[:, :, 0:4], v[:, :, 4:8], ALU.min)
                dve.wait_ge(routed, n)
                for wd in (2, 1):
                    a, b = slice(0, wd), slice(wd, 2 * wd)
                    tt(t1[:, :, 0:wd], hi[:, :, a], hi[:, :, b], ALU.min)
                    tt(t2[:, :, 0:wd], lo[:, :, a], lo[:, :, b], ALU.max)
                    tt(hi[:, :, a], hi[:, :, a], hi[:, :, b], ALU.max)
                    dve.wait_ge(routed, n)
                    tt(lo[:, :, a], t1[:, :, 0:wd], t2[:, :, 0:wd], ALU.max)
                    dve.wait_ge(routed, n)
                tt(grp[:].rearrange("p t g -> p (t g)").unsqueeze(2), hi[:, :, 0:1], lo[:, :, 0:1], ALU.add)
                dve.wait_ge(routed, n)
                own = grp[:].unsqueeze(3).broadcast_to([128, TB, GRP, GRP])
                other = grp[:].unsqueeze(2).broadcast_to([128, TB, GRP, GRP])
                g4 = lambda x: x[:].rearrange("p t (a b) -> p t a b", a=GRP)
                tt(g4(gt), other, own, ALU.is_gt)
                tt(g4(eq), other, own, ALU.is_equal)
                dve.wait_ge(routed, n)
                tt(eq[:], eq[:], before[:].unsqueeze(1).broadcast_to([128, TB, GRP * GRP]), ALU.mult)
                dve.wait_ge(routed, n)
                tt(gt[:], gt[:], eq[:], ALU.add)
                dve.wait_ge(routed, n)
                after(dve.tensor_reduce(rank[:], g4(gt), X_AXIS, ALU.add))
                dve.wait_ge(routed, n)
                ts(keep[:], rank[:], 3.5, None, ALU.is_lt)
                dve.wait_ge(routed, n)
                ts(drop[:], keep[:], 1e38, -1e38, ALU.mult, ALU.add)
                e4 = lambda x: x[:].rearrange("p t (g e) -> p t g e", g=GRP)
                wide = lambda x: x[:].unsqueeze(3).broadcast_to([128, TB, GRP, 8])
                tt(e4(masked), e4(sbias), wide(keep), ALU.mult)
                dve.wait_ge(routed, n)
                tt(e4(masked), e4(masked), wide(drop), ALU.add)
                dve.wait_ge(routed, n)
                for tb in range(TB):
                    dve.max(top[:, tb, :], masked[:, tb, :]).then_inc(top_step, 1)
                for tb in range(TB):
                    dve.wait_ge(top_step, tb + 1)
                    dve.match_replace(left[:, tb, :], top[:, tb, :], masked[:, tb, :], -2e38).then_inc(top_step, 1)
                dve.wait_ge(top_step, 2 * TB)
                tt(left[:], left[:], masked[:], ALU.is_lt)
                dve.wait_ge(routed, n)
                tt(score[:], score[:], left[:], ALU.mult)
                dve.wait_ge(routed, n)
                after(dve.tensor_reduce(tot[:], score[:], X_AXIS, ALU.add))
                dve.wait_ge(routed, n)
                ts(tot[:], tot[:], 1e-20, None, ALU.add)
                dve.wait_ge(routed, n)
                after(dve.reciprocal(tot[:], tot[:]))
                dve.wait_ge(routed, n)
                tt(score[:], score[:], tot[:].unsqueeze(2).broadcast_to([128, TB, E]), ALU.mult)
                dve.wait_ge(routed, n)
                part = lambda i: parts[:, :, :, i, :]
                h = lambda x: x[:].rearrange("p t (i e) -> p t i e", i=2)
                for i, op in enumerate(((part(0), h(score)), (h(masked), h(score), part(0)), (part(1), h(masked)),
                                        (h(left), h(masked), part(1)), (part(2), h(left)))):
                    if len(op) == 2:
                        dve.tensor_copy(*op).then_inc(parted, 1)
                    else:
                        dve.tensor_tensor(*op, ALU.subtract).then_inc(parted, 1)
                    dve.wait_ge(parted, i + 2)

                def step(kk, first=False):
                    for i in range(8):
                        m = kk * 8 + i
                        dve.wait_ge(silu_done, m + 1)
                        dve.wait_ge(u_full, m + 1)
                        if not (first and i < 2):
                            dve.wait_ge(d_done, m - 1)
                        dve.tensor_tensor(su[:, i % 2, :], s[:, i % 2, :], R.ps[:, U_BANK, :], ALU.mult)\
                           .then_inc(su_done, 1)
                        dve.wait_ge(su_done, m + 1)
                        dve.wait_ge(w_full, m + 1)
                        dve.tensor_tensor(hid[:, i % 2, :], su[:, i % 2, :], R.ps[:, W_BANK, :], ALU.mult)\
                           .then_inc(hid_done, 1)

                step(0, True)
                with dve.Fori(1, STEPS) as kk:
                    step(kk)
                dve.wait_ge(d_done, EP * 4)
                for c in range(NC):
                    b, t = chunk(c)
                    dve.scalar_tensor_tensor(R.x[:, b, t], R.ps[:, c, :], mod_cols(R, 2, 1, b)[2], R.x[:, b, t],
                                             ALU.mult, ALU.add).then_inc(res_done, 1)


def linear_stage(nc, R, W, attn):
    with ExitStack() as ctx:
        sb = lambda n, s, d=F32: ctx.enter_context(nc.sbuf_tensor("la_" + n, s, d))
        sem = lambda n: nc.alloc_semaphore("la_" + n)
        wq, wkv, sc = W.wq, W.wkv, W.sc
        qf = sb("qf", [C, NC, CW])
        q2 = sb("q2", [C, NC, CW])
        k = sb("k", [128, TB, C])
        v = sb("v", [128, TB, C])
        k2 = sb("k2", [128, TB, C])
        kn = sb("kn", [128, TB, HEADS])
        mask = sb("mask", [128, C])
        kv = sb("kv", [C, B, C])
        qp, q_copied, squared, norm, q_root, q_len, q_hat, kvp, v_copied, k_sq, k_sum, k_root, k_hat, outer, masked, \
            att, done, step, nc_step = (sem(n) for n in (
                "qp", "q_copied", "squared", "norm", "q_root", "q_len", "q_hat", "kvp", "v_copied", "k_sq",
                "k_sum", "k_root", "k_hat", "outer", "masked", "att", "done", "step", "nc_step"))
        with nc.Block() as block:

            @block.tensor
            def _(pe):
                pe.wait_ge(W.loaded, W.count)
                for g in range(TB // 4):
                    if g >= 2:
                        pe.wait_ge(v_copied, g - 1)
                        pe.wait_ge(k_sq, 2 * (g - 1) - 1)
                    for a in range(2):
                        for i in range(4):
                            last = pe.matmul(R.ps[:, 2 * (g % 2) + a, i * C:(i + 1) * C], h_block(R, 4 * g + i),
                                             wkv[:, a, :], start=True, stop=True)
                    last.then_inc(kvp, 1)
                for c in range(NC):
                    pe.matmul(R.ps[:, 4 + c, :], wq[:], h_chunk(R, c), start=True, stop=True).then_inc(qp, 1)
                pe.wait_ge(v_copied, TB // 4)
                pe.wait_ge(k_sq, TB // 2)
                for c in range(NC):
                    pe.wait_ge(squared, c + 1)
                    pe.matmul(R.ps[:, c, :], R.blk8[:], q2[:, c, :], start=True, stop=True).then_inc(norm, 1)
                pe.wait_ge(q_root, NC)
                pe.wait_ge(k_hat, 1)
                for b in range(B):
                    for s in range(8):
                        last = pe.matmul(R.ps[:, 0, b * C:(b + 1) * C], k[:, 8 * b + s, :], v[:, 8 * b + s, :],
                                         start=(s == 0), stop=(s == 7))
                    last.then_inc(outer, 1)
                pe.wait_ge(q_hat, NC)
                for c in range(NC):
                    pe.wait_ge(masked, c // 2 + 1)
                    pe.matmul(R.ps[:, 4 + c, :], kv[:, c // 2, :], qf[:, c, :], start=True, stop=True).then_inc(att, 1)

            @block.scalar
            def _(act):
                act.wait_ge(W.loaded, W.count)
                act.activation(sc[:], sc[:], ACT.Sigmoid).then_inc(nc_step, 1)
                act.wait_ge(nc_step, 1)
                act.activation(sc[:], sc[:], ACT.Exp, scale=-math.log(T)).then_inc(nc_step, 1)
                for g in range(TB // 4):
                    act.wait_ge(kvp, g + 1)
                    act.activation(v[:, 4 * g:4 * g + 4, :].rearrange("p t c -> p (t c)"), R.ps[:, 2 * (g % 2) + 1, :],
                                   ACT.Copy).then_inc(v_copied, 1)
                for c in range(NC):
                    act.wait_ge(qp, c + 1)
                    act.activation(q2[:, c, :], R.ps[:, 4 + c, :], ACT.Square).then_inc(squared, 1)
                act.wait_ge(k_sum, 1)
                act.activation(kn[:], kn[:], ACT.Sqrt).then_inc(k_root, 1)
                for c in range(NC):
                    act.wait_ge(norm, c + 1)
                    act.activation(q2[:, c, :], R.ps[:, c, :], ACT.Sqrt).then_inc(q_root, 1)
                for c in range(NC):
                    b, t = chunk(c)
                    act.wait_ge(att, c + 1)
                    act.activation(attn[:, b, t], R.ps[:, 4 + c, :], ACT.Copy).then_inc(done, 1)

            @block.vector
            def _(dve):
                for g in range(TB // 4):
                    dve.wait_ge(kvp, g + 1)
                    kg = k[:, 4 * g:4 * g + 4, :].rearrange("p t c -> p (t c)")
                    dve.tensor_copy(kg, R.ps[:, 2 * (g % 2), :]).then_inc(k_sq, 1)
                    dve.wait_ge(k_sq, 2 * g + 1)
                    dve.tensor_tensor(k2[:, 4 * g:4 * g + 4, :].rearrange("p t c -> p (t c)"), kg, kg, ALU.mult)\
                       .then_inc(k_sq, 1)
                dve.wait_ge(k_sq, TB // 2)
                kh = lambda x: x[:].rearrange("p t (h c) -> p t h c", c=8)
                dve.tensor_reduce(kn[:], kh(k2), X_AXIS, ALU.add).then_inc(k_sum, 1)
                dve.wait_ge(k_root, 1)
                dve.tensor_scalar(kn[:], kn[:], 1e-12, None, ALU.max).then_inc(step, 1)
                dve.wait_ge(step, 1)
                dve.reciprocal(kn[:], kn[:]).then_inc(step, 1)
                dve.wait_ge(step, 2)
                dve.tensor_tensor(kh(k), kh(k), kn[:].unsqueeze(3).broadcast_to([128, TB, HEADS, 8]), ALU.mult)\
                   .then_inc(k_hat, 1)
                dve.wait_ge(nc_step, 2)
                dve.tensor_tensor(mask[:].rearrange("p (h c) -> p h c", c=8), R.blk8[:].rearrange("p (h c) -> p h c", c=8),
                                  sc[:].unsqueeze(2).broadcast_to([128, HEADS, 8]), ALU.mult).then_inc(step, 1)
                for c in range(NC):
                    dve.wait_ge(q_root, c + 1)
                    dve.tensor_scalar(q2[:, c, :], q2[:, c, :], 1e-12, None, ALU.max).then_inc(q_len, 1)
                    dve.wait_ge(q_len, 2 * c + 1)
                    dve.reciprocal(q2[:, c, :], q2[:, c, :]).then_inc(q_len, 1)
                    dve.wait_ge(q_len, 2 * c + 2)
                    dve.tensor_tensor(qf[:, c, :], R.ps[:, 4 + c, :], q2[:, c, :], ALU.mult).then_inc(q_hat, 1)
                dve.wait_ge(step, 3)
                dve.wait_ge(outer, 2)
                for b in range(B):
                    dve.tensor_tensor(kv[:, b, :], R.ps[:, 0, b * C:(b + 1) * C], mask[:], ALU.mult).then_inc(masked, 1)


def store_stage(nc, R, out):
    stored = nc.alloc_semaphore("stored")
    with nc.Block() as block:

        @block.sync
        def _(sp):
            sp.dma_start(out, R.x[:]).then_inc(stored, 16)
            sp.wait_ge(stored, 16)


def build_program(nc, dram, out, halves=8):
    R = Residents(nc)
    setup_stage(nc, R, dram)

    def softmax_layer(name, layer, rows, dim, groups, hg, mask):
        with ExitStack() as ctx:
            A = Attn(nc, name, rows, dim, groups, hg, mask)
            W = Weights(nc, ctx, name)
            W.w = W.tile("w", [C, 3, C])
            W.loads += [(W.w[:, i, :], dram[f"L{layer}_w{n}T"]) for i, n in enumerate("qkv")]
            W.bqk, W.bv = (W.tile("bqk", [C, 2]), W.add("bv", [128, C], dram["L1_bv"].broadcast_to([128, C]))) \
                if mask else (None, None)
            if mask:
                W.loads += [(W.bqk[:, i:i + 1], dram[f"L1_b{n}"]) for i, n in enumerate("qk")]
            W.den_sel = W.add("den_sel", [128, 64], dram["den_sel"])
            W.den_spread = W.add("den_spread", [128, 2, 128], dram["den_spread"])
            if layer == 0:
                W.lam, W.cols = W.tile("lam", [128, 4, 4]), W.tile("cols", [128, 8])
                W.loads += [(W.lam[:, i, :], dram[f"L0_lam{i}"].broadcast_to([128, 4])) for i in range(4)]
                W.loads += [(W.cols[:, 0:2], dram["parity"]), (W.cols[:, 2:3], dram["subln_col"])]
                W.pick = W.add("pick", [128, 4, C], dram["pick"])
                W.head_sum = W.add("head_sum", [128, 32], dram["head_sum"])
                W.head_spread = W.add("head_spread", [128, NC, 128], dram["head_spread"])
                W.prod, W.dots = W.tile("prod", [128, 2, 4]), W.tile("dots", [128, 2])
                W.lam_step, W.exped = nc.alloc_semaphore("lam_step"), nc.alloc_semaphore("lam_exped")
                W.wo = W.add("wo", [C, C], dram["L0_woT"])
            else:
                W.wo, W.bo = W.add("wo", [128, 2, C], dram["L1_woG"]), W.add("bo", [C, 1], dram["L1_bo"])
            A.v = ctx.enter_context(nc.sbuf_tensor(name + "v", [128, groups, 8, hg, 9], F32))
            A.q = ctx.enter_context(nc.sbuf_tensor(name + "q", [128, 2, A.row_tiles, T], BF16))
            A.k = ctx.enter_context(nc.sbuf_tensor(name + "k", [128, 2, 4, T], BF16))
            norm_stage(nc, R, layer, 0, W, init_operands(A))
            project_stage(nc, R, W, A, layer)
            A.on = ctx.enter_context(nc.sbuf_tensor(name + "on", [128, groups // 2, T], F32))
            softmax_stage(nc, R, W, A)
            if layer == 0:
                diff_out_stage(nc, R, W, A)
            else:
                out_stage(nc, R, W, 1, 0, "o1", lambda i, c: A.on[:, (c // 2) * 2 + i, chunk(c)[1]], 2, W.wo, W.bo)

    def lora_layer(layer):
        with ExitStack() as ctx:
            W = Weights(nc, ctx, f"f{layer}")
            p = f"L{layer}_f"
            W.w1, W.w2 = W.add("w1", [C, HID], dram[p + "W1T"]), W.add("w2", [C, HB, C], dram[p + "W2T"])
            W.b1, W.b2 = W.add("b1", [C, HB], dram[p + "b1"]), W.add("b2", [C, 1], dram[p + "b2"])
            W.scale = W.add("scale", [128, 1], dram[p + "scale"].broadcast_to([128, 1]))
            W.eye8 = W.add("eye8", [8, 8], dram["ident"][0:8, 0:8])
            norm_stage(nc, R, layer, 1, W)
            lora_stage(nc, R, W, layer)

    def layer_0a():
        softmax_layer("a0", 0, 32, 4, 16, 2, False)

    def layer_0b():
        lora_layer(0)

    def layer_1a():
        softmax_layer("a1", 1, 64, 8, 8, 4, True)

    def layer_1b():
        with ExitStack() as ctx:
            W = Weights(nc, ctx, "mx")
            W.w, W.mu = W.tile("w", [C, 3, C]), W.tile("mu", [C, 4])
            W.loads += [(W.w[:, i, :], dram[f"L1_W{n}T"]) for i, n in enumerate("rkv")]
            W.loads += [(W.mu[:, i:i + 1], dram[f"L1_mu{n}"]) for i, n in enumerate("rk")]
            norm_stage(nc, R, 1, 1, W)
            mix_stage(nc, R, W)

    def layer_2a():
        with ExitStack() as ctx:
            W = Weights(nc, ctx, "a2")
            W.down = W.add("down", [C, C], dram["L2_kv_down"])
            W.wo = W.add("wo", [128, HEADS // 2, C], dram["L2_wout"])
            norm_stage(nc, R, 2, 0, W)
            y = ctx.enter_context(nc.sbuf_tensor("y2", [128, HEADS // 2, B, T], F32))
            with ExitStack() as inner:
                lat = inner.enter_context(nc.sbuf_tensor("lat", [C, B, T], F32))
                latent_stage(nc, R, W, lat)
                causal_stage(nc, R, dram, lat, y)
            out_stage(nc, R, W, 2, 0, "o2", lambda i, c: y[:, i, c // 2, chunk(c)[1]], HEADS // 2, W.wo)

    def layer_2b():
        with ExitStack() as ctx:
            W = Weights(nc, ctx, "f2")
            W.rw = W.add("rw", [C, E], dram["L2_routerT"])
            W.bias = W.add("bias", [128, E], dram["L2_ebias"].broadcast_to([128, E]))
            W.before = W.add("before", [128, GRP * GRP], dram["before"].broadcast_to([128, GRP * GRP]))
            W.shw = W.tile("shw", [C, 3, 2, C])
            W.loads += [(W.shw[:, i], dram["sh_" + n]) for i, n in enumerate(("gate", "up", "down"))]
            norm_stage(nc, R, 2, 1, W)
            moe_stage(nc, R, W, dram)

    def layer_3a():
        with ExitStack() as ctx:
            W = Weights(nc, ctx, "a3")
            W.wq, W.wkv = W.add("wq", [C, C], dram["L3_wqT"]), W.tile("wkv", [C, 2, C])
            W.loads += [(W.wkv[:, i, :], dram[f"L3_w{n}T"]) for i, n in enumerate("kv")]
            W.sc = W.add("sc", [128, HEADS], dram["L3_norm"].broadcast_to([128, HEADS]))
            W.wo = W.add("wo", [C, 1, C], dram["L3_woT"])
            norm_stage(nc, R, 3, 0, W)
            attn = ctx.enter_context(nc.sbuf_tensor("attn3", [C, B, T], F32))
            linear_stage(nc, R, W, attn)
            out_stage(nc, R, W, 3, 0, "o3", lambda i, c: attn[:, c // 2, chunk(c)[1]], 1, W.wo)

    def layer_3b():
        lora_layer(3)

    for i, half in enumerate((layer_0a, layer_0b, layer_1a, layer_1b, layer_2a, layer_2b, layer_3a, layer_3b)):
        if i in halves:
            with nc.cleanup_on_exit():
                half()
    store_stage(nc, R, out)


def constants():
    r = np.arange(128)
    k = {"ident": np.eye(128, dtype=np.float32), "blk8": (r[:, None] // 8 == r[None, :] // 8).astype(np.float32),
         "den_sel": (r[:, None] == r[None, :64] % 8 * 16 + 8).astype(np.float32),
         "den_spread": np.stack([(r[:, None] == 64 * w + r[None, :] // 16) & (r[None, :] % 16 < 8) for w in range(2)],
                                1).astype(np.float32),
         "head_sum": (r[:, None] // 8 == r[None, :32] % 16).astype(np.float32),
         "head_spread": np.stack([(r[:, None] == 32 * c + r[None, :] // 8) for c in range(NC)], 1).astype(np.float32),
         "parity": np.stack([(r // 32) % 2 == 0, (r // 32) % 2 == 1], 1).astype(np.float32),
         "late": np.where(r[None, :] > r[:, None], NEG, 0.0).astype(np.float32),
         "lateT": np.where(r[:, None] > r[None, :], NEG, 0.0).astype(np.float32)}
    pick = np.zeros((128, 4, C), np.float32)
    for pair in range(4):
        for j in range(4):
            for odd in range(2):
                for c in range(8):
                    pick[32 * j + 16 * odd + c, pair, (2 * (2 * pair + odd) + j // 2) * 8 + c] = 1
    k["pick"] = pick
    g = np.arange(GRP)
    k["before"] = (g[None, :] < g[:, None]).astype(np.float32).reshape(1, -1)
    choose = np.zeros((128, EP // 2, C), np.float32)
    for e in range(E // 2):
        choose[[e, 32 + e, 64 + e], e // 2, (e % 2) * EH:(e % 2) * EH + EH] = 1
    k["choose"] = choose
    return k


def lay_out(inputs):
    i = {k: np.asarray(v) for k, v in inputs.items()}
    d = {"xT": i["L0_attn_query"].transpose(2, 0, 1)}
    for l in range(LAYERS):
        d[f"L{l}_wmod"] = i[f"L{l}_wmod"]
        d[f"L{l}_cT"] = i[f"L{l}_c"].T
    for n in "qkv":
        d[f"L0_w{n}T"] = i[f"L0_attn_W{n}"].T
        d[f"L1_w{n}T"] = i[f"L1_attn_w{n}_w"].T
        d[f"L3_w{n}T"] = i[f"L3_attn_W{n}"].T
    for n, m in enumerate(("q1", "k1", "q2", "k2")):
        d[f"L0_lam{n}"] = i[f"L0_attn_lambda_{m}"].reshape(1, 4)
    d["subln_col"] = np.tile(i["L0_attn_subln_w"], HEADS).reshape(C, 1)
    d["L0_woT"] = i["L0_attn_Wo"].T
    for l in (0, 3):
        d[f"L{l}_fW1T"] = i[f"L{l}_ffn_W1"].T
        d[f"L{l}_fW2T"] = i[f"L{l}_ffn_W2"].T.reshape(HB, C, C).transpose(1, 0, 2)
        d[f"L{l}_fb1"] = i[f"L{l}_ffn_b1"].reshape(HB, C).T
        d[f"L{l}_fb2"] = i[f"L{l}_ffn_b2"].reshape(C, 1)
        d[f"L{l}_fscale"] = i[f"L{l}_ffn_scale"].reshape(1, 1)
    d["L1_bq"], d["L1_bk"] = i["L1_attn_wq_b"].reshape(C, 1), i["L1_attn_wk_b"].reshape(C, 1)
    d["L1_bv"], d["L1_bo"] = i["L1_attn_wv_b"].reshape(1, C), i["L1_attn_wo_b"].reshape(C, 1)
    wo = np.zeros((4, 2, 16, 2, C), np.float32)
    wo[:, :, 0:8] = i["L1_attn_wo_w"].T.reshape(2, 2, 4, 8, C).transpose(2, 1, 3, 0, 4)
    d["L1_woG"] = wo.reshape(128, 2, C)
    for n in "rkv":
        d[f"L1_W{n}T"] = i[f"L1_ffn_W_{n}"].T
    for n in "rk":
        d[f"L1_mu{n}"] = i[f"L1_ffn_mu_{n}"].reshape(C, 1)
    d["L2_kv_down"] = i["L2_attn_w_kv_down"]
    d["L2_wq"] = i["L2_attn_w_q"]
    d["L2_wk"], d["L2_wv"] = i["L2_attn_w_kv_up"][:, :HEADS * PH], i["L2_attn_w_kv_up"][:, HEADS * PH:]
    d["L2_wout"] = i["L2_attn_w_out"].reshape(HEADS // 2, C, C).transpose(1, 0, 2)
    d["L2_routerT"] = i["L2_ffn_router_w"].T
    d["L2_ebias"] = i["L2_ffn_e_bias"].reshape(1, E)

    for n in ("gate", "up"):
        d["sh_" + n] = i[f"L2_ffn_sh_{n}_w"].reshape(C, 2, C)
        d["ex_" + n] = i[f"L2_ffn_{n}_w"].reshape(EP, 2, C, EH).transpose(0, 2, 1, 3).reshape(-1, C)
    d["sh_down"] = i["L2_ffn_sh_down_w"].reshape(2, C, C).transpose(1, 0, 2)
    d["ex_down"] = i["L2_ffn_down_w"].reshape(-1, C)
    d["L3_woT"] = i["L3_attn_Wo"].T.reshape(C, 1, C)
    d["L3_norm"] = i["L3_attn_norm_const"].reshape(1, HEADS)
    d.update(constants())
    return {k: np.ascontiguousarray(v) for k, v in d.items()}


def kernel(**inputs):
    import concourse.bacc as bacc
    from concourse.bass_utils import run_bass_kernel_spmd

    nc = bacc.Bacc("TRN2", target_bir_lowering=False, num_devices=1)
    arrays = {"in_" + k: v for k, v in lay_out(inputs).items()}
    dram = {k[3:]: nc.dram_tensor(k, a.shape, mybir.dt.from_np(a.dtype), kind="ExternalInput").ap()
            for k, a in arrays.items()}
    out = nc.dram_tensor("out_x", (C, B, T), F32, kind="ExternalOutput").ap()
    build_program(nc, dram, out, range(8))
    r = run_bass_kernel_spmd(nc, [arrays], core_ids=[0])
    return np.ascontiguousarray(r.results[0]["out_x"].transpose(1, 2, 0))
```

```python
import math

import numpy as np

import concourse.bass as bass
from concourse import mybir
from contextlib import ExitStack

F32 = mybir.dt.float32
BF16 = mybir.dt.bfloat16
ALU = mybir.AluOpType
ACT = mybir.ActivationFunctionType
X_AXIS = mybir.AxisListType.X

C = 128
B = 2
T = 1024
N = B * T
CW = 512
NC = N // CW
TB = N // 128
HEADS = 16
LAYERS = 4
NEG = -1e30
LN_EPS = 1e-5
LAMBDA_INIT = float(0.8 - 0.6 * np.exp(-0.3 * 12))
HID = 512
HB = HID // C
E = 64
EH = 64
EP = E // 2
GRP = 8
PH = 64
HALF = T // 2


class NormSems:

    def __init__(self, nc):
        sem = lambda n: nc.alloc_semaphore("norm_" + n)
        self.mean, self.centred, self.squared, self.var = sem("mean"), sem("centred"), sem("squared"), sem("var")
        self.dev, self.step, self.out = sem("dev"), sem("step"), sem("out")
        self.spread, self.scaled, self.warm = sem("spread"), sem("scaled"), sem("warm")
        self.calls = 0


class Residents:

    def __init__(self, nc):
        sb = lambda n, s, d=F32: nc.alloc_sbuf_tensor(n + "_res", s, d)
        self.x = sb("x", [C, B, T])
        self.h = sb("h", [C, B, T + 4])
        self.mod = sb("mod", [C, LAYERS, 6, B])
        self.scale1 = sb("scale1", [C, LAYERS, 2, B])
        self.gate = sb("gate", [C, LAYERS * 2 * B])
        self.ident = sb("ident", [128, 128])
        self.identb = sb("identb", [128, 128], BF16)
        self.centre = sb("centre", [128, 128])
        self.ones8 = sb("ones8", [128, 4, 32])
        self.blk8 = sb("blk8", [128, 128])
        self.eps = sb("eps", [128, 1])
        self.ps = nc.alloc_psum_tensor("ps", [128, 8, CW], F32)
        self.norm_sems = NormSems(nc)


class Weights:

    def __init__(self, nc, ctx, name):
        self.nc, self.ctx, self.name, self.loads = nc, ctx, name, []
        self.loaded = nc.alloc_semaphore(name + "weights_loaded")

    def tile(self, name, shape):
        return self.ctx.enter_context(self.nc.sbuf_tensor(self.name + name, shape, F32))

    def add(self, name, shape, src):
        t = self.tile(name, shape)
        self.loads.append((t[:], src))
        return t

    @property
    def count(self):
        return 16 * len(self.loads)


class Attn:

    def __init__(self, nc, name, rows, dim, groups, heads_of_group, mask):
        self.name, self.rows, self.dim, self.groups = name, rows, dim, groups
        self.row_tiles = 4 * rows // 128
        self.heads_of_group, self.mask = heads_of_group, mask
        self.parts_dram = nc.dram_tensor(name + "parts", [2, 3, B * C, T], BF16, kind="Internal").ap()
        self.mask_dram = nc.dram_tensor(name + "mask", [groups, T], BF16, kind="Internal").ap() if mask else None
        self.first_part = 4 if mask else 3
        self.scale = dim ** -0.5
        self.n_scaled = 2 if mask else 1
        self.ld = [nc.alloc_semaphore(name + "ld0"), nc.alloc_semaphore(name + "ld1")]
        self.first_k = nc.alloc_semaphore(name + "first_k")
        self.n_k_loads = 2 * (3 + (1 if mask else 0))
        self.stored = [nc.alloc_semaphore(name + "stored0"), nc.alloc_semaphore(name + "stored1")]
        self.inited = nc.alloc_semaphore(name + "inited")
        self.n_inited = 7 + (2 * 128 // rows if mask else 0)



def chunk(c):
    return c // 2, slice((c % 2) * CW, (c % 2) * CW + CW)


class Modulation:

    PARTS = (slice(0, 1), slice(1, LAYERS))

    def __init__(self, nc, ctx):
        sb = lambda n, s: ctx.enter_context(nc.sbuf_tensor("mod_" + n, s, F32))
        self.w = sb("w", [C, LAYERS, 6 * C])
        self.cT = sb("cT", [C, LAYERS, B])
        self.sil = sb("sil", [C, LAYERS, B])
        self.sgn, self.mag, self.raw = (sb(n, [C, LAYERS, 2, B]) for n in ("sgn", "mag", "raw"))
        sems = lambda n: [nc.alloc_semaphore(f"mod_{n}{part}") for part in range(2)]
        self.loaded, self.silu_done, self.products, self.step = sems("loaded"), sems("silu"), sems("products"), sems("step")
        self.n_loads = [0, 0]


def modulation_programs(R, M, part):
    layers = M.PARTS[part]
    n = layers.stop - layers.start
    loaded, silu_done, products, step = M.loaded[part], M.silu_done[part], M.products[part], M.step[part]

    def on_pe(pe):
        pe.wait_ge(loaded, 16 * M.n_loads[part])
        pe.wait_ge(silu_done, 1)
        for l in range(n):
            for k in range(6):
                col = (l * 6 + k) * B
                last = pe.matmul(R.ps[:, 0, col:col + B], M.w[:, layers.start + l, k * C:(k + 1) * C],
                                 M.sil[:, layers.start + l, :], start=True, stop=True)
        last.then_inc(products, 1)

    def on_act(act):
        act.wait_ge(M.loaded[0], 16 * M.n_loads[0])
        act.activation(M.sil[:, layers], M.cT[:, layers], ACT.Silu).then_inc(silu_done, 1)

    def on_dve(dve):
        mod, gate = R.mod[:, layers], R.gate[:, layers.start * 2 * B:layers.stop * 2 * B]
        gates, scales = mod[:, :, 2:6:3, :], mod[:, :, 1:5:3, :]
        sgn, mag, raw = M.sgn[:, layers], M.mag[:, layers], M.raw[:, layers]
        flat = lambda x: x.rearrange("p l k b -> p (l k b)")
        dve.wait_ge(products, 1)
        dve.tensor_copy(mod, R.ps[:, 0, 0:n * 6 * B].rearrange("p (l k b) -> p l k b", l=n, k=6)).then_inc(step, 1)
        dve.wait_ge(step, 1)
        dve.tensor_scalar(sgn, gates, 0.0, 2.0, ALU.is_ge, ALU.mult).then_inc(step, 1)
        dve.tensor_copy(raw, gates).then_inc(step, 1)
        dve.wait_ge(step, 3)
        dve.scalar_tensor_tensor(flat(mag), flat(sgn), -1.0, flat(raw), ALU.add, ALU.mult).then_inc(step, 1)
        dve.wait_ge(step, 4)
        dve.tensor_scalar(mag, mag, 0.25, None, ALU.max).then_inc(step, 1)
        dve.wait_ge(step, 5)
        dve.scalar_tensor_tensor(gate, flat(sgn), -1.0, flat(mag), ALU.add, ALU.mult).then_inc(step, 1)
        dve.tensor_scalar(R.scale1[:, layers], scales, 1.0, None, ALU.add).then_inc(step, 1)

    return on_pe, on_act, on_dve


def setup_stage(nc, R, M, dram, parts):
    ones_done = nc.alloc_semaphore("setup_ones_done")
    cast_loaded = nc.alloc_semaphore("setup_cast_loaded")
    centre_done = nc.alloc_semaphore("setup_centre_done")
    loads = [(0, M.w[:, 0, :], dram["L0_wmod"]), (0, M.cT[:], dram["cT"]), (0, R.ident[:], dram["ident"]),
             (0, R.x[:], dram["xT"]), (1, R.blk8[:], dram["blk8"])]
    loads += [(1, M.w[:, l, :], dram[f"L{l}_wmod"]) for l in range(1, LAYERS)]
    M.n_loads = [sum(part == p for part, _d, _s in loads) for p in range(2)]
    programs = [modulation_programs(R, M, part) for part in parts]
    with nc.Block() as block:

        @block.sync
        def _(sp):
            for part, dst, src in loads:
                sp.dma_start(dst, src).then_inc(M.loaded[part], 16)
            for part in parts:
                sp.wait_ge(M.loaded[part], 16 * M.n_loads[part])

        @block.gpsimd
        def _(pool):
            pool.memset(R.centre[:], -1.0 / C).then_inc(ones_done, 1)
            pool.memset(R.h[:, :, 0:4], 0.0).then_inc(ones_done, 1)
            pool.memset(R.ones8[:], 0.0).then_inc(ones_done, 1)
            pool.wait_ge(ones_done, 3)
            for i in range(4):
                pool.memset(R.ones8[:, i, 8 * i:8 * i + 8], 1.0 / C).then_inc(ones_done, 1)
            pool.memset(R.eps[:], LN_EPS).then_inc(ones_done, 1)
            pool.dma_start(R.identb[:], dram["ident"]).then_inc(cast_loaded, 16)
            pool.wait_ge(cast_loaded, 16)

        @block.tensor
        def _(pe):
            for part, (on_pe, _a, _d) in zip(parts, programs):
                if part:
                    pe.wait_ge(M.step[0], 1)
                on_pe(pe)

        @block.scalar
        def _(act):
            for _p, on_act, _d in programs:
                on_act(act)

        @block.vector
        def _(dve):
            dve.wait_ge(ones_done, 3)
            dve.wait_ge(M.loaded[0], 16 * M.n_loads[0])
            dve.tensor_tensor(R.centre[:], R.centre[:], R.ident[:], ALU.add).then_inc(centre_done, 1)
            for _p, _a, on_dve in programs:
                on_dve(dve)


def mod_cols(R, layer, half, b):
    k = (layer * 2 + half) * B + b
    return R.mod[:, layer, 3 * half, b:b + 1], R.scale1[:, layer, half, b:b + 1], R.gate[:, k:k + 1]


def norm_stage(nc, R, layer, half, W=None, pool_program=None):
    S = R.norm_sems
    k = S.calls
    n0 = k * NC
    S.calls += 1
    with ExitStack() as ctx:
        xc = ctx.enter_context(nc.sbuf_tensor(f"ln_xc{n0}", [C, NC, CW], F32))
        sq = ctx.enter_context(nc.sbuf_tensor(f"ln_sq{n0}", [C, NC, CW], F32))
        dev = ctx.enter_context(nc.sbuf_tensor(f"ln_dev{n0}", [C, 2, 128], F32))
        with nc.Block() as block:
            if pool_program:
                block.gpsimd(pool_program)

            @block.sync
            def _(sp):
                for dst, src in W.loads if W else []:
                    sp.dma_start(dst, src).then_inc(W.loaded, 16)

            @block.tensor
            def _(pe):
                for c in range(NC):
                    b, t = chunk(c)
                    pe.matmul(R.ps[:, c, :], R.centre[:], R.x[:, b, t], start=True, stop=True).then_inc(S.mean, 1)
                for c in range(NC):
                    pe.wait_ge(S.squared, n0 + c + 1)
                    for i in range(4):
                        last = pe.matmul(R.ps[32 * c:32 * c + 32, 4, 0:128], R.ones8[:, i, :],
                                         sq[:, c, i * 128:(i + 1) * 128], start=(i == 0), stop=(i == 3))
                last.then_inc(S.var, 1)
                pe.wait_ge(S.step, k + 1)
                pe.wait_ge(S.centred, n0 + NC)
                for c in range(NC):
                    for i in range(4):
                        row = 32 * c + 8 * i
                        last = pe.matmul(R.ps[:, c, i * 128:(i + 1) * 128], R.ident[:, row:row + 1].broadcast_to([128, 128]),
                                         dev[:, 1, :], start=True, stop=True)
                    last.then_inc(S.spread, 1)

            @block.scalar
            def _(act):
                act.activation(dev[0:1, 0, 0:1], R.eps[0:1], ACT.Sqrt).then_inc(S.warm, 1)
                for c in range(NC):
                    act.wait_ge(S.mean, n0 + c + 1)
                    act.activation(sq[:, c, :], R.ps[:, c, :], ACT.Square).then_inc(S.squared, 1)
                act.wait_ge(S.warm, k + 1)
                act.wait_ge(S.var, k + 1)
                act.activation(dev[:, 0, :], R.ps[:, 4, 0:128], ACT.Sqrt, bias=R.eps[:]).then_inc(S.dev, 1)
                for c in range(NC):
                    b, t = chunk(c)
                    shift, scale1, _g = mod_cols(R, layer, half, b)
                    act.wait_ge(S.scaled, n0 + c + 1)
                    act.activation(R.h[:, b, 4 + t.start:4 + t.stop], xc[:, c, :], ACT.Identity, scale=scale1,
                                   bias=shift).then_inc(S.out, 1)

            @block.vector
            def _(dve):
                for c in range(NC):
                    b, t = chunk(c)
                    dve.wait_ge(S.squared, n0 + c + 1)
                    dve.tensor_copy(xc[:, c, :], R.ps[:, c, :]).then_inc(S.centred, 1)
                dve.wait_ge(S.dev, k + 1)
                dve.reciprocal(dev[:, 1, :], dev[:, 0, :]).then_inc(S.step, 1)
                for c in range(NC):
                    dve.wait_ge(S.centred, n0 + c + 1)
                    dve.wait_ge(S.spread, n0 + c + 1)
                    dve.tensor_tensor(xc[:, c, :], xc[:, c, :], R.ps[:, c, :], ALU.mult).then_inc(S.scaled, 1)


def h_chunk(R, c):
    b, t = chunk(c)
    return R.h[:, b, 4 + t.start:4 + t.stop]


def h_block(R, tb):
    b, s = tb // 8, tb % 8
    return R.h[:, b, 4 + s * 128:4 + s * 128 + 128]


def head_row(A, j):
    return (A.rows * j) % 128


def load_rows(A, idx, slot, operand, queue, loaded=None, heads=range(4)):
    D, W, QP, KP, P = A.dim, A.rows, A.first_part, A.first_part + 3 * A.dim, A.parts_dram
    for j in heads:
        r = head_row(A, j)
        f = bass.ds(idx * (4 * D) + j * D, D)
        if operand == 0:
            t = A.q[:, slot, (W * j) // 128, :]
            loads = [(t[r + QP:r + QP + 3 * D, :], P[0, 0:1, f, :].broadcast_to([3, D, T])),
                     (t[r + KP:r + KP + 2 * D, :], P[0, 1:2, f, :].broadcast_to([2, D, T])),
                     (t[r + KP + 2 * D:r + KP + 3 * D, :], P[0, 2, f, :])]
        else:
            t = A.k[:, slot, j, :]
            loads = [(t[r + QP:r + QP + 3 * D, :], P[1, 0:3, f, :]),
                     (t[r + KP:r + KP + 2 * D, :], P[1, 0:2, f, :]),
                     (t[r + KP + 2 * D:r + KP + 3 * D, :], P[1, 0, f, :])]
            if A.mask:
                loads += [(t[r + 3:r + 4, :], A.mask_dram[bass.ds(idx, 1), :])]
        for dst, src in loads:
            queue.dma_start(dst, src).then_inc(loaded or A.ld[slot], 16)


def load_group(A, idx, slot, queue):
    load_rows(A, idx, slot, 0, queue)
    load_rows(A, idx, slot, 1, queue)


def init_operands(A, stage):
    two_ones = float(np.array([0x3F803F80], np.uint32).view(np.float32)[0])

    def program(pool):
        rows = sorted({head_row(A, j) for j in range(4)})
        steps = [(A.q[:].bitcast(F32), 0.0), (A.k[:].bitcast(F32), 0.0)]
        if A.mask:
            steps += [(A.q[r:r + 4].bitcast(F32), two_ones) for r in rows]
        cut = len(steps)
        if A.mask:
            steps += [(A.q[r:r + 3].bitcast(F32), 0.0) for r in rows]
        steps += [(A.k[head_row(A, j):head_row(A, j) + 3, :, j, :].bitcast(F32), two_ones) for j in range(4)]
        steps += [(A.v[:, :, :, :, 8:9], 1.0)]
        assert len(steps) == A.n_inited
        for i in range(cut) if stage == 0 else range(cut, len(steps)):
            if i:
                pool.wait_ge(A.inited, i)
            pool.memset(*steps[i]).then_inc(A.inited, 1)

    return program


def project_stage(nc, R, W, A, layer, modulation=None):
    pre = f"pj{layer}"
    bias = A.mask
    with ExitStack() as ctx:
        sb = lambda n, s, d=F32: ctx.enter_context(nc.sbuf_tensor(pre + n, s, d))
        w, bqk, bv = W.w, W.bqk, W.bv
        rest = sb("rest", [C, 4, CW])
        parts, stored = A.parts, A.stored
        mrow = sb("mrow", [1, B, T], BF16)
        sem = lambda n: nc.alloc_semaphore(pre + n)
        scaled, qk, part1, rested, part2, part3, vp, v_done, mask_set, mask_stored = (
            sem(n) for n in ("scaled", "qk", "part1", "rested", "part2", "part3", "vp", "v", "mask_set",
                             "mask_stored"))
        heads = A.heads_of_group
        TILES = 2 * NC
        n_masks = A.groups // B if bias else 0
        with nc.Block() as block:

            @block.sync
            def _(sp):
                if bias:
                    sp.wait_ge(mask_set, 1)
                    for g in range(n_masks):
                        sp.dma_start(A.mask_dram[g::A.groups // B, :].unsqueeze(0), mrow[:]).then_inc(mask_stored, 16)
                for c in range(NC):
                    b, t = chunk(c)
                    sp.wait_ge(part3, 2 * (c + 1))
                    for o in range(2):
                        sp.dma_start(A.parts_dram[o, :, b * C:(b + 1) * C, t].rearrange("s f t -> f s t"),
                                     parts[:, o, :, b, t]).then_inc(stored[b], 16)
                    if c == NC // B - 1:
                        sp.wait_ge(A.inited, A.n_inited)
                        sp.wait_ge(stored[0], 16 * 2 * NC // B)
                        load_rows(A, 0, 0, 0, sp)
                        load_rows(A, 0, 0, 1, sp, heads=range(2))

            @block.gpsimd
            def _(pool):
                init_operands(A, 1)(pool)
                pool.wait_ge(A.inited, A.n_inited)
                pool.wait_ge(stored[0], 16 * 2 * NC // B)
                if bias:
                    pool.wait_ge(mask_stored, 16 * n_masks)
                load_rows(A, 0, 0, 1, pool, A.first_k, range(2, 4))

            @block.tensor
            def _(pe):
                def values(g):
                    for i in range(4):
                        last = pe.matmul(R.ps[:, 4 + g, i * C:(i + 1) * C], h_block(R, 4 * g + i), w[:, 2, :],
                                         start=True, stop=True)
                    last.then_inc(vp, 1)

                pe.wait_ge(W.loaded, W.count)
                pe.wait_ge(scaled, A.n_scaled)
                for c in range(NC):
                    for o in range(2):
                        n = 2 * c + o
                        if n >= 4:
                            pe.wait_ge(rested, n - 3)
                        pe.matmul(R.ps[:, n % 4, :], w[:, o, :], h_chunk(R, c), start=True, stop=True).then_inc(qk, 1)
                    values(c)
                if modulation:
                    pe.wait_ge(rested, TILES)
                    modulation[0](pe)

            @block.scalar
            def _(act):
                bias_of = lambda o: bqk[:, o:o + 1]
                if bias:
                    act.wait_ge(scaled, A.n_scaled)
                for n in range(TILES + 1):
                    if n < TILES:
                        b, t = chunk(n // 2)
                        act.wait_ge(qk, n + 1)
                        dst = parts[:, n % 2, 0, b, t]
                        if bias:
                            act.activation(dst, R.ps[:, n % 4, :], ACT.Identity, bias=bias_of(n % 2)).then_inc(part1, 1)
                        else:
                            act.activation(dst, R.ps[:, n % 4, :], ACT.Copy).then_inc(part1, 1)
                    if n:
                        m = n - 1
                        b, t = chunk(m // 2)
                        act.wait_ge(rested, m + 1)
                        act.activation(parts[:, m % 2, 1, b, t], rest[:, m % 4, :], ACT.Copy).then_inc(part2, 1)
                if layer == 0:
                    lambda_programs(W)[0](act)
                if modulation:
                    modulation[1](act)

            @block.vector
            def _(dve):
                if bias:
                    dve.tensor_scalar(mrow[:], R.h[0:1, :, 4:4 + T], 0.0, NEG, ALU.is_equal, ALU.mult)\
                       .then_inc(mask_set, 1)
                dve.wait_ge(W.loaded, W.count)
                dve.tensor_scalar(w[:, 0, :], w[:, 0, :], A.scale, None, ALU.mult).then_inc(scaled, 1)
                if bias:
                    dve.tensor_scalar(bqk[:, 0:1], bqk[:, 0:1], A.scale, None, ALU.mult).then_inc(scaled, 1)
                    dve.wait_ge(scaled, A.n_scaled)
                for n in range(TILES + 1):
                    if n < TILES:
                        b, t = chunk(n // 2)
                        dve.wait_ge(part1, n + 1)
                        if n >= 4:
                            dve.wait_ge(part3, n - 3)
                        first = parts[:, n % 2, 0, b, t]
                        if bias:
                            dve.scalar_tensor_tensor(rest[:, n % 4, :], R.ps[:, n % 4, :], bqk[:, n % 2:n % 2 + 1], first,
                                                     ALU.add, ALU.subtract).then_inc(rested, 1)
                        else:
                            dve.tensor_tensor(rest[:, n % 4, :], R.ps[:, n % 4, :], first, ALU.subtract).then_inc(rested, 1)
                    if n:
                        m = n - 1
                        b, t = chunk(m // 2)
                        dve.wait_ge(part2, m + 1)
                        dve.tensor_tensor(parts[:, m % 2, 2, b, t], rest[:, m % 4, :], parts[:, m % 2, 1, b, t],
                                          ALU.subtract).then_inc(part3, 1)
                for g in range(TB // 4):
                    dve.wait_ge(vp, g + 1)
                    b, s = g // 2, (g % 2) * 4
                    for i in range(4):
                        src = R.ps[:, 4 + g, i * C:(i + 1) * C].rearrange("p (g h c) -> p g h c", h=heads, c=8)
                        dst = A.v[:, b * (A.groups // B):(b + 1) * (A.groups // B), s + i, :, 0:8]
                        if bias:
                            dve.tensor_tensor(dst, src, bv[:].rearrange("p (g h c) -> p g h c", h=heads, c=8),
                                              ALU.add).then_inc(v_done, 1)
                        else:
                            dve.tensor_copy(dst, src).then_inc(v_done, 1)
                if layer == 0:
                    lambda_programs(W)[1](dve)
                if modulation:
                    modulation[2](dve)



def softmax_stage(nc, R, W, A):
    pre, RT, ROWS, D, NG = A.name, A.row_tiles, A.rows, A.dim, A.groups
    HG = A.heads_of_group
    UNITS = 2 * NG
    with ExitStack() as ctx:
        sb = lambda n, s, d=F32: ctx.enter_context(nc.sbuf_tensor(pre + n, s, d))
        sem = lambda n: nc.alloc_semaphore(pre + n)
        q, k, ld = A.q, A.k, A.ld
        qm = sb("qm", [128, 2, RT, CW], BF16)
        vst = sb("vst", [128, 2, 8, HG, 32])
        p = sb("p", [128, 2, 4, CW])
        o = sb("o", [128, 2, CW])
        rec = sb("rec", [128, CW])
        nm = sb("nm", [128, 2, 4, 4])
        m1 = sb("m1", [128, 4, 4])
        m2 = sb("m2", [128, 4, 4])
        mt = sb("mt", [128, 4, 4, ROWS], BF16)
        zero = sb("zero", [128, 8, 9])
        den_sel, den_spread = W.den_sel, W.den_spread
        p1_full, p1_free = sem("p1_full"), sem("p1_free")
        mt_ready, mt_turned, qm_ready = sem("mt_ready"), sem("mt_turned"), sem("qm_ready")
        p2_full, exp_done, pv_done, pv_out = sem("p2_full"), sem("exp_done"), sem("pv_done"), sem("pv_out")
        den_ready, rec_done, rec_spread, on_done = sem("den_ready"), sem("rec_done"), sem("rec_spread"), sem("on_done")
        v_ready, pool_step = sem("v_ready"), sem("pool_step")
        MISC = 7
        misc_b = R.ps[:, MISC, :].bitcast(BF16).rearrange("p (r t) -> p r t", r=2)[:, 0:RT, :]
        n_loads = 4 * (6 + (1 if A.mask else 0))

        def score_bank(j, last_unit):
            return (4, 5, 0, 1)[j] if last_unit else 4 + j % 2

        with nc.Block() as block:

            @block.sync
            def _(sp):
                load_group(A, 1, 1, sp)
                sp.wait_ge(A.stored[1], 16 * 2 * NC // B)
                with sp.Fori(1, NG // 2) as kk:
                    sp.wait_ge(exp_done, kk * 128 - 64)
                    load_group(A, kk * 2, 0, sp)
                    sp.wait_ge(exp_done, kk * 128)
                    load_group(A, kk * 2 + 1, 1, sp)

            @block.gpsimd
            def _(pool):
                pool.memset(vst[:], 0.0).then_inc(pool_step, 1)
                pool.memset(mt[:], 0.0).then_inc(pool_step, 1)
                pool.memset(zero[:], 0.0).then_inc(pool_step, 1)
                pool.wait_ge(pool_step, 3)

                def stage_v(idx, slot):
                    pool.tensor_tensor(vst[:, slot, :, :, 16 * slot:16 * slot + 9], A.v[:, bass.ds(idx, 1)].squeeze(1),
                                       zero[:].unsqueeze(2).broadcast_to([128, 8, HG, 9]), ALU.add).then_inc(v_ready, 1)

                def split(kk, w):
                    u = kk * 4 + w
                    pool.wait_ge(p1_free, u * 16 + 16)
                    if not (isinstance(u, int) and u == 0):
                        pool.wait_ge(mt_turned, u)
                    m = nm[:, w % 2]
                    ops = ((mt[:, :, :, 0], m), (m1[:], m, mt[:, :, :, 0]), (mt[:, :, :, 1], m1[:]),
                           (m2[:], m1[:], mt[:, :, :, 1]), (mt[:, :, :, 2], m2[:]))
                    for i, op in enumerate(ops):
                        if len(op) == 2:
                            ins = pool.tensor_tensor(*op, zero[:, 0:4, 0:4], ALU.add)
                        else:
                            ins = pool.tensor_tensor(*op, ALU.subtract)
                        if i == 4:
                            ins.then_inc(mt_ready, 1)
                        else:
                            ins.then_inc(pool_step, 1)
                            pool.wait_ge(pool_step, u * 4 + (4 + i))

                stage_v(0, 0)
                split(0, 0)

                def body(kk, last):
                    for w in range(4):
                        if w % 2 and not (last and w == 3):
                            e = (w + 1) // 2
                            idx = kk * 2 + e
                            if not (isinstance(kk, int) and kk == 0 and e == 1):
                                pool.wait_ge(pv_done, (idx - 1) * 16)
                            stage_v(idx, e % 2)
                        if not (last and w == 3):
                            split(kk, w + 1)

                if NG > 2:
                    body(0, False)
                if NG // 2 > 2:
                    with pool.Fori(1, NG // 2 - 1) as kk:
                        body(kk, False)
                body(NG // 2 - 1, True)

            @block.tensor
            def _(pe):
                def p1_slot(kk, w, i):
                    tb, j = i // 4, i % 4
                    u, g_slot = kk * 4 + w, (w // 2) % 2
                    if i == 0 and w % 2 == 0:
                        not_counted = 0 if g_slot else 16 * A.n_k_loads
                        pe.wait_ge(ld[g_slot], kk * (16 * n_loads) + ((w // 4 + 1) * 16 * n_loads - not_counted))
                    if not (isinstance(u, int) and u == 0 and i < 2):
                        pe.wait_ge(p1_free, u * 16 + (i - 1))
                    t0 = (w % 2) * CW + tb * 128
                    for hf in range(2):
                        last = pe.matmul(R.ps[:, 2 * (i % 2) + hf, :], q[:, g_slot, (ROWS * j) // 128, t0:t0 + 128],
                                         k[:, g_slot, j, hf * CW:(hf + 1) * CW], start=True, stop=True)
                    last.then_inc(p1_full, 1)

                def turn(kk, w):
                    u = kk * 4 + w
                    pe.wait_ge(mt_ready, u + 1)
                    if w in (1, 2) and not (isinstance(kk, int) and kk == 0):
                        pe.wait_ge(on_done, kk * 2 + (w - 2))
                    for tb in range(4):
                        for r in range(RT):
                            last = pe.transpose(misc_b[:, r, tb * 128:(tb + 1) * 128],
                                                mt[:].rearrange("p b h w -> p b (h w)")[:, tb, r * 128:(r + 1) * 128],
                                                R.identb[:])
                    last.then_inc(mt_turned, 1)

                def score(kk, w, s, j, last_unit):
                    u = kk * 4 + w
                    if last_unit and j >= 2 and s == 0:
                        pe.wait_ge(p1_free, u * 16 + 16)
                    elif last_unit and s:
                        pe.wait_ge(exp_done, u * 32 + (4 * s + j - 3))
                    elif not (isinstance(u, int) and u == 0 and s == 0 and j < 2):
                        pe.wait_ge(exp_done, u * 32 + (4 * s + j - 1))
                    pe.matmul(R.ps[:, score_bank(j, last_unit), :], k[:, (w // 2) % 2, j, s * 128:(s + 1) * 128],
                              qm[:, w % 2, (ROWS * j) // 128, :], start=True, stop=True).then_inc(p2_full, 1)

                def pv(kk, w, s):
                    u = kk * 4 + w
                    if s == 0:
                        if not (isinstance(u, int) and u == 0):
                            pe.wait_ge(pv_out, u)
                        if w % 2 == 0:
                            pe.wait_ge(v_ready, kk * 2 + (w // 2 + 1))
                    pe.wait_ge(exp_done, u * 32 + (4 * s + 4))
                    for j in range(4):
                        last = pe.matmul(R.ps[32 * j:32 * j + 32, 6, :], vst[:, (w // 2) % 2, s, j * HG // 4, :],
                                         p[:, s % 2, j, :], start=(s == 0), stop=(s == 7))
                    last.then_inc(pv_done, 1)

                def den(kk):
                    pe.wait_ge(pv_out, kk * 4)
                    for w in range(2):
                        last = pe.matmul(R.ps[64 * w:64 * w + 64, MISC, :], den_sel[:], o[:, w, :], start=True, stop=True)
                    last.then_inc(den_ready, 1)

                def spread(kk, w):
                    pe.wait_ge(rec_done, kk * 4)
                    pe.matmul(R.ps[:, MISC, :], den_spread[:, w, :], rec[:], start=True, stop=True).then_inc(rec_spread, 1)

                def body(kk, last, first=False):
                    for w in range(4):
                        pe.wait_ge(qm_ready, kk * 4 + (w + 1))
                        end = last and w == 3
                        for s in range(8):
                            def ahead(i):
                                n = 4 + 2 * s + i
                                wv = w + 1 + n // 16
                                if not (last and wv > 3):
                                    p1_slot(kk, wv, n % 16)
                            score(kk, w, s, 0, end)
                            score(kk, w, s, 1, end)
                            ahead(0)
                            ahead(1)
                            score(kk, w, s, 2, end)
                            score(kk, w, s, 3, end)
                            if s > 0:
                                pv(kk, w, s - 1)
                            elif not (first and w == 0):
                                pv(kk, w - 1, 7)
                            if s == 1 and w == 0 and not first:
                                den(kk)
                            if w < 2 and s == (4 if w == 0 else 2) and not first:
                                spread(kk, w)
                            if s == 6 and not (last and w == 3):
                                turn(kk, w + 1)
                    if last:
                        pv(kk, 3, 7)
                        den(kk + 1)
                        for w in range(2):
                            if w:
                                pe.wait_ge(on_done, kk * 2 + w)
                            spread(kk + 1, w)

                pe.wait_ge(W.loaded, W.count)
                pe.wait_ge(A.first_k, 16 * A.n_k_loads)
                for i in range(16):
                    p1_slot(0, 0, i)
                turn(0, 0)
                for i in range(4):
                    p1_slot(0, 1, i)
                if NG > 2:
                    body(0, False, True)
                if NG // 2 > 2:
                    with pe.Fori(1, NG // 2 - 1) as kk:
                        body(kk, False)
                body(NG // 2 - 1, True)

            @block.scalar
            def _(act):
                def body(kk, first=False, last=False):
                    for w in range(4):
                        u = kk * 4 + w
                        for s in range(8):
                            if not (first and w == 0 and s < 2):
                                act.wait_ge(pv_done, u * 8 + (s - 1))
                            for j in range(4):
                                act.wait_ge(p2_full, u * 32 + (4 * s + j + 1))
                                act.activation(p[:, s % 2, j, :], R.ps[:, score_bank(j, last and w == 3), :], ACT.Exp)\
                                   .then_inc(exp_done, 1)
                                if s == 1 and j == 1 and w in (1, 2):
                                    take(kk, w - 1, first)

                def take(kk, w, first):
                    act.wait_ge(pv_done, kk * 32 + (w * 8 + 8))
                    if not first:
                        act.wait_ge(on_done, kk * 2 + (w - 1))
                    act.activation(o[:, w, :], R.ps[:, 6, :], ACT.Copy).then_inc(pv_out, 1)

                body(0, first=True)
                if NG // 2 > 2:
                    with act.Fori(1, NG // 2 - 1) as kk:
                        body(kk)
                body(NG // 2 - 1, last=True)

            @block.vector
            def _(dve):
                def reduce(kk, w, i):
                    u = kk * 4 + w
                    dve.wait_ge(p1_full, u * 16 + (i + 1))
                    dve.tensor_reduce(nm[:, w % 2, i // 4, i % 4:i % 4 + 1], R.ps[:, 2 * (i % 2):2 * (i % 2) + 2, :],
                                      mybir.AxisListType.XY, ALU.max, negate=True).then_inc(p1_free, 1)

                def merge(kk, w):
                    u = kk * 4 + w
                    dve.wait_ge(mt_turned, u + 1)
                    if not (isinstance(u, int) and u < 2):
                        dve.wait_ge(exp_done, u * 32 - 32)
                    t0 = (w % 2) * CW
                    dve.tensor_tensor(qm[:, w % 2], q[:, (w // 2) % 2, :, t0:t0 + CW], misc_b, ALU.add)\
                       .then_inc(qm_ready, 1)

                def take(kk, w):
                    dve.wait_ge(pv_done, kk * 32 + (w * 8 + 8))
                    dve.wait_ge(pv_out, kk * 4 + (w - 1))
                    dve.tensor_tensor(o[:, w - 2, :], o[:, w - 2, :], R.ps[:, 6, :], ALU.add).then_inc(pv_out, 1)

                def invert(kk, part):
                    dve.wait_ge(den_ready, kk)
                    cols = slice(part * 128, part * 128 + 128)
                    dve.reciprocal(rec[:, cols], R.ps[:, MISC, cols]).then_inc(rec_done, 1)

                def divide(kk, w):
                    dve.wait_ge(rec_spread, (kk - 1) * 2 + (w + 1))
                    t0 = w * CW
                    dve.tensor_tensor(A.on[:, bass.ds(kk - 1, 1), t0:t0 + CW], o[:, w, :].unsqueeze(1),
                                      R.ps[:, MISC, :].unsqueeze(1), ALU.mult).then_inc(on_done, 1)

                def body(kk, last, first=False):
                    for w in range(4):
                        for s in range(8):
                            for i in range(2):
                                if w == 0 and s in (2, 3) and not first:
                                    invert(kk, 2 * (s - 2) + i)
                                n = 4 + 2 * s + i
                                wv = w + 1 + n // 16
                                if not (last and wv > 3):
                                    reduce(kk, wv, n % 16)
                                if s == 7 and i == 0 and not (last and w == 3):
                                    merge(kk, w + 1)
                                if s == 1 and i == 0 and w == 0 and not first:
                                    take(kk - 1, 3)
                                if s == 1 and i == 0 and w == 3:
                                    take(kk, 2)
                            if w < 2 and s == (4 if w == 0 else 2) and not first:
                                divide(kk, w)
                    if last:
                        take(kk, 3)
                        for part in range(4):
                            invert(kk + 1, part)
                        for w in range(2):
                            divide(kk + 1, w)

                for i in range(16):
                    reduce(0, 0, i)
                merge(0, 0)
                for i in range(4):
                    reduce(0, 1, i)
                if NG > 2:
                    body(0, False, True)
                if NG // 2 > 2:
                    with dve.Fori(1, NG // 2 - 1) as kk:
                        body(kk, False)
                body(NG // 2 - 1, True)


def lambda_programs(W):
    lam, cols, prod, dots, pick, step, exped = W.lam, W.cols, W.prod, W.dots, W.pick, W.lam_step, W.exped

    def on_act(act):
        act.wait_ge(step, 2)
        act.activation(dots[:], dots[:], ACT.Exp).then_inc(exped, 1)

    def on_dve(dve):
        dve.tensor_tensor(prod[:], lam[:, 0:3:2, :], lam[:, 1:4:2, :], ALU.mult).then_inc(step, 1)
        dve.wait_ge(step, 1)
        dve.tensor_reduce(dots[:], prod[:], X_AXIS, ALU.add).then_inc(step, 1)
        dve.wait_ge(exped, 1)
        dve.tensor_tensor(cols[:, 3:4], dots[:, 1:2], dots[:, 0:1], ALU.subtract).then_inc(step, 1)
        dve.wait_ge(step, 3)
        dve.tensor_scalar(cols[:, 4:5], cols[:, 3:4], LAMBDA_INIT, None, ALU.subtract).then_inc(step, 1)
        dve.wait_ge(step, 4)
        dve.tensor_tensor(cols[:, 5:6], cols[:, 4:5], cols[:, 1:2], ALU.mult).then_inc(step, 1)
        dve.wait_ge(step, 5)
        dve.tensor_tensor(cols[:, 6:7], cols[:, 5:6], cols[:, 0:1], ALU.add).then_inc(step, 1)
        dve.tensor_scalar(cols[:, 7:8], cols[:, 2:3], 1.0 - LAMBDA_INIT, None, ALU.mult).then_inc(step, 1)
        dve.wait_ge(step, 7)
        dve.tensor_scalar(pick[:], pick[:], cols[:, 6:7], None, ALU.mult).then_inc(step, 1)

    return on_act, on_dve


def diff_out_stage(nc, R, W, A):
    PAIRS = A.groups // 2 // B
    with ExitStack() as ctx:
        sb = lambda n, s, d=F32: ctx.enter_context(nc.sbuf_tensor("do_" + n, s, d))
        sem = lambda n: nc.alloc_semaphore("do_" + n)
        cols, pick, wo = W.cols, W.pick, W.wo
        a = sb("a", [C, NC, CW])
        sq = sb("sq", [C, NC, CW])
        dev = sb("dev", [128, 2, CW])
        got, copied, squared, ms, deviated, inverted, spread, normed, proj, done = (
            sem(n) for n in ("got", "copied", "squared", "ms", "dev", "inverted", "spread", "normed", "proj", "done"))
        with nc.Block() as block:

            @block.tensor
            def _(pe):
                for c in range(NC):
                    b, t = chunk(c)
                    for g in range(PAIRS):
                        last = pe.matmul(R.ps[:, c, :], pick[:, g, :], A.on[:, b * PAIRS + g, t], start=(g == 0),
                                         stop=(g == PAIRS - 1))
                    last.then_inc(got, 1)
                for c in range(NC):
                    pe.wait_ge(squared, c + 1)
                    last = pe.matmul(R.ps[32 * c:32 * c + 32, 4, :], W.head_sum[:], sq[:, c, :], start=True, stop=True)
                last.then_inc(ms, 1)
                pe.wait_ge(inverted, 1)
                pe.wait_ge(copied, NC)
                for c in range(NC):
                    pe.matmul(R.ps[:, c, :], W.head_spread[:, c, :], dev[:, 1, :], start=True, stop=True).then_inc(spread, 1)
                for c in range(NC):
                    pe.wait_ge(normed, c + 1)
                    pe.matmul(R.ps[:, 4 + c, :], wo[:], a[:, c, :], start=True, stop=True).then_inc(proj, 1)

            @block.scalar
            def _(act):
                for c in range(NC):
                    act.wait_ge(got, c + 1)
                    act.activation(sq[:, c, :], R.ps[:, c, :], ACT.Square, scale=8 ** -0.5).then_inc(squared, 1)
                act.wait_ge(ms, 1)
                act.activation(dev[:, 0, :], R.ps[:, 4, :], ACT.Sqrt, bias=R.eps[:]).then_inc(deviated, 1)

            @block.vector
            def _(dve):
                for c in range(NC):
                    dve.wait_ge(squared, c + 1)
                    dve.tensor_scalar(a[:, c, :], R.ps[:, c, :], cols[:, 7:8], None, ALU.mult).then_inc(copied, 1)
                dve.wait_ge(deviated, 1)
                dve.reciprocal(dev[:, 1, :], dev[:, 0, :]).then_inc(inverted, 1)
                for c in range(NC):
                    dve.wait_ge(copied, c + 1)
                    dve.wait_ge(spread, c + 1)
                    dve.tensor_tensor(a[:, c, :], a[:, c, :], R.ps[:, c, :], ALU.mult).then_inc(normed, 1)
                for c in range(NC):
                    b, t = chunk(c)
                    dve.wait_ge(proj, c + 1)
                    dve.scalar_tensor_tensor(R.x[:, b, t], R.ps[:, 4 + c, :], mod_cols(R, 0, 0, b)[2], R.x[:, b, t],
                                             ALU.mult, ALU.add).then_inc(done, 1)


def out_stage(nc, R, W, layer, half, name, rhs, parts, w, bias=None):
    with ExitStack() as ctx:
        tmp = ctx.enter_context(nc.sbuf_tensor(name + "tmp", [C, NC, CW], F32))
        proj, biased, done = (nc.alloc_semaphore(name + n) for n in ("proj", "biased", "done"))
        with nc.Block() as block:

            @block.tensor
            def _(pe):
                pe.wait_ge(W.loaded, W.count)
                for c in range(NC):
                    for i in range(parts):
                        last = pe.matmul(R.ps[:, c, :], w[:, i, :], rhs(i, c), start=(i == 0), stop=(i == parts - 1))
                    last.then_inc(proj, 1)

            @block.vector
            def _(dve):
                dve.wait_ge(W.loaded, W.count)
                for c in range(NC):
                    b, t = chunk(c)
                    gate = mod_cols(R, layer, half, b)[2]
                    dve.wait_ge(proj, c + 1)
                    src = R.ps[:, c, :]
                    if bias is not None:
                        dve.tensor_scalar(tmp[:, c, :], src, bias[:], None, ALU.add).then_inc(biased, 1)
                        dve.wait_ge(biased, c + 1)
                        src = tmp[:, c, :]
                    dve.scalar_tensor_tensor(R.x[:, b, t], src, gate, R.x[:, b, t], ALU.mult, ALU.add).then_inc(done, 1)


def lora_stage(nc, R, W, layer):
    pre = f"ff{layer}"
    with ExitStack() as ctx:
        sb = lambda n, s, d=F32: ctx.enter_context(nc.sbuf_tensor(pre + n, s, d))
        sem = lambda n: nc.alloc_semaphore(pre + n)
        w1, w2, b1, b2, scale, eye8 = W.w1, W.w2, W.b1, W.b2, W.scale, W.eye8
        w1e = sb("w1e", [C, B, HID])
        w2e = sb("w2e", [C, B, HB, C])
        even = sb("even", [8, B, C])
        odd = sb("odd", [8, B, C])
        bd = sb("bd", [8, B, 8, C])
        hid = sb("hid", [C, 2, HB, CW])
        tmp = sb("tmp", [C, NC, CW])
        turned, copied, spread, outer, eff, up, act_done, down, biased, done = (
            sem(n) for n in ("turned", "copied", "spread", "outer", "eff", "up", "act", "down", "biased", "done"))
        with nc.Block() as block:

            @block.tensor
            def _(pe):
                for b in range(B):
                    for i in range(2):
                        lt = R.h[:, b, 5 + i:5 + i + 15:2]
                        last = pe.transpose(R.ps[0:8, b, i * C:(i + 1) * C], lt, R.ident[:])
                last.then_inc(turned, 1)
                for b in range(B):
                    pe.wait_ge(spread, b + 1)
                    pe.matmul(R.ps[:, 2 + 2 * b, :], odd[:, b, :], bd[:, b, 0:4, :], start=True, stop=True).then_inc(outer, 1)
                    for r in range(HB):
                        last = pe.matmul(R.ps[:, 3 + 2 * b, r * C:(r + 1) * C], odd[:, b, :],
                                         bd[:, b, 4:8, :].rearrange("p i (c r) -> p r i c", r=4)[:, r], start=True, stop=True)
                    last.then_inc(outer, 1)

                def ups(c):
                    for hb in range(HB):
                        n = c * HB + hb
                        if n >= 4:
                            pe.wait_ge(act_done, n - 3)
                        pe.matmul(R.ps[:, hb, :], w1e[:, c // 2, hb * C:(hb + 1) * C], h_chunk(R, c),
                                  start=True, stop=True).then_inc(up, 1)

                def downs(c):
                    pe.wait_ge(act_done, (c + 1) * HB)
                    for hb in range(HB):
                        last = pe.matmul(R.ps[:, 4 + c, :], w2e[:, c // 2, hb, :], hid[:, c % 2, hb, :],
                                         start=(hb == 0), stop=(hb == HB - 1))
                    last.then_inc(down, 1)

                for c in range(NC):
                    pe.wait_ge(eff, 2 * (c // 2) + 2)
                    ups(c)
                    if c:
                        pe.wait_ge(eff, 2 * B)
                        downs(c - 1)
                downs(NC - 1)

            @block.scalar
            def _(act):
                act.wait_ge(W.loaded, W.count)
                for c in range(NC):
                    for hb in range(HB):
                        act.wait_ge(up, c * HB + hb + 1)
                        if c >= 2:
                            act.wait_ge(down, c - 1)
                        act.activation(hid[:, c % 2, hb, :], R.ps[:, hb, :], ACT.Gelu, bias=b1[:, hb:hb + 1])\
                           .then_inc(act_done, 1)

            @block.vector
            def _(dve):
                dve.wait_ge(W.loaded, W.count)
                dve.wait_ge(turned, 1)
                dve.tensor_copy(even[:], R.ps[0:8, 0:B, 0:C]).then_inc(copied, 1)
                dve.tensor_copy(odd[:], R.ps[0:8, 0:B, C:2 * C]).then_inc(copied, 1)
                dve.wait_ge(copied, 2)
                for b in range(B):
                    dve.tensor_tensor(bd[:, b], even[:, b, :].unsqueeze(1).broadcast_to([8, 8, C]),
                                      eye8[:].unsqueeze(2).broadcast_to([8, 8, C]), ALU.mult).then_inc(spread, 1)
                for b in range(B):
                    for i, (w, we) in enumerate(((w1[:], w1e[:, b]), (w2[:], w2e[:, b]))):
                        dve.wait_ge(outer, 2 * b + i + 1)
                        if i:
                            w, we = w.rearrange("p r o -> p (r o)"), we.rearrange("p r o -> p (r o)")
                        dve.scalar_tensor_tensor(we, R.ps[:, 2 + 2 * b + i, :], scale[:], w, ALU.mult, ALU.add)\
                           .then_inc(eff, 1)
                for c in range(NC):
                    b, t = chunk(c)
                    dve.wait_ge(down, c + 1)
                    dve.tensor_scalar(tmp[:, c, :], R.ps[:, 4 + c, :], b2[:], None, ALU.add).then_inc(biased, 1)
                    dve.wait_ge(biased, c + 1)
                    dve.scalar_tensor_tensor(R.x[:, b, t], tmp[:, c, :], mod_cols(R, layer, 1, b)[2], R.x[:, b, t],
                                             ALU.mult, ALU.add).then_inc(done, 1)


def mix_stage(nc, R, W):
    with ExitStack() as ctx:
        sb = lambda n, s, d=F32: ctx.enter_context(nc.sbuf_tensor("mx_" + n, s, d))
        sem = lambda n: nc.alloc_semaphore("mx_" + n)
        w, mu = W.w, W.mu
        own = sb("own", [C, 2, NC, CW])
        mixed = sb("mixed", [C, 2, NC, CW])
        r = sb("r", [C, NC, CW])
        k = sb("k", [C, NC, CW])
        k2 = sb("k2", [C, NC, CW])
        inv, part, mix, prod, sig, relu, sqd, vprod, step, done = (
            sem(n) for n in ("inv", "part", "mix", "prod", "sig", "relu", "sqd", "vprod", "step", "done"))
        with nc.Block() as block:

            @block.tensor
            def _(pe):
                pe.wait_ge(W.loaded, W.count)
                for c in range(NC):
                    for i in range(2):
                        pe.wait_ge(mix, 2 * c + i + 1)
                        pe.matmul(R.ps[:, 2 * (c % 2) + i, :], w[:, i, :], mixed[:, i, c, :], start=True, stop=True)\
                          .then_inc(prod, 1)
                    if c == 1:
                        pe.wait_ge(sig, 2)
                        pe.wait_ge(relu, 2)
                for c in range(NC):
                    pe.wait_ge(sqd, c + 1)
                    pe.matmul(R.ps[:, 4 + c, :], w[:, 2, :], k2[:, c, :], start=True, stop=True).then_inc(vprod, 1)

            @block.scalar
            def _(act):
                for c in range(NC):
                    act.wait_ge(prod, 2 * c + 1)
                    act.activation(r[:, c, :], R.ps[:, 2 * (c % 2), :], ACT.Sigmoid).then_inc(sig, 1)
                    act.wait_ge(prod, 2 * c + 2)
                    act.activation(k[:, c, :], R.ps[:, 2 * (c % 2) + 1, :], ACT.Relu).then_inc(relu, 1)

            @block.vector
            def _(dve):
                dve.wait_ge(W.loaded, W.count)
                dve.tensor_scalar(mu[:, 2:4], mu[:, 0:2], -1.0, 1.0, ALU.mult, ALU.add).then_inc(inv, 1)
                dve.wait_ge(inv, 1)
                for c in range(NC):
                    b, t = chunk(c)
                    before = R.h[:, b, 3 + t.start:3 + t.stop]
                    for i in range(2):
                        dve.tensor_scalar(own[:, i, c, :], h_chunk(R, c), mu[:, i:i + 1], None, ALU.mult).then_inc(part, 1)
                        dve.wait_ge(part, 2 * c + i + 1)
                        dve.scalar_tensor_tensor(mixed[:, i, c, :], before, mu[:, 2 + i:3 + i], own[:, i, c, :],
                                                 ALU.mult, ALU.add).then_inc(mix, 1)
                for c in range(NC):
                    dve.wait_ge(relu, c + 1)
                    dve.tensor_tensor(k2[:, c, :], k[:, c, :], k[:, c, :], ALU.mult).then_inc(sqd, 1)
                for c in range(NC):
                    b, t = chunk(c)
                    dve.wait_ge(vprod, c + 1)
                    dve.wait_ge(sqd, c + 1)
                    dve.scalar_tensor_tensor(k[:, c, :], R.ps[:, 4 + c, :], mod_cols(R, 1, 1, b)[2], r[:, c, :],
                                             ALU.mult, ALU.mult).then_inc(step, 1)
                    dve.wait_ge(step, c + 1)
                    dve.tensor_tensor(R.x[:, b, t], R.x[:, b, t], k[:, c, :], ALU.add).then_inc(done, 1)


def latent_stage(nc, R, W, lat):
    with ExitStack() as ctx:
        w = W.down
        prod, done = (nc.alloc_semaphore("lt_" + n) for n in ("prod", "done"))
        with nc.Block() as block:

            @block.tensor
            def _(pe):
                pe.wait_ge(W.loaded, W.count)
                for c in range(NC):
                    pe.matmul(R.ps[:, c, :], w[:], h_chunk(R, c), start=True, stop=True).then_inc(prod, 1)

            @block.scalar
            def _(act):
                for c in range(NC):
                    b, t = chunk(c)
                    act.wait_ge(prod, c + 1)
                    act.activation(lat[:, b, t], R.ps[:, c, :], ACT.Copy).then_inc(done, 1)


def causal_stage(nc, R, W, dram, lat, y):
    pre = "ca"
    with ExitStack() as ctx:
        sb = lambda n, s, d=F32: ctx.enter_context(nc.sbuf_tensor(pre + n, s, d))
        sem = lambda n: nc.alloc_semaphore(pre + n)
        w, q, k = W.qkv, W.q, W.k
        v = sb("v", [128, B, 8, C])
        p = sb("p", [128, 2, 2, T])
        pT = sb("pT", [128, 2, 2, 8, 128])
        nm = sb("nm", [128, 4])
        rs = sb("rs", [128, B, 8, 2])
        rinv = sb("rinv", [128, B, 8, 2])
        rrow = sb("rrow", [128, 2, CW])
        late = W.late
        w_loaded = sem("w_loaded")
        pj, pj_a, pj_d = sem("pj"), sem("pj_a"), sem("pj_d")
        s_full, max_done, exp_done = sem("s_full"), sem("max_done"), sem("exp_done")
        t_full, t_a, t_d = sem("t_full"), sem("t_a"), sem("t_d")
        pv_done, inv_done, y_done = sem("pv_done"), sem("inv_done"), sem("y_done")
        STEPS = HEADS // 2
        PJ = 10
        items = [(b, tb) for b in range(B) for tb in (0, 7, 1, 6, 2, 5, 3, 4)]
        I = len(items)
        groups, of_item = [], {}

        def events():
            yield "score", 0, 0
            yield "score", 0, 1
            for i in range(I + 1):
                if i and i % 8 == 0:
                    yield "invert", i - 1, None
                for hh in range(2):
                    if i + 1 < I:
                        yield "score", i + 1, hh
                    if i < I:
                        for g in range(items[i][1] // 4 + 1):
                            yield "turn", i, (hh, g)
                if i:
                    if i % 8 == 0:
                        for th in range(2):
                            yield "spread", items[i - 1][0], th
                    yield "product", i - 1, None

        order = list(events())
        for kind, i, x in order:
            if kind in ("turn", "spread"):
                of_item[kind, i, x] = len(groups)
                groups.append((kind, i, x))
        NG = len(groups)
        assert NG % 2 == 0

        act_order, held = [], []
        for event in order:
            if held and event[0] != "turn":
                act_order += held
                held = []
            if event[0] == "score":
                held = [event]
            else:
                act_order.append(event)
        act_order += held

        def turned_of(i):
            return of_item["turn", i, (1, items[i][1] // 4)] + 1

        with nc.Block() as block:

            @block.sync
            def _(sp):
                def load(hp):
                    for i, n in enumerate(("q", "k", "v")):
                        sp.dma_start(w[:, i, :], dram[f"L2_w{n}"][:, bass.ds(hp * C, C)]).then_inc(w_loaded, 16)

                with sp.Fori(1, STEPS) as hp:
                    sp.wait_ge(pj, hp * PJ)
                    load(hp)

            @block.tensor
            def _(pe):
                def project(hp):
                    if not (isinstance(hp, int) and hp == 0):
                        pe.wait_ge(w_loaded, hp * 48)
                    for n in range(PJ):
                        if 4 <= n < 8:
                            pe.wait_ge(pj_d if n % 2 else pj_a, hp * PJ + (n // 2 * 2 - 2))
                        if n < 8:
                            b, t = chunk(n % 4)
                            pe.matmul(R.ps[:, n % 4, :], w[:, n // 4, :], h_chunk(R, n) if n < 4 else lat[:, b, t],
                                      start=True, stop=True).then_inc(pj, 1)
                            continue
                        b = n - 8
                        if not (isinstance(hp, int) and hp == 0):
                            if b == 0:
                                pe.wait_ge(t_a, hp * (NG // 2))
                                pe.wait_ge(t_d, hp * (NG // 2))
                            else:
                                pe.wait_ge(y_done, hp * 4)
                        for i in range(8):
                            bank = 4 + 2 * b + i // 4
                            last = pe.matmul(R.ps[:, bank, (i % 4) * C:(i % 4 + 1) * C], lat[:, b, i * 128:(i + 1) * 128],
                                             w[:, 2, :], start=True, stop=True)
                        last.then_inc(pj, 1)

                def score(hp, i, hh):
                    b, tb = items[i]
                    a = 2 * i + hh
                    if i:
                        pe.wait_ge(exp_done, hp * (2 * I) + (a - 1))
                    full = (tb + 1) * 128
                    for c0 in range(0, full, CW):
                        n = min(CW, full - c0)
                        diag = c0 + n == full
                        bank = 2 * hh + c0 // CW
                        if diag:
                            pe.matmul(R.ps[:, bank, n - 128:n], R.identb[:], late[:], start=True, stop=False,
                                      skip_group_check=True)
                        last = pe.matmul(R.ps[:, bank, 0:n], q[:, hh, b, tb * 128:(tb + 1) * 128],
                                         k[:, hh, b, c0:c0 + n], start=not diag, stop=True, skip_group_check=True)
                    last.then_inc(s_full, 1)

                def group(hp, g):
                    kind, i, x = groups[g]
                    first = isinstance(hp, int) and hp == 0 and g < 2
                    if g == 0:
                        pe.wait_ge(pj_a, hp * PJ + PJ)
                    if not first:
                        pe.wait_ge(t_d if g % 2 else t_a, hp * (NG // 2) + g // 2)
                    if kind == "turn":
                        hh, part = x
                        pe.wait_ge(exp_done, hp * (2 * I) + (2 * i + hh + 1))
                        for s in range(4 * part, min(4 * part + 4, items[i][1] + 1)):
                            last = pe.transpose(R.ps[:, 4 + g % 2, (s % 4) * 128:(s % 4 + 1) * 128],
                                                p[:, i % 2, hh, s * 128:(s + 1) * 128], R.ident[:])
                    else:
                        pe.wait_ge(inv_done, hp * 2 + (i + 1))
                        for n in range(8):
                            j, hh = n // 2, n % 2
                            last = pe.matmul(R.ps[PH * hh:PH * hh + PH, 4 + g % 2, j * 128:(j + 1) * 128],
                                             rinv[:, i, 4 * x + j, hh:hh + 1].broadcast_to([128, PH]), R.ident[:],
                                             start=True, stop=True)
                    last.then_inc(t_full, 1)

                def product(hp, i):
                    b, tb = items[i]
                    n = turned_of(i)
                    pe.wait_ge(t_a, hp * (NG // 2) + (n + 1) // 2)
                    pe.wait_ge(t_d, hp * (NG // 2) + n // 2)
                    if i == 0:
                        pe.wait_ge(pj_a, hp * PJ + PJ)
                        pe.wait_ge(pj_d, hp * PJ + PJ)
                    if i % 8 == 0 and not (isinstance(hp, int) and hp == 0 and i == 0):
                        pe.wait_ge(y_done, hp * 4 + 2 * b)
                    for s in range(tb + 1):
                        for hh in range(2):
                            last = pe.matmul(R.ps[PH * hh:PH * hh + PH, 6 + tb // 4, (tb % 4) * 128:(tb % 4 + 1) * 128],
                                             v[:, b, s, PH * hh:PH * hh + PH], pT[:, i % 2, hh, s, :],
                                             start=(s == 0), stop=(s == tb))
                    last.then_inc(pv_done, 1)

                def step(hp):
                    project(hp)
                    pe.wait_ge(pj_a, hp * PJ + 8)
                    pe.wait_ge(pj_d, hp * PJ + 8)
                    for kind, i, x in order:
                        if kind == "score":
                            score(hp, i, x)
                        elif kind == "product":
                            product(hp, i)
                        elif kind in ("turn", "spread"):
                            group(hp, of_item[kind, i, x])

                pe.wait_ge(W.late_loaded, 16)
                pe.wait_ge(W.zeroed, 2)
                step(0)
                with pe.Fori(1, STEPS) as hp:
                    step(hp)

            def projected(n):
                if n < 8:
                    b, t = chunk(n % 4)
                    return [((q if n < 4 else k)[0:PH, hh, b, t], R.ps[PH * hh:PH * hh + PH, n % 4, :],
                             PH ** -0.5 if n < 4 else 1.0) for hh in range(2)]
                b = n - 8
                return [(v[:, b, 4 * g:4 * g + 4, :].rearrange("p s c -> p (s c)"), R.ps[:, 4 + 2 * b + g, :], 1.0)
                        for g in range(2)]

            def moved(g):
                kind, i, x = groups[g]
                src = R.ps[:, 4 + g % 2, :]
                if kind == "spread":
                    return rrow[:, x, :], src
                hh, part = x
                n = min(4, items[i][1] + 1 - 4 * part)
                return pT[:, i % 2, hh, 4 * part:4 * part + n, :].rearrange("p s t -> p (s t)"), src[:, 0:n * 128]

            @block.scalar
            def _(act):
                def step(hp):
                    for n in range(0, PJ, 2):
                        act.wait_ge(pj, hp * PJ + (n + 1))
                        for dst, src, scale in projected(n):
                            act.activation(dst, src, ACT.Copy, scale=scale).then_inc(pj_a, 1)
                    for kind, i, x in act_order:
                        if kind == "score":
                            b, tb = items[i]
                            a = 2 * i + x
                            act.wait_ge(max_done, hp * (2 * I) + (a + 1))
                            if i >= 2:
                                act.wait_ge(t_full, hp * NG + turned_of(i - 2))
                            n = (tb + 1) * 128
                            src = R.ps[:, 2 * x:2 * x + 2, :].rearrange("p a c -> p (a c)")[:, 0:n]
                            act.activation(p[:, i % 2, x, 0:n], src, ACT.Exp, bias=nm[:, a % 4:a % 4 + 1],
                                           accum_out=rs[:, b, tb, x:x + 1]).then_inc(exp_done, 1)
                        elif kind in ("turn", "spread"):
                            g = of_item[kind, i, x]
                            if g % 2 == 0:
                                act.wait_ge(t_full, hp * NG + (g + 1))
                                if kind == "turn" and i >= 2:
                                    act.wait_ge(pv_done, hp * I + (i - 1))
                                dst, src = moved(g)
                                act.activation(dst, src, ACT.Copy).then_inc(t_a, 1)

                step(0)
                with act.Fori(1, STEPS) as hp:
                    step(hp)

            @block.vector
            def _(dve):
                def divide(hp, b):
                    dve.wait_ge(t_a, hp * (NG // 2) + (of_item["spread", b, 1] + 2) // 2)
                    for th in range(2):
                        dve.tensor_tensor(y[:, bass.ds(hp, 1), b, th * CW:(th + 1) * CW], R.ps[:, 6 + th, :].unsqueeze(1),
                                          rrow[:, th, :].unsqueeze(1), ALU.mult).then_inc(y_done, 1)

                def step(hp):
                    for n in range(1, PJ, 2):
                        dve.wait_ge(pj, hp * PJ + (n + 1))
                        for dst, src, scale in projected(n):
                            dve.tensor_scalar(dst, src, scale, None, ALU.mult).then_inc(pj_d, 1)
                    moved_here = hp * (NG // 2)
                    for kind, i, x in order:
                        if kind == "score":
                            b, tb = items[i]
                            a = 2 * i + x
                            dve.wait_ge(s_full, hp * (2 * I) + (a + 1))
                            if a >= 4:
                                dve.wait_ge(exp_done, hp * (2 * I) + (a - 3))
                            n = (tb + 1) * 128
                            src = R.ps[:, 2 * x:2 * x + 2, :].rearrange("p a c -> p (a c)")[:, 0:n]
                            dve.tensor_reduce(nm[:, a % 4:a % 4 + 1], src, X_AXIS, ALU.max, negate=True)\
                               .then_inc(max_done, 1)
                        elif kind == "invert":
                            b = items[i][0]
                            dve.wait_ge(exp_done, hp * (2 * I) + (2 * i + 2))
                            dve.reciprocal(rinv[:, b], rs[:, b]).then_inc(inv_done, 1)
                        elif kind == "product":
                            if i % 8 == 7:
                                dve.wait_ge(pv_done, hp * I + (i + 1))
                                divide(hp, items[i][0])
                        else:
                            g = of_item[kind, i, x]
                            if g % 2:
                                dve.wait_ge(t_full, hp * NG + (g + 1))
                                if kind == "turn" and i >= 2:
                                    dve.wait_ge(pv_done, hp * I + (i - 1))
                                dst, src = moved(g)
                                dve.tensor_copy(dst, src).then_inc(t_d, 1)
                                if kind == "spread":
                                    dve.wait_ge(t_d, moved_here + (g + 1) // 2)

                step(0)
                with dve.Fori(1, STEPS) as hp:
                    step(hp)


def moe_stage(nc, R, W, dram):
    with ExitStack() as ctx:
        sb = lambda n, s, d=F32: ctx.enter_context(nc.sbuf_tensor("ex_" + n, s, d))
        sem = lambda n: nc.alloc_semaphore("ex_" + n)
        wsplit = sb("wsplit", [128, 2, N], BF16)
        rw, bias, before, shw = W.rw, W.bias, W.before, W.shw
        score = sb("score", [128, TB, E])
        sbias = sb("sbias", [128, TB, E])
        hi, lo = sb("hi", [128, TB * GRP, 4]), sb("lo", [128, TB * GRP, 4])
        t1, t2 = sb("t1", [128, TB * GRP, 4]), sb("t2", [128, TB * GRP, 4])
        grp = sb("grp", [128, TB, GRP])
        gt, eq = sb("gt", [128, TB, GRP * GRP]), sb("eq", [128, TB, GRP * GRP])
        rank = sb("rank", [128, TB, GRP])
        keep, drop = sb("keep", [128, TB, GRP]), sb("drop", [128, TB, GRP])
        masked = sb("masked", [128, TB, E])
        left = sb("left", [128, TB, E])
        top = sb("top", [128, TB, 8])
        tot = sb("tot", [128, TB])
        parts = sb("parts", [128, TB, 2, 4, E // 2], BF16)
        prod, scored, routed, top_step, parted, turned, out = (
            sem(n) for n in ("prod", "scored", "step", "top", "parted", "turned", "out"))
        shs, shu, shh = sb("shs", [C, 2, CW]), sb("shu", [C, 2, CW]), sb("shh", [C, 2, CW])
        sh_g, sh_u, sh_silu, sh_copied, sh_hid, sh_down = (
            sem("sh_" + n) for n in ("g", "u", "silu", "copied", "hid", "down"))
        SH = 2 * NC
        wg = sb("wg", [C, 2, C])
        wu = sb("wu", [C, 2, C])
        wd = sb("wd", [C, 2, C])
        choose = sb("choose", [128, EP // 2, C], BF16)
        s = sb("s", [C, 2, CW])
        su = sb("su", [C, 2, CW])
        hid = sb("hid", [C, 2, CW])
        const_loaded = sem("const")
        ld = [sem("ld0"), sem("ld1")]
        g_full, silu_done, u_full, su_done, w_full, hid_done, d_done, res_done = (
            sem(n) for n in ("g_full", "silu", "u_full", "su", "w_full", "hid", "d", "res"))
        G_BANK, U_BANK, W_BANK = 4, 5, 6
        STEPS = EP // 2
        with nc.Block() as block:

            @block.sync
            def _(sp):
                def load(pair, slot):
                    sp.dma_start(wg[:, slot, :], dram["ex_gate"][bass.ds(pair * C, C), :]).then_inc(ld[slot], 16)
                    sp.dma_start(wu[:, slot, :], dram["ex_up"][bass.ds(pair * C, C), :]).then_inc(ld[slot], 16)
                    sp.dma_start(wd[:, slot, :], dram["ex_down"][bass.ds(pair * C, C), :]).then_inc(ld[slot], 16)

                load(0, 0)
                load(1, 1)
                with sp.Fori(1, STEPS) as kk:
                    for slot in range(2):
                        sp.wait_ge(d_done, kk * 8 + (4 * slot - 4))
                        load(kk * 2 + slot, slot)

            @block.gpsimd
            def _(pool):
                pool.memset(parts[:, :, :, 3, :], 0.0).then_inc(parted, 1)
                pool.dma_start(choose[:], dram["choose"]).then_inc(const_loaded, 16)
                for i in range(SH):
                    pool.wait_ge(sh_silu, i + 1)
                    pool.wait_ge(sh_copied, i + 1)
                    if i >= 2:
                        pool.wait_ge(sh_down, i - 1)
                    pool.tensor_tensor(shh[:, i % 2, :], shs[:, i % 2, :], shu[:, i % 2, :], ALU.mult)\
                        .then_inc(sh_hid, 1)

            @block.tensor
            def _(pe):
                pe.wait_ge(W.loaded, W.count)
                for tb in range(TB):
                    last = pe.matmul(R.ps[:, 6 + tb // 8, (tb % 8) * E:(tb % 8 + 1) * E], h_block(R, tb), rw[:],
                                     start=True, stop=True)
                last.then_inc(prod, 1)

                def shared_down(i):
                    pe.wait_ge(sh_hid, i + 1)
                    pe.matmul(R.ps[:, i % 4, :], shw[:, 2, i // 4, :], shh[:, i % 2, :], start=(i < 4), stop=True,
                              skip_group_check=True).then_inc(sh_down, 1)

                for i in range(SH):
                    if i:
                        pe.wait_ge(sh_silu, i)
                    pe.matmul(R.ps[:, G_BANK, :], shw[:, 0, i // 4, :], h_chunk(R, i % 4), start=True, stop=True)\
                        .then_inc(sh_g, 1)
                    if i:
                        pe.wait_ge(sh_copied, i)
                    pe.matmul(R.ps[:, U_BANK, :], shw[:, 1, i // 4, :], h_chunk(R, i % 4), start=True, stop=True)\
                        .then_inc(sh_u, 1)
                    if i:
                        shared_down(i - 1)
                shared_down(SH - 1)

                pe.wait_ge(sh_silu, SH)
                pe.wait_ge(sh_copied, SH)
                pe.wait_ge(parted, 6)
                for tb in range(TB):
                    for i in range(2):
                        dst = R.ps[:, 4 + tb // 4, :].bitcast(BF16)[:, ((tb % 4) * 2 + i) * 128:((tb % 4) * 2 + i + 1) * 128]
                        last = pe.transpose(dst, parts[:, tb, i].rearrange("p a e -> p (a e)"), R.identb[:])
                    if tb % 4 == 3:
                        last.then_inc(turned, 1)

                def down(kk, i):
                    m = kk * 8 + i
                    pe.wait_ge(hid_done, m + 1)
                    pe.matmul(R.ps[:, i % 4, :], wd[:, (i // 4) % 2, :], hid[:, i % 2, :], start=False,
                              stop=True, skip_group_check=True).then_inc(d_done, 1)

                def step(kk, half, first=False):
                    for i in range(8):
                        m = kk * 8 + i
                        slot, c = i // 4, i % 4
                        if c == 0:
                            pe.wait_ge(ld[slot], kk * 48 + 48)
                        if not (first and i == 0):
                            pe.wait_ge(silu_done, m)
                        pe.matmul(R.ps[:, G_BANK, :], wg[:, slot, :], h_chunk(R, c), start=True, stop=True).then_inc(g_full, 1)
                        if not (first and i == 0):
                            pe.wait_ge(su_done, m)
                        pe.matmul(R.ps[:, U_BANK, :], wu[:, slot, :], h_chunk(R, c), start=True, stop=True).then_inc(u_full, 1)
                        if not (first and i == 0):
                            pe.wait_ge(hid_done, m)
                        pair = choose[:, bass.ds(kk * 2 + (slot - half * (EP // 2)), 1), :]
                        pe.matmul(R.ps[:, W_BANK, :], pair, wsplit[:, half, c * CW:(c + 1) * CW],
                                  start=True, stop=True).then_inc(w_full, 1)
                        if not (first and i == 0):
                            down(kk, i - 1)

                pe.wait_ge(out, TB // 4)
                pe.wait_ge(const_loaded, 16)
                step(0, 0, True)
                with pe.Fori(1, STEPS // 2) as kk:
                    step(kk, 0)
                with pe.Fori(STEPS // 2, STEPS) as kk:
                    step(kk, 1)
                down(STEPS - 1, 7)

            @block.scalar
            def _(act):
                act.wait_ge(prod, 1)
                logits = R.ps[:, 6:8, :].rearrange("p a (t e) -> p (a t) e", e=E)
                act.activation(score[:], logits, ACT.Sigmoid).then_inc(scored, 1)
                for i in range(SH):
                    act.wait_ge(sh_g, i + 1)
                    if i >= 2:
                        act.wait_ge(sh_hid, i - 1)
                    act.activation(shs[:, i % 2, :], R.ps[:, G_BANK, :], ACT.Silu).then_inc(sh_silu, 1)
                    act.wait_ge(sh_u, i + 1)
                    act.activation(shu[:, i % 2, :], R.ps[:, U_BANK, :], ACT.Copy).then_inc(sh_copied, 1)
                for g in range(TB // 4):
                    act.wait_ge(turned, g + 1)
                    src = R.ps[:, 4 + g, :].bitcast(BF16).rearrange("p (t i c) -> p i t c", t=4, i=2)
                    act.activation(wsplit[:, :, g * CW:(g + 1) * CW].rearrange("p i (t c) -> p i t c", t=4), src, ACT.Copy)\
                       .then_inc(out, 1)

                def step(kk, first=False):
                    for i in range(8):
                        m = kk * 8 + i
                        act.wait_ge(g_full, m + 1)
                        if not (first and i < 2):
                            act.wait_ge(su_done, m - 1)
                        act.activation(s[:, i % 2, :], R.ps[:, G_BANK, :], ACT.Silu).then_inc(silu_done, 1)

                step(0, True)
                with act.Fori(1, STEPS) as kk:
                    step(kk)

            @block.vector
            def _(dve):
                n = 0

                def after(ins):
                    nonlocal n
                    n += 1
                    ins.then_inc(routed, 1)

                def tt(out, a, b, op):
                    after(dve.tensor_tensor(out, a, b, op))

                def ts(out, a, s1, s2, op0, op1=None):
                    after(dve.tensor_scalar(out, a, s1, s2, op0, op1) if op1 else dve.tensor_scalar(out, a, s1, s2, op0))

                dve.wait_ge(W.loaded, W.count)
                dve.wait_ge(scored, 1)
                tt(sbias[:], score[:], bias[:].unsqueeze(1).broadcast_to([128, TB, E]), ALU.add)
                dve.wait_ge(routed, n)
                v = sbias[:].rearrange("p t (g e) -> p (t g) e", g=GRP)
                tt(hi[:], v[:, :, 0:4], v[:, :, 4:8], ALU.max)
                tt(lo[:], v[:, :, 0:4], v[:, :, 4:8], ALU.min)
                dve.wait_ge(routed, n)
                for wd in (2, 1):
                    a, b = slice(0, wd), slice(wd, 2 * wd)
                    tt(t1[:, :, 0:wd], hi[:, :, a], hi[:, :, b], ALU.min)
                    tt(t2[:, :, 0:wd], lo[:, :, a], lo[:, :, b], ALU.max)
                    tt(hi[:, :, a], hi[:, :, a], hi[:, :, b], ALU.max)
                    dve.wait_ge(routed, n)
                    tt(lo[:, :, a], t1[:, :, 0:wd], t2[:, :, 0:wd], ALU.max)
                    dve.wait_ge(routed, n)
                tt(grp[:].rearrange("p t g -> p (t g)").unsqueeze(2), hi[:, :, 0:1], lo[:, :, 0:1], ALU.add)
                dve.wait_ge(routed, n)
                own = grp[:].unsqueeze(3).broadcast_to([128, TB, GRP, GRP])
                other = grp[:].unsqueeze(2).broadcast_to([128, TB, GRP, GRP])
                g4 = lambda x: x[:].rearrange("p t (a b) -> p t a b", a=GRP)
                tt(g4(gt), other, own, ALU.is_gt)
                tt(g4(eq), other, own, ALU.is_equal)
                dve.wait_ge(routed, n)
                tt(eq[:], eq[:], before[:].unsqueeze(1).broadcast_to([128, TB, GRP * GRP]), ALU.mult)
                dve.wait_ge(routed, n)
                tt(gt[:], gt[:], eq[:], ALU.add)
                dve.wait_ge(routed, n)
                after(dve.tensor_reduce(rank[:], g4(gt), X_AXIS, ALU.add))
                dve.wait_ge(routed, n)
                ts(keep[:], rank[:], 3.5, None, ALU.is_lt)
                dve.wait_ge(routed, n)
                ts(drop[:], keep[:], 1e38, -1e38, ALU.mult, ALU.add)
                e4 = lambda x: x[:].rearrange("p t (g e) -> p t g e", g=GRP)
                wide = lambda x: x[:].unsqueeze(3).broadcast_to([128, TB, GRP, 8])
                tt(e4(masked), e4(sbias), wide(keep), ALU.mult)
                dve.wait_ge(routed, n)
                tt(e4(masked), e4(masked), wide(drop), ALU.add)
                dve.wait_ge(routed, n)
                for tb in range(TB):
                    dve.max(top[:, tb, :], masked[:, tb, :]).then_inc(top_step, 1)
                for tb in range(TB):
                    dve.wait_ge(top_step, tb + 1)
                    dve.match_replace(left[:, tb, :], top[:, tb, :], masked[:, tb, :], -2e38).then_inc(top_step, 1)
                dve.wait_ge(top_step, 2 * TB)
                tt(left[:], left[:], masked[:], ALU.is_lt)
                dve.wait_ge(routed, n)
                tt(score[:], score[:], left[:], ALU.mult)
                dve.wait_ge(routed, n)
                after(dve.tensor_reduce(tot[:], score[:], X_AXIS, ALU.add))
                dve.wait_ge(routed, n)
                ts(tot[:], tot[:], 1e-20, None, ALU.add)
                dve.wait_ge(routed, n)
                after(dve.reciprocal(tot[:], tot[:]))
                dve.wait_ge(routed, n)
                tt(score[:], score[:], tot[:].unsqueeze(2).broadcast_to([128, TB, E]), ALU.mult)
                dve.wait_ge(routed, n)
                part = lambda i: parts[:, :, :, i, :]
                h = lambda x: x[:].rearrange("p t (i e) -> p t i e", i=2)
                for i, op in enumerate(((part(0), h(score)), (h(masked), h(score), part(0)), (part(1), h(masked)),
                                        (h(left), h(masked), part(1)), (part(2), h(left)))):
                    if len(op) == 2:
                        dve.tensor_copy(*op).then_inc(parted, 1)
                    else:
                        dve.tensor_tensor(*op, ALU.subtract).then_inc(parted, 1)
                    dve.wait_ge(parted, i + 2)

                def step(kk, first=False):
                    for i in range(8):
                        m = kk * 8 + i
                        dve.wait_ge(silu_done, m + 1)
                        dve.wait_ge(u_full, m + 1)
                        if not (first and i < 2):
                            dve.wait_ge(d_done, m - 1)
                        dve.tensor_tensor(su[:, i % 2, :], s[:, i % 2, :], R.ps[:, U_BANK, :], ALU.mult)\
                           .then_inc(su_done, 1)
                        dve.wait_ge(su_done, m + 1)
                        dve.wait_ge(w_full, m + 1)
                        dve.tensor_tensor(hid[:, i % 2, :], su[:, i % 2, :], R.ps[:, W_BANK, :], ALU.mult)\
                           .then_inc(hid_done, 1)

                step(0, True)
                with dve.Fori(1, STEPS) as kk:
                    step(kk)
                dve.wait_ge(d_done, EP * 4)
                for c in range(NC):
                    b, t = chunk(c)
                    dve.scalar_tensor_tensor(R.x[:, b, t], R.ps[:, c, :], mod_cols(R, 2, 1, b)[2], R.x[:, b, t],
                                             ALU.mult, ALU.add).then_inc(res_done, 1)


def linear_stage(nc, R, W, attn):
    with ExitStack() as ctx:
        sb = lambda n, s, d=F32: ctx.enter_context(nc.sbuf_tensor("la_" + n, s, d))
        sem = lambda n: nc.alloc_semaphore("la_" + n)
        wq, wkv, sc = W.wq, W.wkv, W.sc
        qf = sb("qf", [C, NC, CW])
        q2 = sb("q2", [C, NC, CW])
        k = sb("k", [128, TB, C])
        v = sb("v", [128, TB, C])
        k2 = sb("k2", [128, TB, C])
        kn = sb("kn", [128, TB, HEADS])
        mask = sb("mask", [128, C])
        kv = sb("kv", [C, B, C])
        qp, q_copied, squared, norm, q_root, q_len, inverted, spread, q_hat, kvp, v_copied, k_sq, k_sum, k_root, k_hat, outer, masked, \
            att, done, step, nc_step = (sem(n) for n in (
                "qp", "q_copied", "squared", "norm", "q_root", "q_len", "inverted", "spread", "q_hat", "kvp", "v_copied", "k_sq",
                "k_sum", "k_root", "k_hat", "outer", "masked", "att", "done", "step", "nc_step"))
        with nc.Block() as block:

            @block.tensor
            def _(pe):
                pe.wait_ge(W.loaded, W.count)
                for c in range(NC):
                    pe.matmul(R.ps[:, 4 + c, :], wq[:], h_chunk(R, c), start=True, stop=True).then_inc(qp, 1)
                for g in range(TB // 4):
                    if g >= 2:
                        pe.wait_ge(v_copied, g - 1)
                        pe.wait_ge(k_sq, 2 * (g - 1) - 1)
                    for a in range(2):
                        for i in range(4):
                            last = pe.matmul(R.ps[:, 2 * (g % 2) + a, i * C:(i + 1) * C], h_block(R, 4 * g + i),
                                             wkv[:, a, :], start=True, stop=True)
                    last.then_inc(kvp, 1)
                pe.wait_ge(v_copied, TB // 4)
                pe.wait_ge(k_sq, TB // 2)
                for c in range(NC):
                    pe.wait_ge(squared, c + 1)
                    last = pe.matmul(R.ps[32 * c:32 * c + 32, 3, :], W.head_sum[:], q2[:, c, :], start=True, stop=True)
                last.then_inc(norm, 1)
                pe.wait_ge(k_hat, 1)
                for b in range(B):
                    for s in range(8):
                        last = pe.matmul(R.ps[:, 2, b * C:(b + 1) * C], k[:, 8 * b + s, :], v[:, 8 * b + s, :],
                                         start=(s == 0), stop=(s == 7))
                    last.then_inc(outer, 1)
                pe.wait_ge(inverted, 1)
                for c in range(NC):
                    if c >= 2:
                        pe.wait_ge(q_hat, c - 1)
                    pe.matmul(R.ps[:, c % 2, :], W.head_spread[:, c, :], q2[:, 0, :], start=True, stop=True)\
                        .then_inc(spread, 1)
                for c in range(NC):
                    pe.wait_ge(q_hat, c + 1)
                    pe.wait_ge(q_copied, c + 1)
                    pe.wait_ge(masked, c // 2 + 1)
                    pe.matmul(R.ps[:, 4 + c, :], kv[:, c // 2, :], qf[:, c, :], start=True, stop=True).then_inc(att, 1)

            @block.scalar
            def _(act):
                for c in range(NC):
                    act.wait_ge(qp, c + 1)
                    act.activation(q2[:, c, :], R.ps[:, 4 + c, :], ACT.Square).then_inc(squared, 1)
                    act.activation(qf[:, c, :], R.ps[:, 4 + c, :], ACT.Copy).then_inc(q_copied, 1)
                for g in range(TB // 4):
                    act.wait_ge(kvp, g + 1)
                    act.activation(v[:, 4 * g:4 * g + 4, :].rearrange("p t c -> p (t c)"), R.ps[:, 2 * (g % 2) + 1, :],
                                   ACT.Copy).then_inc(v_copied, 1)
                act.wait_ge(k_sum, 1)
                act.activation(kn[:], kn[:], ACT.Sqrt).then_inc(k_root, 1)
                act.wait_ge(norm, 1)
                act.activation(q2[:, 1, :], R.ps[:, 3, :], ACT.Sqrt).then_inc(q_root, 1)
                act.wait_ge(W.loaded, W.count)
                act.activation(sc[:], sc[:], ACT.Sigmoid).then_inc(nc_step, 1)
                act.wait_ge(nc_step, 1)
                act.activation(sc[:], sc[:], ACT.Exp, scale=-math.log(T)).then_inc(nc_step, 1)
                for c in range(NC):
                    b, t = chunk(c)
                    act.wait_ge(att, c + 1)
                    act.activation(attn[:, b, t], R.ps[:, 4 + c, :], ACT.Copy).then_inc(done, 1)

            @block.vector
            def _(dve):
                for g in range(TB // 4):
                    dve.wait_ge(kvp, g + 1)
                    kg = k[:, 4 * g:4 * g + 4, :].rearrange("p t c -> p (t c)")
                    dve.tensor_copy(kg, R.ps[:, 2 * (g % 2), :]).then_inc(k_sq, 1)
                    dve.wait_ge(k_sq, 2 * g + 1)
                    dve.tensor_tensor(k2[:, 4 * g:4 * g + 4, :].rearrange("p t c -> p (t c)"), kg, kg, ALU.mult)\
                       .then_inc(k_sq, 1)
                dve.wait_ge(k_sq, TB // 2)
                kh = lambda x: x[:].rearrange("p t (h c) -> p t h c", c=8)
                dve.tensor_reduce(kn[:], kh(k2), X_AXIS, ALU.add).then_inc(k_sum, 1)
                dve.wait_ge(k_root, 1)
                dve.tensor_scalar(kn[:], kn[:], 1e-12, None, ALU.max).then_inc(step, 1)
                dve.wait_ge(step, 1)
                dve.reciprocal(kn[:], kn[:]).then_inc(step, 1)
                dve.wait_ge(step, 2)
                dve.tensor_tensor(kh(k), kh(k), kn[:].unsqueeze(3).broadcast_to([128, TB, HEADS, 8]), ALU.mult)\
                   .then_inc(k_hat, 1)
                dve.wait_ge(q_root, 1)
                dve.tensor_scalar(q2[:, 1, :], q2[:, 1, :], 1e-12, None, ALU.max).then_inc(q_len, 1)
                dve.wait_ge(q_len, 1)
                dve.reciprocal(q2[:, 0, :], q2[:, 1, :]).then_inc(inverted, 1)
                dve.wait_ge(nc_step, 2)
                dve.tensor_tensor(mask[:].rearrange("p (h c) -> p h c", c=8), R.blk8[:].rearrange("p (h c) -> p h c", c=8),
                                  sc[:].unsqueeze(2).broadcast_to([128, HEADS, 8]), ALU.mult).then_inc(step, 1)
                for c in range(NC):
                    dve.wait_ge(spread, c + 1)
                    dve.wait_ge(q_copied, c + 1)
                    dve.tensor_tensor(qf[:, c, :], qf[:, c, :], R.ps[:, c % 2, :], ALU.mult).then_inc(q_hat, 1)
                dve.wait_ge(step, 3)
                dve.wait_ge(outer, 2)
                for b in range(B):
                    dve.tensor_tensor(kv[:, b, :], R.ps[:, 2, b * C:(b + 1) * C], mask[:], ALU.mult).then_inc(masked, 1)


def store_stage(nc, R, out):
    stored = nc.alloc_semaphore("stored")
    with nc.Block() as block:

        @block.sync
        def _(sp):
            sp.dma_start(out, R.x[:]).then_inc(stored, 16)
            sp.wait_ge(stored, 16)


def build_program(nc, dram, out, halves=8):
    R = Residents(nc)
    early = ExitStack()
    M = Modulation(nc, early)
    setup_stage(nc, R, M, dram, (0,) if 0 in halves else (0, 1))
    if 0 not in halves:
        early.close()

    def softmax_layer(name, layer, rows, dim, groups, hg, mask):
        with ExitStack() as ctx:
            A = Attn(nc, name, rows, dim, groups, hg, mask)
            W = Weights(nc, ctx, name)
            W.w = W.tile("w", [C, 3, C])
            W.loads += [(W.w[:, i, :], dram[f"L{layer}_w{n}T"]) for i, n in enumerate("qkv")]
            W.bqk, W.bv = (W.tile("bqk", [C, 2]), W.add("bv", [128, C], dram["L1_bv"].broadcast_to([128, C]))) \
                if mask else (None, None)
            if mask:
                W.loads += [(W.bqk[:, i:i + 1], dram[f"L1_b{n}"]) for i, n in enumerate("qk")]
            W.den_sel = W.add("den_sel", [128, 64], dram["den_sel"])
            W.den_spread = W.add("den_spread", [128, 2, 128], dram["den_spread"])
            if layer == 0:
                W.lam, W.cols = W.tile("lam", [128, 4, 4]), W.tile("cols", [128, 8])
                W.loads += [(W.lam[:, i, :], dram[f"L0_lam{i}"].broadcast_to([128, 4])) for i in range(4)]
                W.loads += [(W.cols[:, 0:2], dram["parity"]), (W.cols[:, 2:3], dram["subln_col"])]
                W.pick = W.add("pick", [128, 4, C], dram["pick"])
                W.head_sum = W.add("head_sum", [128, 32], dram["head_sum"])
                W.head_spread = W.add("head_spread", [128, NC, 128], dram["head_spread"])
                W.prod, W.dots = W.tile("prod", [128, 2, 4]), W.tile("dots", [128, 2])
                W.lam_step, W.exped = nc.alloc_semaphore("lam_step"), nc.alloc_semaphore("lam_exped")
                W.wo = W.add("wo", [C, C], dram["L0_woT"])
            else:
                W.wo, W.bo = W.add("wo", [128, 2, C], dram["L1_woG"]), W.add("bo", [C, 1], dram["L1_bo"])
            A.v = ctx.enter_context(nc.sbuf_tensor(name + "v", [128, groups, 8, hg, 9], F32))
            A.parts = ctx.enter_context(nc.sbuf_tensor(name + "parts_sb", [C, 2, 3, B, T], BF16))
            A.q = ctx.enter_context(nc.sbuf_tensor(name + "q", [128, 2, A.row_tiles, T], BF16))
            A.k = ctx.enter_context(nc.sbuf_tensor(name + "k", [128, 2, 4, T], BF16))
            norm_stage(nc, R, layer, 0, W, init_operands(A, 0))
            project_stage(nc, R, W, A, layer, modulation_programs(R, M, 1) if layer == 0 else None)
            A.on = ctx.enter_context(nc.sbuf_tensor(name + "on", [128, groups // 2, T], F32))
            softmax_stage(nc, R, W, A)
            if layer == 0:
                diff_out_stage(nc, R, W, A)
            else:
                out_stage(nc, R, W, 1, 0, "o1", lambda i, c: A.on[:, (c // 2) * 2 + i, chunk(c)[1]], 2, W.wo, W.bo)

    def lora_layer(layer):
        with ExitStack() as ctx:
            W = Weights(nc, ctx, f"f{layer}")
            p = f"L{layer}_f"
            W.w1, W.w2 = W.add("w1", [C, HID], dram[p + "W1T"]), W.add("w2", [C, HB, C], dram[p + "W2T"])
            W.b1, W.b2 = W.add("b1", [C, HB], dram[p + "b1"]), W.add("b2", [C, 1], dram[p + "b2"])
            W.scale = W.add("scale", [128, 1], dram[p + "scale"].broadcast_to([128, 1]))
            W.eye8 = W.add("eye8", [8, 8], dram["ident"][0:8, 0:8])
            norm_stage(nc, R, layer, 1, W)
            lora_stage(nc, R, W, layer)

    def layer_0a():
        softmax_layer("a0", 0, 32, 4, 16, 2, False)

    def layer_0b():
        lora_layer(0)

    def layer_1a():
        softmax_layer("a1", 1, 64, 8, 8, 4, True)

    def layer_1b():
        with ExitStack() as ctx:
            W = Weights(nc, ctx, "mx")
            W.w, W.mu = W.tile("w", [C, 3, C]), W.tile("mu", [C, 4])
            W.loads += [(W.w[:, i, :], dram[f"L1_W{n}T"]) for i, n in enumerate("rkv")]
            W.loads += [(W.mu[:, i:i + 1], dram[f"L1_mu{n}"]) for i, n in enumerate("rk")]
            norm_stage(nc, R, 1, 1, W)
            mix_stage(nc, R, W)

    def layer_2a():
        with ExitStack() as ctx:
            W = Weights(nc, ctx, "a2")
            W.down = W.add("down", [C, C], dram["L2_kv_down"])
            W.wo = W.add("wo", [128, HEADS // 2, C], dram["L2_wout"])
            W.late = ctx.enter_context(nc.sbuf_tensor("late", [128, 128], BF16))
            W.late_loaded = nc.alloc_semaphore("late_loaded")

            W.qkv = W.tile("qkv", [C, 3, C])
            W.loads += [(W.qkv[:, i, :], dram[f"L2_w{n}"][:, 0:C]) for i, n in enumerate(("q", "k", "v"))]
            W.q, W.k = W.tile("q", [96, 2, B, T]), W.tile("k", [96, 2, B, T])
            W.zeroed = nc.alloc_semaphore("a2zeroed")

            def prepare(pool):
                pool.dma_start(W.late[:], dram["late"]).then_inc(W.late_loaded, 16)
                pool.memset(W.q[PH:96], 0.0).then_inc(W.zeroed, 1)
                pool.memset(W.k[PH:96], 0.0).then_inc(W.zeroed, 1)

            norm_stage(nc, R, 2, 0, W, prepare)
            y = ctx.enter_context(nc.sbuf_tensor("y2", [128, HEADS // 2, B, T], F32))
            with ExitStack() as inner:
                lat = inner.enter_context(nc.sbuf_tensor("lat", [C, B, T], F32))
                latent_stage(nc, R, W, lat)
                causal_stage(nc, R, W, dram, lat, y)
            out_stage(nc, R, W, 2, 0, "o2", lambda i, c: y[:, i, c // 2, chunk(c)[1]], HEADS // 2, W.wo)

    def layer_2b():
        with ExitStack() as ctx:
            W = Weights(nc, ctx, "f2")
            W.rw = W.add("rw", [C, E], dram["L2_routerT"])
            W.bias = W.add("bias", [128, E], dram["L2_ebias"].broadcast_to([128, E]))
            W.before = W.add("before", [128, GRP * GRP], dram["before"].broadcast_to([128, GRP * GRP]))
            W.shw = W.tile("shw", [C, 3, 2, C])
            W.loads += [(W.shw[:, i], dram["sh_" + n]) for i, n in enumerate(("gate", "up", "down"))]
            norm_stage(nc, R, 2, 1, W)
            moe_stage(nc, R, W, dram)

    def layer_3a():
        with ExitStack() as ctx:
            W = Weights(nc, ctx, "a3")
            W.wq, W.wkv = W.add("wq", [C, C], dram["L3_wqT"]), W.tile("wkv", [C, 2, C])
            W.loads += [(W.wkv[:, i, :], dram[f"L3_w{n}T"]) for i, n in enumerate("kv")]
            W.sc = W.add("sc", [128, HEADS], dram["L3_norm"].broadcast_to([128, HEADS]))
            W.wo = W.add("wo", [C, 1, C], dram["L3_woT"])
            W.head_sum = W.add("head_sum", [128, 32], dram["head_sum"])
            W.head_spread = W.add("head_spread", [128, NC, 128], dram["head_spread"])
            norm_stage(nc, R, 3, 0, W)
            attn = ctx.enter_context(nc.sbuf_tensor("attn3", [C, B, T], F32))
            linear_stage(nc, R, W, attn)
            out_stage(nc, R, W, 3, 0, "o3", lambda i, c: attn[:, c // 2, chunk(c)[1]], 1, W.wo)

    def layer_3b():
        lora_layer(3)

    for i, half in enumerate((layer_0a, layer_0b, layer_1a, layer_1b, layer_2a, layer_2b, layer_3a, layer_3b)):
        if i in halves:
            with nc.cleanup_on_exit():
                half()
            if i == 0:
                early.close()
    store_stage(nc, R, out)


def constants():
    r = np.arange(128)
    k = {"ident": np.eye(128, dtype=np.float32), "blk8": (r[:, None] // 8 == r[None, :] // 8).astype(np.float32),
         "den_sel": (r[:, None] == r[None, :64] % 8 * 16 + 8).astype(np.float32),
         "den_spread": np.stack([(r[:, None] == 64 * w + r[None, :] // 16) & (r[None, :] % 16 < 8) for w in range(2)],
                                1).astype(np.float32),
         "head_sum": (r[:, None] // 8 == r[None, :32] % 16).astype(np.float32),
         "head_spread": np.stack([(r[:, None] == 32 * c + r[None, :] // 8) for c in range(NC)], 1).astype(np.float32),
         "parity": np.stack([(r // 32) % 2 == 0, (r // 32) % 2 == 1], 1).astype(np.float32),
         "late": np.where(r[None, :] > r[:, None], NEG, 0.0).astype(np.float32),
         "lateT": np.where(r[:, None] > r[None, :], NEG, 0.0).astype(np.float32)}
    pick = np.zeros((128, 4, C), np.float32)
    for pair in range(4):
        for j in range(4):
            for odd in range(2):
                for c in range(8):
                    pick[32 * j + 16 * odd + c, pair, (2 * (2 * pair + odd) + j // 2) * 8 + c] = 1
    k["pick"] = pick
    g = np.arange(GRP)
    k["before"] = (g[None, :] < g[:, None]).astype(np.float32).reshape(1, -1)
    choose = np.zeros((128, EP // 2, C), np.float32)
    for e in range(E // 2):
        choose[[e, 32 + e, 64 + e], e // 2, (e % 2) * EH:(e % 2) * EH + EH] = 1
    k["choose"] = choose
    return k


def lay_out(inputs):
    i = {k: np.asarray(v) for k, v in inputs.items()}
    d = {"xT": i["L0_attn_query"].transpose(2, 0, 1)}
    for l in range(LAYERS):
        d[f"L{l}_wmod"] = i[f"L{l}_wmod"]
    d["cT"] = np.stack([i[f"L{l}_c"].T for l in range(LAYERS)], 1)
    for n in "qkv":
        d[f"L0_w{n}T"] = i[f"L0_attn_W{n}"].T
        d[f"L1_w{n}T"] = i[f"L1_attn_w{n}_w"].T
        d[f"L3_w{n}T"] = i[f"L3_attn_W{n}"].T
    for n, m in enumerate(("q1", "k1", "q2", "k2")):
        d[f"L0_lam{n}"] = i[f"L0_attn_lambda_{m}"].reshape(1, 4)
    d["subln_col"] = np.tile(i["L0_attn_subln_w"], HEADS).reshape(C, 1)
    d["L0_woT"] = i["L0_attn_Wo"].T
    for l in (0, 3):
        d[f"L{l}_fW1T"] = i[f"L{l}_ffn_W1"].T
        d[f"L{l}_fW2T"] = i[f"L{l}_ffn_W2"].T.reshape(HB, C, C).transpose(1, 0, 2)
        d[f"L{l}_fb1"] = i[f"L{l}_ffn_b1"].reshape(HB, C).T
        d[f"L{l}_fb2"] = i[f"L{l}_ffn_b2"].reshape(C, 1)
        d[f"L{l}_fscale"] = i[f"L{l}_ffn_scale"].reshape(1, 1)
    d["L1_bq"], d["L1_bk"] = i["L1_attn_wq_b"].reshape(C, 1), i["L1_attn_wk_b"].reshape(C, 1)
    d["L1_bv"], d["L1_bo"] = i["L1_attn_wv_b"].reshape(1, C), i["L1_attn_wo_b"].reshape(C, 1)
    wo = np.zeros((4, 2, 16, 2, C), np.float32)
    wo[:, :, 0:8] = i["L1_attn_wo_w"].T.reshape(2, 2, 4, 8, C).transpose(2, 1, 3, 0, 4)
    d["L1_woG"] = wo.reshape(128, 2, C)
    for n in "rkv":
        d[f"L1_W{n}T"] = i[f"L1_ffn_W_{n}"].T
    for n in "rk":
        d[f"L1_mu{n}"] = i[f"L1_ffn_mu_{n}"].reshape(C, 1)
    d["L2_kv_down"] = i["L2_attn_w_kv_down"]
    d["L2_wq"] = i["L2_attn_w_q"]
    d["L2_wk"], d["L2_wv"] = i["L2_attn_w_kv_up"][:, :HEADS * PH], i["L2_attn_w_kv_up"][:, HEADS * PH:]
    d["L2_wout"] = i["L2_attn_w_out"].reshape(HEADS // 2, C, C).transpose(1, 0, 2)
    d["L2_routerT"] = i["L2_ffn_router_w"].T
    d["L2_ebias"] = i["L2_ffn_e_bias"].reshape(1, E)

    for n in ("gate", "up"):
        d["sh_" + n] = i[f"L2_ffn_sh_{n}_w"].reshape(C, 2, C)
        d["ex_" + n] = i[f"L2_ffn_{n}_w"].reshape(EP, 2, C, EH).transpose(0, 2, 1, 3).reshape(-1, C)
    d["sh_down"] = i["L2_ffn_sh_down_w"].reshape(2, C, C).transpose(1, 0, 2)
    d["ex_down"] = i["L2_ffn_down_w"].reshape(-1, C)
    d["L3_woT"] = i["L3_attn_Wo"].T.reshape(C, 1, C)
    d["L3_norm"] = i["L3_attn_norm_const"].reshape(1, HEADS)
    d.update(constants())
    return {k: np.ascontiguousarray(v) for k, v in d.items()}


def kernel(**inputs):
    import concourse.bacc as bacc
    from concourse.bass_utils import run_bass_kernel_spmd

    nc = bacc.Bacc("TRN2", target_bir_lowering=False, num_devices=1)
    arrays = {"in_" + k: v for k, v in lay_out(inputs).items()}
    dram = {k[3:]: nc.dram_tensor(k, a.shape, mybir.dt.from_np(a.dtype), kind="ExternalInput").ap()
            for k, a in arrays.items()}
    out = nc.dram_tensor("out_x", (C, B, T), F32, kind="ExternalOutput").ap()
    build_program(nc, dram, out, range(8))
    r = run_bass_kernel_spmd(nc, [arrays], core_ids=[0])
    return np.ascontiguousarray(r.results[0]["out_x"].transpose(1, 2, 0))
```
